# Optimizing a Trainium2 kernel written in Bass

```python
import numpy as np
import jax
import jax.numpy as jnp

def _softmax(x, axis=-1):
    return jax.nn.softmax(x, axis=axis)

def _gelu(x):
    return jax.nn.gelu(x, approximate=True)

def _silu(x):
    return jax.nn.silu(x)

def _sigmoid(x):
    return jax.nn.sigmoid(x)

def _layernorm(x, axis=-1, eps=1e-05):
    m = jnp.mean(x, axis=axis, keepdims=True)
    v = jnp.var(x, axis=axis, keepdims=True)
    return (x - m) / jnp.sqrt(v + eps)

def _scatter_add(tgt, idx, src, axis=0):
    return tgt.at[idx].add(src)

def _segment_sum(src, seg, n):
    return jax.ops.segment_sum(src, seg, n)
kernel_name = 'mk_decoder_postln_d2_seqx_r8_93bd35'

def setup_inputs(seed: int=0):
    np.random.seed(seed)
    _w = jnp.asarray

    def _rec_inputs():
        import jax
        import jax.numpy as jnp
        _rk = jax.random.key(seed)
        x = -0.000125 + 0.9999 * jax.random.normal(jax.random.fold_in(_rk, 1), (32, 100, 256), jnp.float32)
        _lenS = 100 - jax.random.randint(jax.random.fold_in(_rk, 7), (32,), 0, max(1, 100 // 4) + 1, jnp.int32)
        _lenS2 = 1444 - jax.random.randint(jax.random.fold_in(_rk, 8), (32,), 0, max(1, 1444 // 4) + 1, jnp.int32)
        _ctx_2048P = jax.random.normal(jax.random.fold_in(_rk, 11), (32, 16, 256), jnp.float32)
        _ctx_2048c = jax.random.dirichlet(jax.random.fold_in(_rk, 511), 0.3 * jnp.ones((16,), jnp.float32), (32, 1444))
        _ctx_2048t = jnp.einsum('bsk,bkd->bsd', _ctx_2048c, _ctx_2048P)
        _ctx_2048t = _ctx_2048t * jax.lax.rsqrt(jnp.mean(jnp.square(_ctx_2048t)) + 1e-12) * 0.953939
        ctx_2048 = -0.000514642 + 1.00011 * (_ctx_2048t + 0.3 * jax.random.normal(jax.random.fold_in(_rk, 611), (32, 1444, 256), jnp.float32))
        _validS = jnp.arange(100)[None, :] < _lenS[:, None]
        _validS2 = jnp.arange(1444)[None, :] < _lenS2[:, None]
        _causal = jnp.tril(jnp.ones((100, 100), dtype=bool))
        mask_BxS2_bk0 = jnp.logical_not(jnp.broadcast_to(_validS2[:, :], (32, 1444)))
        return (x, ctx_2048, mask_BxS2_bk0)
    x, ctx_2048, mask_BxS2_bk0 = _rec_inputs()

    def _L0_attn_setup():
        import jax, jax.numpy as jnp
        import numpy as np
        D_MODEL = 256
        N_HEADS = 16
        D_HEAD = D_MODEL // N_HEADS
        B, S = (2, 256)
        EPS = 1e-05

        def _mhsa(X, ln_g, ln_b, Wq, bq, Wk, bk, Wv, bv, Wo, bo):
            n_ctx = X.shape[-2]
            mu = jnp.mean(X, axis=-1, keepdims=True)
            var = jnp.mean(jnp.square(X - mu), axis=-1, keepdims=True)
            Xn = (X - mu) * jax.lax.rsqrt(var + EPS) * ln_g + ln_b

            def split_heads(t):
                return t.reshape(t.shape[:-1] + (N_HEADS, D_HEAD)).swapaxes(-2, -3)
            Q = split_heads(Xn @ Wq + bq)
            K = split_heads(Xn @ Wk + bk)
            V = split_heads(Xn @ Wv + bv)
            scores = jnp.einsum('bhqd,bhkd->bhqk', Q, K) / jnp.sqrt(jnp.float32(D_HEAD))
            causal = jnp.tril(jnp.ones((n_ctx, n_ctx), dtype=bool))
            scores = jnp.where(causal, scores, jnp.float32(-jnp.inf))
            A = jax.nn.softmax(scores, axis=-1)
            AV = jnp.einsum('bhqk,bhkd->bhqd', A, V)
            AV = AV.swapaxes(-2, -3).reshape(X.shape[:-1] + (D_MODEL,))
            return AV @ Wo + bo
        key = jax.random.key(seed)
        ks = jax.random.split(key, 10)
        sd = 1.0 / np.sqrt(D_MODEL)
        inp = {'X': jax.random.normal(ks[0], (B, S, D_MODEL), dtype=jnp.float32), 'ln_g': jnp.ones((D_MODEL,), jnp.float32), 'ln_b': jnp.zeros((D_MODEL,), jnp.float32), 'Wq': jax.random.uniform(ks[1], (D_MODEL, D_MODEL), jnp.float32, -sd, sd), 'bq': jax.random.uniform(ks[2], (D_MODEL,), jnp.float32, -sd, sd), 'Wk': jax.random.uniform(ks[3], (D_MODEL, D_MODEL), jnp.float32, -sd, sd), 'bk': jax.random.uniform(ks[4], (D_MODEL,), jnp.float32, -sd, sd), 'Wv': jax.random.uniform(ks[5], (D_MODEL, D_MODEL), jnp.float32, -sd, sd), 'bv': jax.random.uniform(ks[6], (D_MODEL,), jnp.float32, -sd, sd), 'Wo': jax.random.uniform(ks[7], (D_MODEL, D_MODEL), jnp.float32, -sd, sd), 'bo': jax.random.uniform(ks[8], (D_MODEL,), jnp.float32, -sd, sd)}
        return inp
    _L0_attn_all = _L0_attn_setup()
    _L0_attn_in = {k: v for k, v in _L0_attn_all.items() if k in ('ln_g', 'ln_b', 'Wq', 'bq', 'Wk', 'bk', 'Wv', 'bv', 'Wo', 'bo')}
    del _L0_attn_all

    def _L0_xattn_setup():
        import jax, jax.numpy as jnp
        import numpy as np
        key = jax.random.key(seed)
        k1, k2, k3 = jax.random.split(key, 3)
        B, S, D, M = (8, 256, 256, 128)
        hidden_states = jax.random.normal(k1, (B, S, D), dtype=jnp.float32)
        memory_tokens = jax.random.normal(k2, (B, M, D), dtype=jnp.float32)
        memory_mask = jax.random.randint(k3, (B, M), 0, 2).astype(jnp.bool_)
        return {'hidden_states': hidden_states, 'memory_tokens': memory_tokens, 'memory_mask': memory_mask}
    _L0_xattn_all = _L0_xattn_setup()
    _L0_xattn_in = {k: v for k, v in _L0_xattn_all.items() if k in ()}
    del _L0_xattn_all

    def _L0_ffn_setup():
        import jax, jax.numpy as jnp
        import numpy as np
        GOLDEN_CENTER = 1.0 / np.e
        GOLDEN_LOWER = 0.5 - np.log(4.0 / 3.0)
        GOLDEN_UPPER = 0.5

        def _golden_weights(x, Wr, temperature):
            inh = jax.nn.sigmoid(x @ Wr / temperature)
            in_zone = (inh >= GOLDEN_LOWER) & (inh <= GOLDEN_UPPER)
            distance = jnp.abs(inh - GOLDEN_CENTER)
            weights = jnp.exp(-distance / 0.1) * in_zone.astype(x.dtype)
            wsum = jnp.sum(weights, axis=-1, keepdims=True)
            no_expert = wsum < 1e-08
            fb = jnp.exp(-distance / 0.3)
            _, top2 = jax.lax.top_k(fb, 2)
            fb_mask = jnp.sum(jax.nn.one_hot(top2, weights.shape[-1], dtype=x.dtype), axis=-2)
            fb_w = fb * fb_mask
            fb_w = fb_w / jnp.maximum(jnp.sum(fb_w, axis=-1, keepdims=True), 1e-08)
            weights = jnp.where(no_expert, fb_w, weights)
            weights = weights / jnp.maximum(jnp.sum(weights, axis=-1, keepdims=True), 1e-08)
            return weights
        key = jax.random.key(seed)
        ks = jax.random.split(key, 5)
        B, T, D, E, F = (2, 256, 256, 8, 256)
        s_in = 1.0 / np.sqrt(D)
        s_f = 1.0 / np.sqrt(F)
        return {'x': jax.random.normal(ks[0], (B, T, D), dtype=jnp.float32), 'Wg': jax.random.normal(ks[1], (E, D, F), dtype=jnp.float32) * s_in, 'Wu': jax.random.normal(ks[2], (E, D, F), dtype=jnp.float32) * s_in, 'Wd': jax.random.normal(ks[3], (E, F, D), dtype=jnp.float32) * s_f, 'Wr': jax.random.normal(ks[4], (D, E), dtype=jnp.float32) * s_in, 'temperature': jnp.ones((1,), dtype=jnp.float32)}
    _L0_ffn_all = _L0_ffn_setup()
    _L0_ffn_in = {k: v for k, v in _L0_ffn_all.items() if k in ('Wg', 'Wu', 'Wd', 'Wr', 'temperature')}
    del _L0_ffn_all

    def _L1_attn_setup():
        import jax, jax.numpy as jnp
        import numpy as np
        B, S, D = (2, 256, 256)
        H = 16
        HD = D // H
        key = jax.random.key(seed)
        ks = jax.random.split(key, 9)
        scale = 0.02
        return {'x': jax.random.normal(ks[0], (B, S, D), dtype=jnp.float32), 'wq': jax.random.normal(ks[1], (D, D), dtype=jnp.float32) * scale, 'bq': jnp.zeros((D,), dtype=jnp.float32), 'wk': jax.random.normal(ks[2], (D, D), dtype=jnp.float32) * scale, 'bk': jnp.zeros((D,), dtype=jnp.float32), 'wv': jax.random.normal(ks[3], (D, D), dtype=jnp.float32) * scale, 'bv': jnp.zeros((D,), dtype=jnp.float32), 'wp': jax.random.normal(ks[4], (D, D), dtype=jnp.float32) * scale, 'bp': jnp.zeros((D,), dtype=jnp.float32)}
    _L1_attn_all = _L1_attn_setup()
    _L1_attn_in = {k: v for k, v in _L1_attn_all.items() if k in ('wq', 'bq', 'wk', 'bk', 'wv', 'bv', 'wp', 'bp')}
    del _L1_attn_all

    def _L1_xattn_setup():
        import math
        import jax, jax.numpy as jnp
        import numpy as np
        HEADS = 16
        MASKED_BIAS = -10000.0

        def _mha(q, k, v):
            B, Sq, D = q.shape
            Sk = k.shape[-2]
            hd = D // HEADS
            qh = q.reshape(B, Sq, HEADS, hd).transpose(0, 2, 1, 3)
            kh = k.reshape(B, Sk, HEADS, hd).transpose(0, 2, 1, 3)
            vh = v.reshape(B, Sk, HEADS, hd).transpose(0, 2, 1, 3)
            scores = jnp.einsum('bhqd,bhkd->bhqk', qh, kh) / math.sqrt(hd)
            qi = jnp.arange(Sq)[:, None] + (Sk - Sq)
            ki = jnp.arange(Sk)[None, :]
            causal = ki <= qi
            scores = jnp.where(causal[None, None], scores, jnp.asarray(MASKED_BIAS, scores.dtype))
            attn = jax.nn.softmax(scores, axis=-1)
            out = jnp.einsum('bhqk,bhkd->bhqd', attn, vh)
            return out.transpose(0, 2, 1, 3).reshape(B, Sq, D)
        key = jax.random.key(seed)
        kq, kk, kv = jax.random.split(key, 3)
        B, S, D = (4, 128, 256)
        q = jax.random.normal(kq, (B, S, D), dtype=jnp.float32)
        k = jax.random.normal(kk, (B, S, D), dtype=jnp.float32)
        v = jax.random.normal(kv, (B, S, D), dtype=jnp.float32)
        return {'q': q, 'k': k, 'v': v}
    _L1_xattn_all = _L1_xattn_setup()
    _L1_xattn_in = {k: v for k, v in _L1_xattn_all.items() if k in ()}
    del _L1_xattn_all

    def _L1_ffn_setup():
        import jax, jax.numpy as jnp
        import numpy as np
        HIDDEN = 256
        INTER = 1024
        B, S = (4, 128)

        def _qmatmul(x, w_int8, scale):
            y = jnp.einsum('bsh,ho->bso', x, w_int8.astype(x.dtype))
            return y * scale
        key = jax.random.key(seed)
        ks = jax.random.split(key, 7)
        x = jax.random.normal(ks[0], (B, S, HIDDEN), dtype=jnp.float32)
        w_gate = jax.random.randint(ks[1], (HIDDEN, INTER), -128, 128, dtype=jnp.int32).astype(jnp.int8)
        w_up = jax.random.randint(ks[2], (HIDDEN, INTER), -128, 128, dtype=jnp.int32).astype(jnp.int8)
        w_down = jax.random.randint(ks[3], (INTER, HIDDEN), -128, 128, dtype=jnp.int32).astype(jnp.int8)
        s_gate = jax.random.uniform(ks[4], (INTER,), dtype=jnp.float32) * 0.02 + 0.001
        s_up = jax.random.uniform(ks[5], (INTER,), dtype=jnp.float32) * 0.02 + 0.001
        s_down = jax.random.uniform(ks[6], (HIDDEN,), dtype=jnp.float32) * 0.02 + 0.001
        return {'x': x, 'w_gate': w_gate, 'w_up': w_up, 'w_down': w_down, 's_gate': s_gate, 's_up': s_up, 's_down': s_down}
    _L1_ffn_all = _L1_ffn_setup()
    _L1_ffn_in = {k: v for k, v in _L1_ffn_all.items() if k in ('w_gate', 'w_up', 'w_down', 's_gate', 's_up', 's_down')}
    del _L1_ffn_all
    return {'x': x, 'ctx_2048': ctx_2048, 'mask_BxS2_bk0': mask_BxS2_bk0, 'L0_attn_ln_g': _L0_attn_in['ln_g'], 'L0_attn_ln_b': _L0_attn_in['ln_b'], 'L0_attn_Wq': _L0_attn_in['Wq'], 'L0_attn_bq': _L0_attn_in['bq'], 'L0_attn_Wk': _L0_attn_in['Wk'], 'L0_attn_bk': _L0_attn_in['bk'], 'L0_attn_Wv': _L0_attn_in['Wv'], 'L0_attn_bv': _L0_attn_in['bv'], 'L0_attn_Wo': _L0_attn_in['Wo'], 'L0_attn_bo': _L0_attn_in['bo'], 'L0_ffn_Wg': _L0_ffn_in['Wg'], 'L0_ffn_Wu': _L0_ffn_in['Wu'], 'L0_ffn_Wd': _L0_ffn_in['Wd'], 'L0_ffn_Wr': _L0_ffn_in['Wr'], 'L0_ffn_temperature': _L0_ffn_in['temperature'], 'L1_attn_wq': _L1_attn_in['wq'], 'L1_attn_bq': _L1_attn_in['bq'], 'L1_attn_wk': _L1_attn_in['wk'], 'L1_attn_bk': _L1_attn_in['bk'], 'L1_attn_wv': _L1_attn_in['wv'], 'L1_attn_bv': _L1_attn_in['bv'], 'L1_attn_wp': _L1_attn_in['wp'], 'L1_attn_bp': _L1_attn_in['bp'], 'L1_ffn_w_gate': _L1_ffn_in['w_gate'], 'L1_ffn_w_up': _L1_ffn_in['w_up'], 'L1_ffn_w_down': _L1_ffn_in['w_down'], 'L1_ffn_s_gate': _L1_ffn_in['s_gate'], 'L1_ffn_s_up': _L1_ffn_in['s_up'], 'L1_ffn_s_down': _L1_ffn_in['s_down']}

def reference(x, ctx_2048, mask_BxS2_bk0, L0_attn_ln_g, L0_attn_ln_b, L0_attn_Wq, L0_attn_bq, L0_attn_Wk, L0_attn_bk, L0_attn_Wv, L0_attn_bv, L0_attn_Wo, L0_attn_bo, L0_ffn_Wg, L0_ffn_Wu, L0_ffn_Wd, L0_ffn_Wr, L0_ffn_temperature, L1_attn_wq, L1_attn_bq, L1_attn_wk, L1_attn_bk, L1_attn_wv, L1_attn_bv, L1_attn_wp, L1_attn_bp, L1_ffn_w_gate, L1_ffn_w_up, L1_ffn_w_down, L1_ffn_s_gate, L1_ffn_s_up, L1_ffn_s_down):
    import jax
    import jax.numpy as jnp

    def _L0_attn_ref(X, ln_g, ln_b, Wq, bq, Wk, bk, Wv, bv, Wo, bo):
        import jax, jax.numpy as jnp
        import numpy as np
        D_MODEL = 256
        N_HEADS = 16
        D_HEAD = D_MODEL // N_HEADS
        B, S = (2, 256)
        EPS = 1e-05

        def _mhsa(X, ln_g, ln_b, Wq, bq, Wk, bk, Wv, bv, Wo, bo):
            n_ctx = X.shape[-2]
            mu = jnp.mean(X, axis=-1, keepdims=True)
            var = jnp.mean(jnp.square(X - mu), axis=-1, keepdims=True)
            Xn = (X - mu) * jax.lax.rsqrt(var + EPS) * ln_g + ln_b

            def split_heads(t):
                return t.reshape(t.shape[:-1] + (N_HEADS, D_HEAD)).swapaxes(-2, -3)
            Q = split_heads(Xn @ Wq + bq)
            K = split_heads(Xn @ Wk + bk)
            V = split_heads(Xn @ Wv + bv)
            scores = jnp.einsum('bhqd,bhkd->bhqk', Q, K) / jnp.sqrt(jnp.float32(D_HEAD))
            causal = jnp.tril(jnp.ones((n_ctx, n_ctx), dtype=bool))
            scores = jnp.where(causal, scores, jnp.float32(-jnp.inf))
            A = jax.nn.softmax(scores, axis=-1)
            AV = jnp.einsum('bhqk,bhkd->bhqd', A, V)
            AV = AV.swapaxes(-2, -3).reshape(X.shape[:-1] + (D_MODEL,))
            return AV @ Wo + bo
        return _mhsa(X, ln_g, ln_b, Wq, bq, Wk, bk, Wv, bv, Wo, bo)

    def _L0_xattn_ref(hidden_states, memory_tokens, memory_mask):
        import jax, jax.numpy as jnp
        import numpy as np
        B, S, D = hidden_states.shape
        scale = 1.0 / jnp.sqrt(jnp.asarray(D, hidden_states.dtype))
        scores = jnp.einsum('bsd,bmd->bsm', hidden_states, memory_tokens) * scale
        neg_inf = jnp.asarray(-1e+30, scores.dtype)
        scores = jnp.where(memory_mask[:, None, :], scores, neg_inf)
        attn = jax.nn.softmax(scores, axis=-1)
        readout = jnp.einsum('bsm,bmd->bsd', attn, memory_tokens)
        valid_b = jnp.any(memory_mask, axis=-1)
        out = jnp.where(valid_b[:, None, None], readout, jnp.zeros_like(readout))
        return out

    def _L0_ffn_ref(x, Wg, Wu, Wd, Wr, temperature):
        import jax, jax.numpy as jnp
        import numpy as np
        GOLDEN_CENTER = 1.0 / np.e
        GOLDEN_LOWER = 0.5 - np.log(4.0 / 3.0)
        GOLDEN_UPPER = 0.5

        def _golden_weights(x, Wr, temperature):
            inh = jax.nn.sigmoid(x @ Wr / temperature)
            in_zone = (inh >= GOLDEN_LOWER) & (inh <= GOLDEN_UPPER)
            distance = jnp.abs(inh - GOLDEN_CENTER)
            weights = jnp.exp(-distance / 0.1) * in_zone.astype(x.dtype)
            wsum = jnp.sum(weights, axis=-1, keepdims=True)
            no_expert = wsum < 1e-08
            fb = jnp.exp(-distance / 0.3)
            _, top2 = jax.lax.top_k(fb, 2)
            fb_mask = jnp.sum(jax.nn.one_hot(top2, weights.shape[-1], dtype=x.dtype), axis=-2)
            fb_w = fb * fb_mask
            fb_w = fb_w / jnp.maximum(jnp.sum(fb_w, axis=-1, keepdims=True), 1e-08)
            weights = jnp.where(no_expert, fb_w, weights)
            weights = weights / jnp.maximum(jnp.sum(weights, axis=-1, keepdims=True), 1e-08)
            return weights
        weights = _golden_weights(x, Wr, temperature)
        gate = jnp.einsum('btd,edf->betf', x, Wg)
        up = jnp.einsum('btd,edf->betf', x, Wu)
        h = jax.nn.silu(gate) * up
        e_out = jnp.einsum('betf,efd->betd', h, Wd)
        out = jnp.einsum('bte,betd->btd', weights, e_out)
        return out

    def _L1_attn_ref(x, wq, bq, wk, bk, wv, bv, wp, bp):
        import jax, jax.numpy as jnp
        import numpy as np
        B, S, D = (2, 256, 256)
        H = 16
        HD = D // H
        b, s, _ = x.shape
        q = (x @ wq + bq).reshape(b, s, H, HD).transpose(0, 2, 1, 3)
        k = (x @ wk + bk).reshape(b, s, H, HD).transpose(0, 2, 1, 3)
        v = (x @ wv + bv).reshape(b, s, H, HD).transpose(0, 2, 1, 3)
        scores = jnp.einsum('bhqd,bhkd->bhqk', q, k)
        causal = jnp.tril(jnp.ones((s, s), dtype=bool))
        scores = jnp.where(causal, scores, -jnp.inf)
        attn = jax.nn.softmax(scores / jnp.sqrt(jnp.float32(HD)), axis=-1)
        ctx = jnp.einsum('bhqk,bhkd->bhqd', attn, v)
        ctx = ctx.transpose(0, 2, 1, 3).reshape(b, s, H * HD)
        return ctx @ wp + bp

    def _L1_xattn_ref(q, k, v):
        import math
        import jax, jax.numpy as jnp
        import numpy as np
        HEADS = 16
        MASKED_BIAS = -10000.0

        def _mha(q, k, v):
            B, Sq, D = q.shape
            Sk = k.shape[-2]
            hd = D // HEADS
            qh = q.reshape(B, Sq, HEADS, hd).transpose(0, 2, 1, 3)
            kh = k.reshape(B, Sk, HEADS, hd).transpose(0, 2, 1, 3)
            vh = v.reshape(B, Sk, HEADS, hd).transpose(0, 2, 1, 3)
            scores = jnp.einsum('bhqd,bhkd->bhqk', qh, kh) / math.sqrt(hd)
            qi = jnp.arange(Sq)[:, None] + (Sk - Sq)
            ki = jnp.arange(Sk)[None, :]
            causal = ki <= qi
            scores = jnp.where(causal[None, None], scores, jnp.asarray(MASKED_BIAS, scores.dtype))
            attn = jax.nn.softmax(scores, axis=-1)
            out = jnp.einsum('bhqk,bhkd->bhqd', attn, vh)
            return out.transpose(0, 2, 1, 3).reshape(B, Sq, D)
        return _mha(q, k, v)

    def _L1_ffn_ref(x, w_gate, w_up, w_down, s_gate, s_up, s_down):
        import jax, jax.numpy as jnp
        import numpy as np
        HIDDEN = 256
        INTER = 1024
        B, S = (4, 128)

        def _qmatmul(x, w_int8, scale):
            y = jnp.einsum('bsh,ho->bso', x, w_int8.astype(x.dtype))
            return y * scale
        gate = jax.nn.silu(_qmatmul(x, w_gate, s_gate))
        up = _qmatmul(x, w_up, s_up)
        fuse = gate * up
        return _qmatmul(fuse, w_down, s_down)
    x = _layernorm(x + _L0_attn_ref(x, L0_attn_ln_g, L0_attn_ln_b, L0_attn_Wq, L0_attn_bq, L0_attn_Wk, L0_attn_bk, L0_attn_Wv, L0_attn_bv, L0_attn_Wo, L0_attn_bo), axis=-1)
    x = _layernorm(x + _L0_xattn_ref(x, ctx_2048, mask_BxS2_bk0), axis=-1)
    x = _layernorm(x + _L0_ffn_ref(x, L0_ffn_Wg, L0_ffn_Wu, L0_ffn_Wd, L0_ffn_Wr, L0_ffn_temperature), axis=-1)
    x = _layernorm(x + _L1_attn_ref(x, L1_attn_wq, L1_attn_bq, L1_attn_wk, L1_attn_bk, L1_attn_wv, L1_attn_bv, L1_attn_wp, L1_attn_bp), axis=-1)
    x = _layernorm(x + _L1_xattn_ref(x, ctx_2048, ctx_2048), axis=-1)
    x = _layernorm(x + _L1_ffn_ref(x, L1_ffn_w_gate, L1_ffn_w_up, L1_ffn_w_down, L1_ffn_s_gate, L1_ffn_s_up, L1_ffn_s_down), axis=-1)
    return x

_drawn_inputs = setup_inputs


def setup_inputs(seed=0):
    import zlib

    import numpy as np

    out = dict(_drawn_inputs(seed))
    spreads = {'L0_attn_ln_g': (1.0, 0.2),
     'L0_attn_ln_b': (0.0, 0.1),
     'L1_attn_bq': (0.0, 0.8),
     'L1_attn_bk': (0.0, 0.8),
     'L1_attn_bv': (0.0, 0.1),
     'L1_attn_bp': (0.0, 0.1)}
    factors = {'L0_attn_bq': 4.646, 'L0_attn_bk': 8.0, 'L1_attn_wq': 8.0, 'L1_attn_wk': 8.0}
    for name, (base, spread) in spreads.items():
        noise = np.random.default_rng([zlib.crc32(name.encode()), seed]).standard_normal(out[name].shape)
        drawn = base * np.exp(spread * noise) if base else spread * noise
        out[name] = jnp.asarray(drawn.astype(out[name].dtype))
    for name, factor in factors.items():
        out[name] = (out[name] * factor).astype(out[name].dtype)
    return out
```

```python
import concourse.bass as bass
from concourse import mybir
from contextlib import ExitStack

F32 = mybir.dt.float32
BF16 = mybir.dt.bfloat16
U8 = mybir.dt.uint8
I8 = mybir.dt.int8
ALU = mybir.AluOpType
ACT = mybir.ActivationFunctionType
AX = mybir.AxisListType

BATCH, SEQ, DIM, HEADS = 32, 100, 256, 16
HD = DIM // HEADS
KD = DIM // 128
HPB = 128 // HD
CTX = 1444
EXPERTS, EXPERT_F = 8, 256
INTER = 1024
LN_EPS = 1e-5
NEG = -1e30
BANK = 512
GROUP = 4


class Memory:

    def __init__(self, nc, stack, prefix):
        self.nc, self.stack, self.prefix, self.sems = nc, stack, prefix, []
        stack.callback(self.release)

    def sbuf(self, name, shape, dt=F32):
        return self.stack.enter_context(self.nc.sbuf_tensor(f"{self.prefix}_{name}", shape, dt))

    def psum(self, name, shape, dt=F32):
        return self.stack.enter_context(self.nc.psum_tensor(f"{self.prefix}_{name}", shape, dt))

    def sem(self, name):
        sem = self.nc.alloc_semaphore(f"{self.prefix}_{name}")
        self.sems.append(sem)
        return sem

    def release(self):
        if self.sems:
            self.nc.clear_and_free_semaphores(self.sems)
            self.nc.all_engine_barrier()


def after(engine, sem, count):
    if not isinstance(count, int) or count > 0:
        engine.wait_ge(sem, count)


class Chain:

    def __init__(self, engine, sem):
        self.engine, self.sem, self.origin, self.n = engine, sem, 0, 0

    def begin(self, origin):
        self.origin, self.n = origin, 0

    def __call__(self, instruction):
        self.n += 1
        instruction.then_inc(self.sem, 1)
        self.engine.wait_ge(self.sem, self.origin + self.n)


def self_attention_pass(nc, prefix, x_tokens, x_dram, ident, minus_half, wq, bq, wk, bk, wv, bv, wo, bo, ln_g, ln_b):
    pre_norm = ln_g is not None
    with ExitStack() as stack:
        mem = Memory(nc, stack, prefix)
        w_sb = {n: mem.sbuf(n, [128, KD, DIM]) for n in ("wq", "wk", "wv", "wo")}
        bias_q = mem.sbuf("bias_q", [128, KD])
        bias_k = mem.sbuf("bias_k", [128, KD])
        bias_v = mem.sbuf("bias_v", [SEQ, DIM])
        bias_o = mem.sbuf("bias_o", [SEQ, DIM])
        gain = mem.sbuf("gain", [128, KD]) if pre_norm else None
        shift = mem.sbuf("shift", [128, KD]) if pre_norm else None
        head_rows = mem.sbuf("head_rows", [128, HPB])
        causal = mem.sbuf("causal", [SEQ, 4 * SEQ], BF16)
        ident_bf = mem.sbuf("ident_bf", [128, 128], BF16)
        normed = mem.sbuf("normed", [SEQ, DIM])
        x_t = mem.sbuf("x_t", [128, KD, SEQ])
        q_t = mem.sbuf("q_t", [128, KD, SEQ])
        k_heads = mem.sbuf("k_heads", [128, KD, HPB, SEQ])
        v_ones = mem.sbuf("v_ones", [SEQ, HEADS, HD + 1])
        row_max = mem.sbuf("row_max", [SEQ, HEADS])
        probs = mem.sbuf("probs", [SEQ, HEADS, SEQ])
        probs_t = mem.sbuf("probs_t", [SEQ, HEADS, SEQ])
        inv_sum = mem.sbuf("inv_sum", [SEQ, HEADS])
        mixed = mem.sbuf("mixed", [SEQ, DIM])
        mixed_t = mem.sbuf("mixed_t", [128, KD, SEQ])
        x_bias = mem.sbuf("x_bias", [SEQ, DIM])
        summed = mem.sbuf("summed", [SEQ, DIM])
        stats = mem.sbuf("stats", [SEQ, 6])
        mean_var = mem.sbuf("mean_var", [SEQ, 2])
        var_eps = mem.sbuf("var_eps", [SEQ, 1])
        rstd = mem.sbuf("rstd", [SEQ, 1])
        stats0 = mem.sbuf("stats0", [SEQ, 6])
        mean_var0 = mem.sbuf("mean_var0", [SEQ, 2])
        var_eps0 = mem.sbuf("var_eps0", [SEQ, 1])
        rstd0 = mem.sbuf("rstd0", [SEQ, 1])

        score_ps = mem.psum("score_ps", [128, 4, BANK])
        turn_ps = mem.psum("turn_ps", [128, 2, BANK])
        misc_ps = mem.psum("misc_ps", [128, BANK])
        out_ps = mem.psum("out_ps", [128, BANK])

        weights_in = mem.sem("weights_in")
        x_in = mem.sem("x_in")
        const_ready = mem.sem("const_ready")
        pool_chain_sem = mem.sem("pool_order")
        dve_chain_sem = mem.sem("dve_order")
        normed_ready, var0_ready, rstd0_ready = mem.sem("normed_ready"), mem.sem("var0_ready"), mem.sem("rstd0_ready")
        xt_done, xt_ready = mem.sem("xt_done"), mem.sem("xt_ready")
        qk_done, v_done = mem.sem("qk_done"), mem.sem("v_done")
        q_ready, k_ready, v_ready = mem.sem("q_ready"), mem.sem("k_ready"), mem.sem("v_ready")
        scores_done, shifted = mem.sem("scores_done"), mem.sem("shifted")
        probs_ready = mem.sem("probs_ready")
        turned, turned_copied = mem.sem("turned"), mem.sem("turned_copied")
        attended, mixed_ready = mem.sem("attended"), mem.sem("mixed_ready")
        mixed_turned, mixed_t_ready = mem.sem("mixed_turned"), mem.sem("mixed_t_ready")
        projected, x_bias_ready = mem.sem("projected"), mem.sem("x_bias_ready")
        summed_done, var_ready, rstd_ready, x_new = (mem.sem("summed_done"), mem.sem("var_ready"),
                                                     mem.sem("rstd_ready"), mem.sem("x_new"))
        WEIGHTS = 16 * (8 + (2 if pre_norm else 0))
        CONSTS = 4
        TURNS = 2
        HT = HEADS // TURNS

        with nc.Block() as block:

            @block.sync
            def _(sp):
                if x_dram is not None:
                    for r in range(0, BATCH, 4):
                        sp.dma_start(x_tokens[:, r:r + 4, :],
                                     x_dram[r:r + 4].rearrange("b s d -> s b d")).then_inc(x_in, 16)
                for name, w in (("wq", wq), ("wk", wk), ("wv", wv), ("wo", wo)):
                    sp.dma_start(w_sb[name][:, :, :], w.rearrange("(k p) n -> p k n", p=128)).then_inc(weights_in, 16)
                with nc.allow_non_contiguous_dma(reason="256 bias values, once"):
                    sp.dma_start(bias_q[:, :], bq.rearrange("(k p) -> p k", p=128)).then_inc(weights_in, 16)
                    sp.dma_start(bias_k[:, :], bk.rearrange("(k p) -> p k", p=128)).then_inc(weights_in, 16)
                    if pre_norm:
                        sp.dma_start(gain[:, :], ln_g.rearrange("(k p) -> p k", p=128)).then_inc(weights_in, 16)
                        sp.dma_start(shift[:, :], ln_b.rearrange("(k p) -> p k", p=128)).then_inc(weights_in, 16)
                sp.dma_start(bias_v[:, :], bv.partition_broadcast(SEQ)).then_inc(weights_in, 16)
                sp.dma_start(bias_o[:, :], bo.partition_broadcast(SEQ)).then_inc(weights_in, 16)
                sp.wait_ge(weights_in, WEIGHTS)

            @block.gpsimd
            def _(pool):
                chain = Chain(pool, pool_chain_sem)
                chain(nc.gpsimd.memset(head_rows[:, :], 1.0))
                chain(nc.gpsimd.affine_select(out=head_rows[:, :], in_=head_rows[:, :], compare_op=ALU.is_ge, fill=0.0,
                                              base=0, pattern=[[-HD, HPB]], channel_multiplier=1))
                nc.gpsimd.affine_select(out=head_rows[:, :], in_=head_rows[:, :], compare_op=ALU.is_ge, fill=0.0,
                                        base=HD - 1, pattern=[[HD, HPB]], channel_multiplier=-1).then_inc(const_ready, 1)
                chain(nc.gpsimd.memset(causal[:, :], 0.0))
                cv = causal[:, :].rearrange("q (h k) -> q h k", h=4)
                nc.gpsimd.affine_select(out=cv, in_=cv, compare_op=ALU.is_ge, fill=NEG, base=0,
                                        pattern=[[0, 4], [-1, SEQ]], channel_multiplier=1).then_inc(const_ready, 1)
                nc.gpsimd.tensor_copy(ident_bf[:, :], ident[:, :]).then_inc(const_ready, 1)
                nc.gpsimd.memset(v_ones[:, :, HD:HD + 1], 1.0).then_inc(const_ready, 1)
                pool.wait_ge(weights_in, WEIGHTS)
                if x_dram is not None:
                    pool.wait_ge(x_in, 16 * (BATCH // 4))

                def norm_power(i):
                    if pre_norm:
                        pool.wait_ge(var0_ready, i + 1)
                        nc.gpsimd.tensor_tensor(out=rstd0[:, :], in0=var_eps0[:, :], in1=minus_half[0:SEQ, :],
                                                op=ALU.pow).then_inc(rstd0_ready, 1)

                def residual_bias(i):
                    after(pool, summed_done, i)
                    nc.gpsimd.tensor_tensor(out=x_bias[:, :], in0=x_tokens[:, i, :], in1=bias_o[:, :],
                                            op=ALU.add).then_inc(x_bias_ready, 1)

                def final_power(i):
                    pool.wait_ge(var_ready, i + 1)
                    nc.gpsimd.tensor_tensor(out=rstd[:, :], in0=var_eps[:, :], in1=minus_half[0:SEQ, :],
                                            op=ALU.pow).then_inc(rstd_ready, 1)

                norm_power(0)
                def step(i):
                    residual_bias(i - 1)
                    norm_power(i)
                    final_power(i - 1)

                step(1)
                with pool.Fori(2, BATCH) as i:
                    step(i)
                residual_bias(BATCH - 1)
                final_power(BATCH - 1)

            @block.scalar
            def _(act):
                act.wait_ge(weights_in, WEIGHTS)

                def queries(i):
                    act.wait_ge(qk_done, i + 1)
                    after(act, scores_done, i)
                    for k in range(KD):
                        last = nc.scalar.activation(q_t[:, k, :], turn_ps[:, 0, k * SEQ:(k + 1) * SEQ],
                                                    ACT.Identity, bias=bias_q[:, k:k + 1])
                    last.then_inc(q_ready, 1)

                def exponentials(i):
                    act.wait_ge(shifted, i + 1)
                    nc.scalar.activation(probs[:, :, :], probs[:, :, :], ACT.Exp,
                                         scale=float(HD) ** -0.5).then_inc(probs_ready, 1)

                def turned_copy(i, t):
                    act.wait_ge(turned, TURNS * i + t + 1)
                    if t == 0:
                        after(act, attended, i)
                    nc.scalar.activation(
                        probs_t[:, HT * t:HT * (t + 1), :].rearrange("k (b h) q -> k b (h q)", b=2),
                        turn_ps[0:SEQ, :, 0:4 * SEQ], ACT.Copy).then_inc(turned_copied, 1)

                queries(0)
                exponentials(0)
                def step(i):
                    turned_copy(i - 1, 0)
                    turned_copy(i - 1, 1)
                    queries(i)
                    exponentials(i)

                step(1)
                with act.Fori(2, BATCH) as i:
                    step(i)
                turned_copy(BATCH - 1, 0)
                turned_copy(BATCH - 1, 1)

            @block.tensor
            def _(pe):
                pe.wait_ge(weights_in, WEIGHTS)
                pe.wait_ge(const_ready, CONSTS)

                def turn_x(i):
                    pe.wait_ge(normed_ready, i + 1)
                    for k in range(KD):
                        last = nc.tensor.transpose(misc_ps[:, k * SEQ:(k + 1) * SEQ],
                                                   normed[:, k * 128:(k + 1) * 128], ident[0:SEQ, 0:SEQ])
                    last.then_inc(xt_done, 1)

                def project(i):
                    pe.wait_ge(xt_ready, i + 1)
                    after(pe, turned_copied, TURNS * i)
                    for n, name in enumerate(("wq", "wk")):
                        for m in range(KD):
                            for k in range(KD):
                                last = nc.tensor.matmul(turn_ps[:, 0, (n * KD + m) * SEQ:(n * KD + m + 1) * SEQ],
                                                        w_sb[name][:, k, m * 128:(m + 1) * 128], x_t[:, k, :],
                                                        start=(k == 0), stop=(k == KD - 1))
                    last.then_inc(qk_done, 1)
                    for k in range(KD):
                        last = nc.tensor.matmul(turn_ps[0:SEQ, 1, 0:DIM], x_t[:, k, :], w_sb["wv"][:, k, :],
                                                start=(k == 0), stop=(k == KD - 1))
                    last.then_inc(v_done, 1)

                def scores(i):
                    pe.wait_ge(q_ready, i + 1)
                    pe.wait_ge(k_ready, i + 1)
                    after(pe, shifted, i)
                    for b in range(4):
                        k, half = b // 2, b % 2
                        nc.tensor.matmul(score_ps[0:SEQ, b, 0:4 * SEQ], q_t[:, k, :],
                                         k_heads[:, k, 4 * half:4 * half + 4, :], start=True, stop=False)
                        last = nc.tensor.matmul(score_ps[0:SEQ, b, 0:4 * SEQ], ident_bf[0:SEQ, 0:SEQ], causal[:, :],
                                                start=False, stop=True)
                    last.then_inc(scores_done, 1)

                def turn_probs(i, t):
                    if t == 0:
                        pe.wait_ge(probs_ready, i + 1)
                        pe.wait_ge(k_ready, i + 1)
                        pe.wait_ge(q_ready, i + 1)
                        pe.wait_ge(v_ready, i + 1)
                    else:
                        pe.wait_ge(turned_copied, TURNS * i + t)
                    for h in range(HT):
                        last = nc.tensor.transpose(turn_ps[0:SEQ, h // 4, (h % 4) * SEQ:(h % 4 + 1) * SEQ],
                                                   probs[:, HT * t + h, :], ident[0:SEQ, 0:SEQ])
                    last.then_inc(turned, 1)

                def attend(i):
                    pe.wait_ge(turned_copied, TURNS * (i + 1))
                    after(pe, summed_done, i)
                    for h in range(HEADS):
                        last = nc.tensor.matmul(out_ps[0:SEQ, (HD + 1) * h:(HD + 1) * (h + 1)], probs_t[:, h, :],
                                                v_ones[:, h, :], start=True, stop=True)
                    last.then_inc(attended, 1)

                def turn_mixed(i):
                    pe.wait_ge(mixed_ready, i + 1)
                    for k in range(KD):
                        last = nc.tensor.transpose(misc_ps[:, (KD + k) * SEQ:(KD + k + 1) * SEQ],
                                                   mixed[:, k * 128:(k + 1) * 128], ident[0:SEQ, 0:SEQ])
                    last.then_inc(mixed_turned, 1)

                def project_out(i):
                    pe.wait_ge(mixed_t_ready, i + 1)
                    for k in range(KD):
                        last = nc.tensor.matmul(out_ps[0:SEQ, 0:DIM], mixed_t[:, k, :], w_sb["wo"][:, k, :],
                                                start=(k == 0), stop=(k == KD - 1))
                    last.then_inc(projected, 1)

                turn_x(0)
                project(0)
                scores(0)
                def step(i):
                    turn_probs(i - 1, 0)
                    turn_x(i)
                    turn_probs(i - 1, 1)
                    attend(i - 1)
                    project(i)
                    turn_mixed(i - 1)
                    scores(i)
                    project_out(i - 1)

                step(1)
                with pe.Fori(2, BATCH) as i:
                    step(i)
                turn_probs(BATCH - 1, 0)
                turn_probs(BATCH - 1, 1)
                attend(BATCH - 1)
                turn_mixed(BATCH - 1)
                project_out(BATCH - 1)

            @block.vector
            def _(dve):
                chain = Chain(dve, dve_chain_sem)
                FRONT_LINKS = (1 if pre_norm else 0) + 1
                BACK_LINKS = 1 + 1
                dve.wait_ge(weights_in, WEIGHTS)
                dve.wait_ge(const_ready, CONSTS)
                if x_dram is not None:
                    dve.wait_ge(x_in, 16 * (BATCH // 4))

                def norm_before(i):
                    after(dve, xt_done, i)
                    if pre_norm:
                        nc.vector.bn_stats(stats0[:, :], x_tokens[:, i, :])
                        dve.drain()
                        chain(nc.vector.bn_aggr(mean_var0[:, :], stats0[:, :]))
                        nc.vector.tensor_scalar_add(var_eps0[:, :], mean_var0[:, 1:2], LN_EPS).then_inc(var0_ready, 1)
                        dve.wait_ge(rstd0_ready, i + 1)
                        nc.vector.tensor_scalar(normed[:, :], x_tokens[:, i, :], mean_var0[:, 0:1], rstd0[:, 0:1],
                                                ALU.subtract, ALU.mult).then_inc(normed_ready, 1)
                    else:
                        nc.vector.tensor_copy(normed[:, :], x_tokens[:, i, :]).then_inc(normed_ready, 1)

                def x_turned(i):
                    dve.wait_ge(xt_done, i + 1)
                    after(dve, v_done, i)
                    if pre_norm:
                        for k in range(KD):
                            last = nc.vector.tensor_scalar(x_t[:, k, :], misc_ps[:, k * SEQ:(k + 1) * SEQ],
                                                           gain[:, k:k + 1], shift[:, k:k + 1], ALU.mult, ALU.add)
                    else:
                        last = nc.vector.tensor_copy(x_t[:, :, :], misc_ps[:, 0:KD * SEQ].rearrange("p (k s) -> p k s", k=KD))
                    last.then_inc(xt_ready, 1)

                def keys(i):
                    dve.wait_ge(qk_done, i + 1)
                    dve.wait_ge(q_ready, i + 1)
                    after(dve, scores_done, i)
                    for k in range(KD):
                        source = turn_ps[:, 0, (KD + k) * SEQ:(KD + k + 1) * SEQ]
                        last = nc.vector.scalar_tensor_tensor(
                            out=k_heads[:, k, :, :], in0=source.unsqueeze(1).to_broadcast([128, HPB, SEQ]),
                            scalar=bias_k[:, k:k + 1], in1=head_rows[:, :].unsqueeze(2).to_broadcast([128, HPB, SEQ]),
                            op0=ALU.add, op1=ALU.mult)
                    last.then_inc(k_ready, 1)

                def values(i):
                    dve.wait_ge(v_done, i + 1)
                    after(dve, attended, i)
                    nc.vector.tensor_tensor(out=v_ones[:, :, 0:HD],
                                            in0=turn_ps[0:SEQ, 1, 0:DIM].rearrange("s (h e) -> s h e", h=HEADS),
                                            in1=bias_v[:, :].rearrange("s (h e) -> s h e", h=HEADS),
                                            op=ALU.add).then_inc(v_ready, 1)

                def shift_scores(i):
                    dve.wait_ge(scores_done, i + 1)
                    after(dve, turned, TURNS * i)
                    view = score_ps[0:SEQ, :, 0:4 * SEQ].rearrange("q b (h k) -> q b h k", h=4)
                    chain(nc.vector.tensor_reduce(row_max[:, :].rearrange("q (b h) -> q b h", b=4), view, AX.X, ALU.max))
                    nc.vector.tensor_tensor(out=probs[:, :, :].rearrange("q (b h) k -> q b h k", b=4), in0=view,
                                            in1=row_max[:, :].rearrange("q (b h) -> q b h", b=4).unsqueeze(3)
                                            .to_broadcast([SEQ, 4, 4, SEQ]),
                                            op=ALU.subtract).then_inc(shifted, 1)

                def normalize(i):
                    dve.wait_ge(attended, i + 1)
                    after(dve, mixed_turned, i)
                    view = out_ps[0:SEQ, 0:HEADS * (HD + 1)].rearrange("q (h e) -> q h e", h=HEADS)
                    chain(nc.vector.reciprocal(inv_sum[:, :].unsqueeze(2), view[:, :, HD:HD + 1]))
                    nc.vector.tensor_tensor(out=mixed[:, :].rearrange("q (h e) -> q h e", h=HEADS), in0=view[:, :, 0:HD],
                                            in1=inv_sum[:, :].unsqueeze(2).to_broadcast([SEQ, HEADS, HD]),
                                            op=ALU.mult).then_inc(mixed_ready, 1)

                def mixed_copy(i):
                    dve.wait_ge(mixed_turned, i + 1)
                    after(dve, projected, i)
                    nc.vector.tensor_copy(mixed_t[:, :, :], misc_ps[:, KD * SEQ:2 * KD * SEQ]
                                          .rearrange("p (k s) -> p k s", k=KD)).then_inc(mixed_t_ready, 1)

                def residual_norm(i):
                    dve.wait_ge(projected, i + 1)
                    dve.wait_ge(x_bias_ready, i + 1)
                    nc.vector.tensor_tensor(out=summed[:, :], in0=out_ps[0:SEQ, 0:DIM], in1=x_bias[:, :],
                                            op=ALU.add).then_inc(summed_done, 1)
                    dve.wait_ge(summed_done, i + 1)
                    nc.vector.bn_stats(stats[:, :], summed[:, :])
                    dve.drain()
                    chain(nc.vector.bn_aggr(mean_var[:, :], stats[:, :]))
                    nc.vector.tensor_scalar_add(var_eps[:, :], mean_var[:, 1:2], LN_EPS).then_inc(var_ready, 1)
                    dve.wait_ge(rstd_ready, i + 1)
                    nc.vector.tensor_scalar(x_tokens[:, i, :], summed[:, :], mean_var[:, 0:1], rstd[:, 0:1],
                                            ALU.subtract, ALU.mult).then_inc(x_new, 1)

                chain.begin(0)
                norm_before(0)
                x_turned(0)
                keys(0)
                values(0)
                shift_scores(0)
                assert chain.n == FRONT_LINKS
                def step(i):
                    chain.begin(FRONT_LINKS + (i - 1) * (FRONT_LINKS + BACK_LINKS))
                    norm_before(i)
                    x_turned(i)
                    normalize(i - 1)
                    keys(i)
                    values(i)
                    mixed_copy(i - 1)
                    shift_scores(i)
                    residual_norm(i - 1)
                    assert chain.n == FRONT_LINKS + BACK_LINKS

                step(1)
                with dve.Fori(2, BATCH) as i:
                    step(i)
                chain.begin(FRONT_LINKS + (BATCH - 1) * (FRONT_LINKS + BACK_LINKS))
                normalize(BATCH - 1)
                mixed_copy(BATCH - 1)
                residual_norm(BATCH - 1)
                dve.wait_ge(x_new, BATCH)


def load_pass(nc, prefix, x_tokens, source):
    with ExitStack() as stack:
        mem = Memory(nc, stack, prefix)
        loaded = mem.sem("loaded")
        with nc.Block() as block:

            @block.sync
            def _(sp):
                for r in range(0, BATCH, 4):
                    sp.dma_start(x_tokens[:, r:r + 4, :], source[r:r + 4].rearrange("b s d -> s b d")).then_inc(loaded, 16)
                sp.wait_ge(loaded, 16 * (BATCH // 4))


def store_pass(nc, prefix, x_tokens, out):
    with ExitStack() as stack:
        mem = Memory(nc, stack, prefix)
        stored = mem.sem("stored")
        with nc.Block() as block:

            @block.sync
            def _(sp):
                for r in range(0, BATCH, 4):
                    sp.dma_start(out[r:r + 4].rearrange("b s d -> s b d"), x_tokens[:, r:r + 4, :]).then_inc(stored, 16)
                sp.wait_ge(stored, 16 * (BATCH // 4))


def constants_pass(nc, ident, minus_half):
    with ExitStack() as stack:
        mem = Memory(nc, stack, "const")
        cleared = mem.sem("cleared")
        with nc.Block() as block:

            @block.gpsimd
            def _(pool):
                nc.gpsimd.memset(minus_half[:, :], -0.5).then_inc(cleared, 1)
                nc.gpsimd.memset(ident[:, :], 0.0).then_inc(cleared, 1)
                pool.wait_ge(cleared, 2)
                nc.gpsimd.affine_select(out=ident[:, :], in_=ident[:, :], compare_op=ALU.not_equal, fill=1.0, base=0,
                                        pattern=[[-1, 128]], channel_multiplier=1).then_inc(cleared, 1)
                pool.wait_ge(cleared, 3)


def experts_pass(nc, x_tokens, ident, minus_half, wg, wu, wd, wr, temperature):
    GROUPS = BATCH // GROUP
    TOK = GROUP * SEQ
    FT = EXPERT_F // 128
    UNITS = EXPERTS * FT
    GOLDEN_CENTER = 0.36787944117144233
    GOLDEN_LOWER = 0.2123179275482191
    GOLDEN_UPPER = 0.5
    with ExitStack() as stack:
        mem = Memory(nc, stack, "moe")
        wg_sb = mem.sbuf("wg", [128, EXPERTS, KD, EXPERT_F])
        wu_sb = mem.sbuf("wu", [128, EXPERTS, KD, EXPERT_F])
        wd_sb = mem.sbuf("wd", [128, EXPERTS, FT, DIM])
        wr_sb = mem.sbuf("wr", [128, KD, EXPERTS])
        temp = mem.sbuf("temp", [SEQ, 1])
        half_inv_temp = mem.sbuf("half_inv_temp", [SEQ, 1])
        lower_expert = mem.sbuf("lower_expert", [SEQ, EXPERTS, EXPERTS])
        x_rows = mem.sbuf("x_rows", [SEQ, GROUP, DIM])
        x_t = mem.sbuf("x_t", [128, KD, TOK])
        tanh_g = mem.sbuf("tanh_g", [128, 2, TOK])
        gated = mem.sbuf("gated", [128, 2, TOK])
        hidden_t = mem.sbuf("hidden_t", [128, 2 * FT, TOK])
        total = mem.sbuf("total", [SEQ, GROUP, DIM])
        SMALL = [SEQ, GROUP, EXPERTS]
        tanh_z, inh, dist, zone, narrow, wide, rank, mix = (mem.sbuf(n, SMALL) for n in (
            "tanh_z", "inh", "dist", "zone", "narrow", "wide", "rank", "mix"))
        greater = mem.sbuf("greater", [SEQ, GROUP, EXPERTS, EXPERTS])
        equal = mem.sbuf("equal", [SEQ, GROUP, EXPERTS, EXPERTS])
        weight_sum = mem.sbuf("weight_sum", [SEQ, GROUP])
        nobody = mem.sbuf("nobody", [SEQ, GROUP])
        stats = mem.sbuf("stats", [SEQ, GROUP, 6])
        mean_var = mem.sbuf("mean_var", [SEQ, GROUP, 2])
        var_eps = mem.sbuf("var_eps", [SEQ, GROUP])
        rstd = mem.sbuf("rstd", [SEQ, GROUP])

        gate_ps = mem.psum("gate_ps", [128, 2, BANK])
        up_ps = mem.psum("up_ps", [128, 2, BANK])
        out_ps = mem.psum("out_ps", [128, 2, BANK])
        xt_ps = mem.psum("xt_ps", [128, KD, BANK])

        weights_in, consts_ready = mem.sem("weights_in"), mem.sem("consts_ready")
        dve_chain_sem, pool_chain_sem = mem.sem("dve_order"), mem.sem("pool_order")
        xt_done, xt_ready, logits_done = mem.sem("xt_done"), mem.sem("xt_ready"), mem.sem("logits_done")
        router_tanh, distance_ready, router_exp = mem.sem("router_tanh"), mem.sem("distance_ready"), mem.sem("router_exp")
        gate_up_done, tanh_ready = mem.sem("gate_up_done"), mem.sem("tanh_ready")
        hidden_ready, down_done, added = mem.sem("hidden_ready"), mem.sem("down_done"), mem.sem("added")
        var_ready, rstd_ready, x_new = mem.sem("var_ready"), mem.sem("rstd_ready"), mem.sem("x_new")
        temp_ready, rows_ready = mem.sem("temp_ready"), mem.sem("rows_ready")
        WEIGHTS = 16 * 5

        with nc.Block() as block:

            @block.sync
            def _(sp):
                sp.dma_start(wr_sb[:, :, :], wr.rearrange("(k p) e -> p k e", p=128)).then_inc(weights_in, 16)
                sp.dma_start(temp[:, :], temperature.partition_broadcast(SEQ)).then_inc(weights_in, 16)
                sp.dma_start(wg_sb[:, :, :, :], wg.rearrange("e (k p) f -> p e k f", p=128)).then_inc(weights_in, 16)
                sp.dma_start(wu_sb[:, :, :, :], wu.rearrange("e (k p) f -> p e k f", p=128)).then_inc(weights_in, 16)
                sp.dma_start(wd_sb[:, :, :, :], wd.rearrange("e (k p) d -> p e k d", p=128)).then_inc(weights_in, 16)
                sp.wait_ge(weights_in, WEIGHTS)

            @block.gpsimd
            def _(pool):
                chain = Chain(pool, pool_chain_sem)
                chain(nc.gpsimd.memset(lower_expert[:, :, :], 1.0))
                nc.gpsimd.affine_select(out=lower_expert[:, :, :], in_=lower_expert[:, :, :], compare_op=ALU.is_gt,
                                        fill=0.0, base=0, pattern=[[1, EXPERTS], [-1, EXPERTS]],
                                        channel_multiplier=0).then_inc(consts_ready, 1)
                with pool.Fori(0, GROUPS) as g:
                    pool.wait_ge(var_ready, g + 1)
                    nc.gpsimd.tensor_tensor(out=rstd[:, :], in0=var_eps[:, :],
                                            in1=minus_half[0:SEQ, :].to_broadcast([SEQ, GROUP]),
                                            op=ALU.pow).then_inc(rstd_ready, 1)

            @block.scalar
            def _(act):
                act.wait_ge(weights_in, WEIGHTS)
                act.wait_ge(temp_ready, 1)

                def gate_tanh(g, u):
                    act.wait_ge(gate_up_done, UNITS * g + u + 1)
                    if u >= 2:
                        act.wait_ge(hidden_ready, UNITS * g + u - 1)
                    else:
                        after(act, hidden_ready, UNITS * g)
                    nc.scalar.activation(tanh_g[:, u % 2, :], gate_ps[:, u % 2, 0:TOK], ACT.Tanh,
                                         scale=0.5).then_inc(tanh_ready, 1)

                def step(g):
                    act.wait_ge(logits_done, g + 1)
                    nc.scalar.activation(tanh_z[:, :, :],
                                         xt_ps[0:SEQ, 0, TOK:TOK + GROUP * EXPERTS].rearrange("s (r e) -> s r e", r=GROUP),
                                         ACT.Tanh, scale=half_inv_temp[:, 0:1]).then_inc(router_tanh, 1)
                    gate_tanh(g, 0)
                    act.wait_ge(distance_ready, g + 1)
                    nc.scalar.activation(narrow[:, :, :], dist[:, :, :], ACT.Exp, scale=-1.0 / 0.1)
                    nc.scalar.activation(wide[:, :, :], dist[:, :, :], ACT.Exp, scale=-1.0 / 0.3).then_inc(router_exp, 1)
                    for u in range(1, UNITS):
                        gate_tanh(g, u)

                step(0)
                with act.Fori(1, GROUPS) as g:
                    step(g)

            @block.tensor
            def _(pe):
                pe.wait_ge(weights_in, WEIGHTS)

                def gate_up(g, u):
                    e, f = u // FT, u % FT
                    if u >= 2:
                        pe.wait_ge(hidden_ready, UNITS * g + u - 1)
                    else:
                        after(pe, hidden_ready, UNITS * g)
                    for w, ps in ((wg_sb, gate_ps), (wu_sb, up_ps)):
                        for k in range(KD):
                            last = nc.tensor.matmul(ps[:, u % 2, 0:TOK], w[:, e, k, f * 128:(f + 1) * 128], x_t[:, k, :],
                                                    start=(k == 0), stop=(k == KD - 1))
                    last.then_inc(gate_up_done, 1)

                def down(g, e):
                    pe.wait_ge(hidden_ready, UNITS * g + FT * (e + 1))
                    if e:
                        pe.wait_ge(added, EXPERTS * g + e)
                    else:
                        after(pe, added, EXPERTS * g)
                    for r in range(GROUP):
                        for k in range(FT):
                            last = nc.tensor.matmul(out_ps[0:SEQ, r // 2, (r % 2) * DIM:(r % 2 + 1) * DIM],
                                                    hidden_t[:, (FT * e + k) % (2 * FT), r * SEQ:(r + 1) * SEQ],
                                                    wd_sb[:, e, k, :], start=(k == 0), stop=(k == FT - 1))
                    last.then_inc(down_done, 1)

                def step(g):
                    pe.wait_ge(rows_ready, g + 1)
                    after(pe, router_tanh, g)
                    for k in range(KD):
                        for r in range(GROUP):
                            last = nc.tensor.transpose(xt_ps[:, k, r * SEQ:(r + 1) * SEQ],
                                                       x_rows[:, r, k * 128:(k + 1) * 128], ident[0:SEQ, 0:SEQ])
                    last.then_inc(xt_done, 1)
                    pe.wait_ge(xt_ready, g + 1)
                    for r in range(GROUP):
                        for k in range(KD):
                            last = nc.tensor.matmul(xt_ps[0:SEQ, 0, TOK + r * EXPERTS:TOK + (r + 1) * EXPERTS],
                                                    x_t[:, k, r * SEQ:(r + 1) * SEQ], wr_sb[:, k, :],
                                                    start=(k == 0), stop=(k == KD - 1))
                    last.then_inc(logits_done, 1)
                    for e in range(EXPERTS):
                        for f in range(FT):
                            gate_up(g, FT * e + f)
                        if e:
                            down(g, e - 1)
                    down(g, EXPERTS - 1)

                step(0)
                with pe.Fori(1, GROUPS) as g:
                    step(g)

            @block.vector
            def _(dve):
                chain = Chain(dve, dve_chain_sem)
                LINKS = 24 + UNITS + 1
                dve.wait_ge(weights_in, WEIGHTS)
                dve.wait_ge(consts_ready, 1)
                chain.begin(0)
                chain(nc.vector.reciprocal(half_inv_temp[:, :], temp[:, :]))
                nc.vector.tensor_scalar(half_inv_temp[:, :], half_inv_temp[:, :], 0.5, None, ALU.mult).then_inc(temp_ready, 1)

                def gather_rows(g):
                    after(dve, xt_done, g)
                    nc.vector.tensor_copy(x_rows[:, :, :], x_tokens[:, bass.ds(g * GROUP, GROUP), :]).then_inc(rows_ready, 1)

                def distances(g):
                    dve.wait_ge(router_tanh, g + 1)
                    chain(nc.vector.tensor_scalar(inh[:, :, :], tanh_z[:, :, :], 0.5, 0.5, ALU.mult, ALU.add))
                    chain(nc.vector.tensor_scalar(dist[:, :, :], inh[:, :, :], GOLDEN_CENTER, None, ALU.subtract))
                    nc.vector.scalar_tensor_tensor(out=dist[:, :, :], in0=dist[:, :, :], scalar=-1.0, in1=dist[:, :, :],
                                                   op0=ALU.mult, op1=ALU.max).then_inc(distance_ready, 1)
                    chain(nc.vector.tensor_scalar(zone[:, :, :], inh[:, :, :], GOLDEN_LOWER, None, ALU.is_ge))
                    chain(nc.vector.scalar_tensor_tensor(out=zone[:, :, :], in0=inh[:, :, :], scalar=GOLDEN_UPPER,
                                                         in1=zone[:, :, :], op0=ALU.is_le, op1=ALU.mult))

                def route(g):
                    dve.wait_ge(router_exp, g + 1)
                    ej = [SEQ, GROUP, EXPERTS, EXPERTS]
                    of_j, of_e = wide[:, :, :].unsqueeze(2).to_broadcast(ej), wide[:, :, :].unsqueeze(3).to_broadcast(ej)
                    nc.vector.tensor_tensor(out=greater[:, :, :, :], in0=of_j, in1=of_e, op=ALU.is_gt)
                    chain(nc.vector.tensor_tensor(out=equal[:, :, :, :], in0=of_j, in1=of_e, op=ALU.is_equal))
                    chain(nc.vector.tensor_tensor(out=equal[:, :, :, :], in0=equal[:, :, :, :],
                                                  in1=lower_expert[:, :, :].unsqueeze(1).to_broadcast(ej), op=ALU.mult))
                    chain(nc.vector.tensor_tensor(out=greater[:, :, :, :], in0=greater[:, :, :, :], in1=equal[:, :, :, :],
                                                  op=ALU.add))
                    chain(nc.vector.tensor_reduce(rank[:, :, :], greater[:, :, :, :], AX.X, ALU.add))
                    chain(nc.vector.scalar_tensor_tensor(out=wide[:, :, :], in0=rank[:, :, :], scalar=2.0,
                                                         in1=wide[:, :, :], op0=ALU.is_lt, op1=ALU.mult))
                    chain(nc.vector.tensor_reduce(weight_sum[:, :], wide[:, :, :], AX.X, ALU.add))
                    chain(nc.vector.tensor_scalar(weight_sum[:, :], weight_sum[:, :], 1e-8, None, ALU.max))
                    chain(nc.vector.reciprocal(weight_sum[:, :], weight_sum[:, :]))
                    chain(nc.vector.tensor_tensor(out=wide[:, :, :], in0=wide[:, :, :],
                                                  in1=weight_sum[:, :].unsqueeze(2).to_broadcast(SMALL), op=ALU.mult))
                    chain(nc.vector.tensor_tensor(out=narrow[:, :, :], in0=narrow[:, :, :], in1=zone[:, :, :], op=ALU.mult))
                    chain(nc.vector.tensor_reduce(weight_sum[:, :], narrow[:, :, :], AX.X, ALU.add))
                    chain(nc.vector.tensor_scalar(nobody[:, :], weight_sum[:, :], 1e-8, None, ALU.is_lt))
                    chain(nc.vector.tensor_tensor(out=wide[:, :, :], in0=wide[:, :, :],
                                                  in1=nobody[:, :].unsqueeze(2).to_broadcast(SMALL), op=ALU.mult))
                    chain(nc.vector.tensor_scalar(nobody[:, :], nobody[:, :], -1.0, 1.0, ALU.mult, ALU.add))
                    chain(nc.vector.tensor_tensor(out=narrow[:, :, :], in0=narrow[:, :, :],
                                                  in1=nobody[:, :].unsqueeze(2).to_broadcast(SMALL), op=ALU.mult))
                    chain(nc.vector.tensor_tensor(out=narrow[:, :, :], in0=narrow[:, :, :], in1=wide[:, :, :], op=ALU.add))
                    chain(nc.vector.tensor_reduce(weight_sum[:, :], narrow[:, :, :], AX.X, ALU.add))
                    chain(nc.vector.tensor_scalar(weight_sum[:, :], weight_sum[:, :], 1e-8, None, ALU.max))
                    chain(nc.vector.reciprocal(weight_sum[:, :], weight_sum[:, :]))
                    chain(nc.vector.tensor_tensor(out=mix[:, :, :], in0=narrow[:, :, :],
                                                  in1=weight_sum[:, :].unsqueeze(2).to_broadcast(SMALL), op=ALU.mult))

                def hidden(g, u):
                    dve.wait_ge(tanh_ready, UNITS * g + u + 1)
                    if u >= 2 * FT:
                        dve.wait_ge(down_done, EXPERTS * g + u // FT - 1)
                    else:
                        after(dve, down_done, EXPERTS * g)
                    chain(nc.vector.scalar_tensor_tensor(out=gated[:, u % 2, :], in0=tanh_g[:, u % 2, :], scalar=1.0,
                                                         in1=gate_ps[:, u % 2, 0:TOK], op0=ALU.add, op1=ALU.mult))
                    nc.vector.scalar_tensor_tensor(out=hidden_t[:, u % (2 * FT), :], in0=gated[:, u % 2, :], scalar=0.5,
                                                   in1=up_ps[:, u % 2, 0:TOK], op0=ALU.mult,
                                                   op1=ALU.mult).then_inc(hidden_ready, 1)

                def add_expert(g, e):
                    dve.wait_ge(down_done, EXPERTS * g + e + 1)
                    if e:
                        dve.wait_ge(added, EXPERTS * g + e)
                    for r in range(GROUP):
                        base = total[:, r, :] if e else x_tokens[:, g * GROUP + r, :]
                        last = nc.vector.scalar_tensor_tensor(
                            out=total[:, r, :], in0=out_ps[0:SEQ, r // 2, (r % 2) * DIM:(r % 2 + 1) * DIM],
                            scalar=mix[:, r, e:e + 1], in1=base, op0=ALU.mult, op1=ALU.add)
                    last.then_inc(added, 1)

                def layer_norm(g):
                    dve.wait_ge(added, EXPERTS * (g + 1))
                    for r in range(GROUP):
                        nc.vector.bn_stats(stats[:, r, :], total[:, r, :])
                    dve.drain()
                    for r in range(GROUP):
                        last = nc.vector.bn_aggr(mean_var[:, r, :], stats[:, r, :])
                    chain(last)
                    nc.vector.tensor_scalar_add(var_eps[:, :], mean_var[:, :, 1], LN_EPS).then_inc(var_ready, 1)
                    dve.wait_ge(rstd_ready, g + 1)
                    for r in range(GROUP):
                        last = nc.vector.tensor_scalar(x_tokens[:, g * GROUP + r, :], total[:, r, :], mean_var[:, r, 0:1],
                                                       rstd[:, r:r + 1], ALU.subtract, ALU.mult)
                    last.then_inc(x_new, 1)

                def step(g):
                    chain.begin(1 + g * LINKS)
                    gather_rows(g)
                    dve.wait_ge(xt_done, g + 1)
                    after(dve, gate_up_done, UNITS * g)
                    nc.vector.tensor_copy(x_t[:, :, :], xt_ps[:, :, 0:TOK]).then_inc(xt_ready, 1)
                    distances(g)
                    hidden(g, 0)
                    route(g)
                    hidden(g, 1)
                    for e in range(1, EXPERTS):
                        for f in range(FT):
                            hidden(g, FT * e + f)
                        add_expert(g, e - 1)
                    add_expert(g, EXPERTS - 1)
                    layer_norm(g)
                    assert chain.n == LINKS

                step(0)
                with dve.Fori(1, GROUPS) as g:
                    step(g)
                dve.wait_ge(x_new, GROUPS)


def quantized_ffn_pass(nc, x_tokens, ident, minus_half, w_gate, w_up, w_down, s_gate, s_up, s_down):
    GROUPS = BATCH // GROUP
    TOK = GROUP * SEQ
    FT = INTER // 128
    with ExitStack() as stack:
        mem = Memory(nc, stack, "qffn")
        packed = mem.sbuf("packed", [128, KD, INTER // 4], mybir.dt.int32)
        packed_up = mem.sbuf("packed_up", [128, KD, INTER // 4], mybir.dt.int32)
        packed_down = mem.sbuf("packed_down", [128, FT, DIM // 4], mybir.dt.int32)
        gate_sb = mem.sbuf("gate_w", [128, KD, INTER])
        up_sb = mem.sbuf("up_w", [128, KD, INTER])
        down_sb = mem.sbuf("down_w", [128, FT, DIM])
        gate_scale = mem.sbuf("gate_scale", [128, FT])
        up_scale = mem.sbuf("up_scale", [128, FT])
        half_gate_scale = mem.sbuf("half_gate_scale", [128, FT])
        product_scale = mem.sbuf("product_scale", [128, FT])
        down_scale = mem.sbuf("down_scale", [SEQ, DIM])
        x_rows = mem.sbuf("x_rows", [SEQ, GROUP, DIM])
        x_t = mem.sbuf("x_t", [128, KD, TOK])
        tanh_g = mem.sbuf("tanh_g", [128, 2, TOK])
        gated = mem.sbuf("gated", [128, 2, TOK])
        hidden_t = mem.sbuf("hidden_t", [128, FT, TOK])
        total = mem.sbuf("total", [SEQ, GROUP, DIM])
        stats = mem.sbuf("stats", [SEQ, GROUP, 6])
        mean_var = mem.sbuf("mean_var", [SEQ, GROUP, 2])
        var_eps = mem.sbuf("var_eps", [SEQ, GROUP])
        rstd = mem.sbuf("rstd", [SEQ, GROUP])

        gate_ps = mem.psum("gate_ps", [128, 2, BANK])
        up_ps = mem.psum("up_ps", [128, 2, BANK])
        out_ps = mem.psum("out_ps", [128, 2, BANK])
        xt_ps = mem.psum("xt_ps", [128, KD, BANK])

        weights_in, weights_ready, scales_ready = mem.sem("weights_in"), mem.sem("weights_ready"), mem.sem("scales_ready")
        dve_chain_sem = mem.sem("dve_order")
        rows_ready, xt_done, xt_ready = mem.sem("rows_ready"), mem.sem("xt_done"), mem.sem("xt_ready")
        gate_up_done, tanh_ready, hidden_ready = mem.sem("gate_up_done"), mem.sem("tanh_ready"), mem.sem("hidden_ready")
        down_done, summed = mem.sem("down_done"), mem.sem("summed")
        var_ready, rstd_ready, x_new = mem.sem("var_ready"), mem.sem("rstd_ready"), mem.sem("x_new")
        WEIGHTS = 16 * 6

        with nc.Block() as block:

            @block.sync
            def _(sp):
                sp.dma_start(packed[:, :, :], w_gate.rearrange("(k p) n -> p k n", p=128)).then_inc(weights_in, 16)
                sp.dma_start(packed_up[:, :, :], w_up.rearrange("(k p) n -> p k n", p=128)).then_inc(weights_in, 16)
                sp.dma_start(packed_down[:, :, :], w_down.rearrange("(k p) n -> p k n", p=128)).then_inc(weights_in, 16)
                with nc.allow_non_contiguous_dma(reason="scales, once"):
                    sp.dma_start(gate_scale[:, :], s_gate.rearrange("(t p) -> p t", p=128)).then_inc(weights_in, 16)
                    sp.dma_start(up_scale[:, :], s_up.rearrange("(t p) -> p t", p=128)).then_inc(weights_in, 16)
                sp.dma_start(down_scale[:, :], s_down.partition_broadcast(SEQ)).then_inc(weights_in, 16)
                sp.wait_ge(weights_in, WEIGHTS)

            @block.gpsimd
            def _(pool):
                with pool.Fori(0, GROUPS) as g:
                    pool.wait_ge(var_ready, g + 1)
                    nc.gpsimd.tensor_tensor(out=rstd[:, :], in0=var_eps[:, :],
                                            in1=minus_half[0:SEQ, :].to_broadcast([SEQ, GROUP]),
                                            op=ALU.pow).then_inc(rstd_ready, 1)

            @block.scalar
            def _(act):
                act.wait_ge(weights_in, WEIGHTS)
                nc.scalar.activation(up_sb[:, :, :], packed_up[:, :, :].bitcast(I8), ACT.Copy).then_inc(weights_ready, 1)
                act.wait_ge(scales_ready, 1)

                def gate_tanh(g, u):
                    act.wait_ge(gate_up_done, FT * g + u + 1)
                    if u >= 2:
                        act.wait_ge(hidden_ready, FT * g + u - 1)
                    else:
                        after(act, hidden_ready, FT * g)
                    nc.scalar.activation(tanh_g[:, u % 2, :], gate_ps[:, u % 2, 0:TOK], ACT.Tanh,
                                         scale=half_gate_scale[:, u:u + 1]).then_inc(tanh_ready, 1)

                def step(g):
                    for u in range(FT):
                        gate_tanh(g, u)

                step(0)
                with act.Fori(1, GROUPS) as g:
                    step(g)

            @block.tensor
            def _(pe):
                pe.wait_ge(weights_ready, 3)

                def gate_up(g, u):
                    if u >= 2:
                        pe.wait_ge(hidden_ready, FT * g + u - 1)
                    else:
                        after(pe, hidden_ready, FT * g)
                    for w, ps in ((gate_sb, gate_ps), (up_sb, up_ps)):
                        for k in range(KD):
                            last = nc.tensor.matmul(ps[:, u % 2, 0:TOK], w[:, k, u * 128:(u + 1) * 128], x_t[:, k, :],
                                                    start=(k == 0), stop=(k == KD - 1))
                    last.then_inc(gate_up_done, 1)

                def step(g):
                    pe.wait_ge(rows_ready, g + 1)
                    after(pe, xt_ready, g)
                    for k in range(KD):
                        for r in range(GROUP):
                            last = nc.tensor.transpose(xt_ps[:, k, r * SEQ:(r + 1) * SEQ],
                                                       x_rows[:, r, k * 128:(k + 1) * 128], ident[0:SEQ, 0:SEQ])
                    last.then_inc(xt_done, 1)
                    pe.wait_ge(xt_ready, g + 1)
                    for u in range(FT):
                        gate_up(g, u)
                    pe.wait_ge(hidden_ready, FT * (g + 1))
                    after(pe, summed, g)
                    for r in range(GROUP):
                        for k in range(FT):
                            last = nc.tensor.matmul(out_ps[0:SEQ, r // 2, (r % 2) * DIM:(r % 2 + 1) * DIM],
                                                    hidden_t[:, k, r * SEQ:(r + 1) * SEQ], down_sb[:, k, :],
                                                    start=(k == 0), stop=(k == FT - 1))
                    last.then_inc(down_done, 1)

                step(0)
                with pe.Fori(1, GROUPS) as g:
                    step(g)

            @block.vector
            def _(dve):
                chain = Chain(dve, dve_chain_sem)
                LINKS = FT + 2
                dve.wait_ge(weights_in, WEIGHTS)
                nc.vector.tensor_copy(gate_sb[:, :, :], packed[:, :, :].bitcast(I8)).then_inc(weights_ready, 1)
                nc.vector.tensor_copy(down_sb[:, :, :], packed_down[:, :, :].bitcast(I8)).then_inc(weights_ready, 1)
                chain.begin(0)
                chain(nc.vector.tensor_scalar(half_gate_scale[:, :], gate_scale[:, :], 0.5, None, ALU.mult))
                nc.vector.tensor_tensor(out=product_scale[:, :], in0=half_gate_scale[:, :], in1=up_scale[:, :],
                                        op=ALU.mult).then_inc(scales_ready, 1)
                dve.wait_ge(scales_ready, 1)

                def hidden(g, u):
                    dve.wait_ge(tanh_ready, FT * g + u + 1)
                    after(dve, down_done, g)
                    chain(nc.vector.scalar_tensor_tensor(out=gated[:, u % 2, :], in0=tanh_g[:, u % 2, :], scalar=1.0,
                                                         in1=gate_ps[:, u % 2, 0:TOK], op0=ALU.add, op1=ALU.mult))
                    nc.vector.scalar_tensor_tensor(out=hidden_t[:, u, :], in0=gated[:, u % 2, :],
                                                   scalar=product_scale[:, u:u + 1],
                                                   in1=up_ps[:, u % 2, 0:TOK], op0=ALU.mult,
                                                   op1=ALU.mult).then_inc(hidden_ready, 1)

                def step(g):
                    chain.begin(1 + g * LINKS)
                    after(dve, xt_done, g)
                    nc.vector.tensor_copy(x_rows[:, :, :], x_tokens[:, bass.ds(g * GROUP, GROUP), :]).then_inc(rows_ready, 1)
                    dve.wait_ge(xt_done, g + 1)
                    after(dve, gate_up_done, FT * g)
                    nc.vector.tensor_copy(x_t[:, :, :], xt_ps[:, :, 0:TOK]).then_inc(xt_ready, 1)
                    for u in range(FT):
                        hidden(g, u)
                    dve.wait_ge(down_done, g + 1)
                    view = out_ps[0:SEQ, :, :].rearrange("s b (r d) -> s (b r) d", r=2)
                    chain(nc.vector.tensor_tensor(out=total[:, :, :], in0=view,
                                                  in1=down_scale[:, :].unsqueeze(1).to_broadcast([SEQ, GROUP, DIM]),
                                                  op=ALU.mult))
                    nc.vector.tensor_tensor(out=total[:, :, :], in0=total[:, :, :],
                                            in1=x_tokens[:, bass.ds(g * GROUP, GROUP), :], op=ALU.add).then_inc(summed, 1)
                    dve.wait_ge(summed, g + 1)
                    for r in range(GROUP):
                        nc.vector.bn_stats(stats[:, r, :], total[:, r, :])
                    dve.drain()
                    for r in range(GROUP):
                        last = nc.vector.bn_aggr(mean_var[:, r, :], stats[:, r, :])
                    chain(last)
                    nc.vector.tensor_scalar_add(var_eps[:, :], mean_var[:, :, 1], LN_EPS).then_inc(var_ready, 1)
                    dve.wait_ge(rstd_ready, g + 1)
                    for r in range(GROUP):
                        last = nc.vector.tensor_scalar(x_tokens[:, g * GROUP + r, :], total[:, r, :], mean_var[:, r, 0:1],
                                                       rstd[:, r:r + 1], ALU.subtract, ALU.mult)
                    last.then_inc(x_new, 1)
                    assert chain.n == LINKS

                step(0)
                with dve.Fori(1, GROUPS) as g:
                    step(g)
                dve.wait_ge(x_new, GROUPS)


TILES = 12
TILE = 120
LAST = CTX - (TILES - 1) * TILE
FOUR = 4
CHUNKS = TILES // FOUR


def tile_rows(t):
    return LAST if t == TILES - 1 else TILE


def chunk_columns(c):
    return c * FOUR * TILE, sum(tile_rows(t) for t in range(FOUR * c, FOUR * c + FOUR))


def load_context(engine, destination, ctx_row, arrived):
    body = (TILES - 1) * TILE
    engine.dma_start(destination[0:TILE, 0:TILES - 1, :],
                     ctx_row[0:body].rearrange("(p t) d -> p t d", t=TILES - 1)).then_inc(arrived, 16)
    engine.dma_start(destination[0:LAST, TILES - 1, :], ctx_row[body:CTX]).then_inc(arrived, 16)


def memory_attention_pass(nc, x_tokens, ctx, mask_words, ident, minus_half):
    SCALE = float(DIM) ** -0.5
    HIDDEN = NEG / SCALE
    TURNS = 1 + KD * CHUNKS
    with ExitStack() as stack:
        mem = Memory(nc, stack, "memory")
        keys = [mem.sbuf(f"keys{p}", [LAST, TILES, DIM]) for p in range(2)]
        keys_t = [mem.sbuf(f"keys_t{p}", [128, KD, CTX]) for p in range(2)]
        mask_row = [mem.sbuf(f"mask_row{p}", [1, CTX // 4], mybir.dt.int32) for p in range(2)]
        mask_bias = [mem.sbuf(f"mask_bias{p}", [1, CTX], BF16) for p in range(2)]
        ones_row = mem.sbuf("ones_row", [1, SEQ], BF16)
        x_row = [mem.sbuf(f"x_row{p}", [SEQ, DIM]) for p in range(2)]
        x_t = mem.sbuf("x_t", [128, KD, SEQ])
        probs = mem.sbuf("probs", [SEQ, CTX])
        probs_t = mem.sbuf("probs_t", [LAST, TILES, SEQ])
        part_max = mem.sbuf("part_max", [SEQ, 2])
        row_max = mem.sbuf("row_max", [SEQ, 1])
        neg_max = mem.sbuf("neg_max", [SEQ, 1])
        any_key = mem.sbuf("any_key", [SEQ, 1])
        part_sum = mem.sbuf("part_sum", [SEQ, 2])
        inv_sum = mem.sbuf("inv_sum", [SEQ, 1])
        factor = mem.sbuf("factor", [SEQ, 1])
        summed = mem.sbuf("summed", [SEQ, DIM])
        stats = mem.sbuf("stats", [SEQ, 6])
        mean_var = mem.sbuf("mean_var", [SEQ, 2])
        var_eps = mem.sbuf("var_eps", [SEQ, 1])
        rstd = mem.sbuf("rstd", [SEQ, 1])

        turn_ps = mem.psum("turn_ps", [128, 2, BANK])
        score_ps = mem.psum("score_ps", [128, CHUNKS, BANK])
        probs_ps = mem.psum("probs_ps", [128, 2, BANK])
        out_ps = mem.psum("out_ps", [128, BANK])

        keys_in = [mem.sem(f"keys_in{p}") for p in range(2)]
        mask_in = [mem.sem(f"mask_in{p}") for p in range(2)]
        ones_ready, dve_chain_sem, pool_chain_sem = mem.sem("ones_ready"), mem.sem("dve_order"), mem.sem("pool_order")
        x_row_ready, mask_ready = mem.sem("x_row_ready"), mem.sem("mask_ready")
        turned = mem.sem("turned")
        copied_dve, copied_act = mem.sem("copied_dve"), mem.sem("copied_act")
        scores_done, max_ready, probs_ready = mem.sem("scores_done"), mem.sem("max_ready"), mem.sem("probs_ready")
        probs_turned, probs_copied, attended = mem.sem("probs_turned"), mem.sem("probs_copied"), mem.sem("attended")
        summed_done, var_ready, rstd_ready, x_new = (mem.sem("summed_done"), mem.sem("var_ready"),
                                                     mem.sem("rstd_ready"), mem.sem("x_new"))
        DVE_TURNS, ACT_TURNS = (TURNS + 1) // 2, TURNS // 2

        def turn_bank(p, u):
            return turn_ps[:, (TURNS * p + u) % 2, :]

        def previous_copied(engine, b, u):
            back = u - 2
            row = b if back >= 0 else b - 1
            back %= TURNS
            if back % 2 == 0:
                after(engine, copied_dve, DVE_TURNS * row + back // 2 + 1 if not isinstance(row, int) or row >= 0 else 0)
            else:
                after(engine, copied_act, ACT_TURNS * row + back // 2 + 1 if not isinstance(row, int) or row >= 0 else 0)

        with nc.Block() as block:

            @block.sync
            def _(sp):
                def load(b, p):
                    after(sp, attended, b - 1 if not isinstance(b, int) or b >= 1 else 0)
                    load_context(sp, keys[p], ctx[b], keys_in[p])
                    after(sp, mask_ready, b - 1 if not isinstance(b, int) or b >= 1 else 0)
                    sp.dma_start(mask_row[p][:, :], mask_words[bass.ds(b, 1), :]).then_inc(mask_in[p], 16)

                load(0, 0)
                load(1, 1)
                with sp.Fori(1, BATCH // 2) as j:
                    load(2 * j, 0)
                    load(2 * j + 1, 1)

            @block.gpsimd
            def _(pool):
                nc.gpsimd.memset(ones_row[:, :], 1.0).then_inc(ones_ready, 1)

                def front(b, p):
                    after(pool, summed_done, b - 1 if not isinstance(b, int) or b >= 1 else 0)
                    nc.gpsimd.tensor_copy(x_row[p][:, :], x_tokens[:, b, :]).then_inc(x_row_ready, 1)

                def back(b):
                    pool.wait_ge(var_ready, b + 1)
                    nc.gpsimd.tensor_tensor(out=rstd[:, :], in0=var_eps[:, :], in1=minus_half[0:SEQ, :],
                                            op=ALU.pow).then_inc(rstd_ready, 1)

                front(0, 0)
                front(1, 1)
                back(0)
                with pool.Fori(1, BATCH // 2) as j:
                    for p in range(2):
                        front(2 * j + p, p)
                        back(2 * j + p - 1)
                back(BATCH - 1)

            @block.scalar
            def _(act):
                def key_copy(b, p, u):
                    act.wait_ge(turned, TURNS * b + u + 1)
                    if u == 1:
                        after(act, scores_done, b - 1 if not isinstance(b, int) or b >= 1 else 0)
                    k, c = (u - 1) // CHUNKS, (u - 1) % CHUNKS
                    at, width = chunk_columns(c)
                    nc.scalar.activation(keys_t[p][:, k, at:at + width], turn_bank(p, u)[:, 0:width],
                                         ACT.Copy).then_inc(copied_act, 1)

                def exponentials(b):
                    act.wait_ge(max_ready, b + 1)
                    after(act, probs_turned, CHUNKS * b)
                    body = 2 * FOUR * TILE
                    nc.scalar.activation(probs[:, 0:body].rearrange("q (c k) -> q c k", c=2),
                                         score_ps[0:SEQ, 0:2, 0:FOUR * TILE], ACT.Exp, bias=neg_max[:, 0:1],
                                         scale=SCALE, accum_out=part_sum[:, 0:1])
                    nc.scalar.activation(probs[:, body:CTX], score_ps[0:SEQ, 2, 0:CTX - body], ACT.Exp,
                                         bias=neg_max[:, 0:1], scale=SCALE,
                                         accum_out=part_sum[:, 1:2]).then_inc(probs_ready, 1)

                def probs_copy(b, p, c):
                    act.wait_ge(probs_turned, CHUNKS * b + c + 1)
                    if c == 0:
                        after(act, attended, b)
                    bank = probs_ps[:, (CHUNKS * p + c) % 2, :]
                    full = FOUR if c < CHUNKS - 1 else FOUR - 1
                    last = nc.scalar.activation(probs_t[0:TILE, FOUR * c:FOUR * c + full, :],
                                                bank[0:TILE, 0:full * SEQ].rearrange("k (t q) -> k t q", t=full), ACT.Copy)
                    if full < FOUR:
                        last = nc.scalar.activation(probs_t[0:LAST, TILES - 1, :], bank[0:LAST, full * SEQ:FOUR * SEQ],
                                                    ACT.Copy)
                    last.then_inc(probs_copied, 1)

                def step(b, p):
                    for u in range(1, TURNS, 2):
                        key_copy(b, p, u)
                    for c in range(CHUNKS):
                        probs_copy(b - 1, 1 - p, c)
                    exponentials(b)

                for u in range(1, TURNS, 2):
                    key_copy(0, 0, u)
                exponentials(0)
                step(1, 1)
                with act.Fori(1, BATCH // 2) as j:
                    for p in range(2):
                        step(2 * j + p, p)
                for c in range(CHUNKS):
                    probs_copy(BATCH - 1, 1, c)

            @block.tensor
            def _(pe):
                pe.wait_ge(ones_ready, 1)

                def turn(b, p, j, u):
                    if u == 0:
                        pe.wait_ge(x_row_ready, b + 1)
                    if u == 1:
                        pe.wait_ge(keys_in[p], 32 * (j + 1))
                    previous_copied(pe, b, u)
                    bank = turn_bank(p, u)
                    if u == 0:
                        for k in range(KD):
                            last = nc.tensor.transpose(bank[:, k * SEQ:(k + 1) * SEQ],
                                                       x_row[p][:, k * 128:(k + 1) * 128], ident[0:SEQ, 0:SEQ])
                    else:
                        k, c = (u - 1) // CHUNKS, (u - 1) % CHUNKS
                        for n in range(FOUR):
                            t = FOUR * c + n
                            rows = tile_rows(t)
                            last = nc.tensor.transpose(bank[:, n * TILE:n * TILE + rows],
                                                       keys[p][0:rows, t, k * 128:(k + 1) * 128], ident[0:rows, 0:rows])
                    last.then_inc(turned, 1)

                def scores(b, p):
                    pe.wait_ge(mask_ready, b + 1)
                    pe.wait_ge(copied_dve, DVE_TURNS * (b + 1))
                    pe.wait_ge(copied_act, ACT_TURNS * (b + 1))
                    after(pe, probs_ready, b)
                    for c in range(CHUNKS):
                        at, width = chunk_columns(c)
                        nc.tensor.matmul(score_ps[0:SEQ, c, 0:width], ones_row[:, :], mask_bias[p][:, at:at + width],
                                         start=True, stop=False)
                        for k in range(KD):
                            last = nc.tensor.matmul(score_ps[0:SEQ, c, 0:width], x_t[:, k, :],
                                                    keys_t[p][:, k, at:at + width], start=False, stop=(k == KD - 1))
                    last.then_inc(scores_done, 1)

                def turn_probs(b, p, c):
                    if c == 0:
                        pe.wait_ge(probs_ready, b + 1)
                    after(pe, probs_copied, CHUNKS * b + c - 1 if not isinstance(b, int) or CHUNKS * b + c >= 1 else 0)
                    bank = probs_ps[:, (CHUNKS * p + c) % 2, :]
                    for n in range(FOUR):
                        t = FOUR * c + n
                        rows = tile_rows(t)
                        last = nc.tensor.transpose(bank[0:rows, n * SEQ:(n + 1) * SEQ],
                                                   probs[:, t * TILE:t * TILE + rows], ident[0:SEQ, 0:SEQ])
                    last.then_inc(probs_turned, 1)

                def attend(b, p):
                    pe.wait_ge(probs_copied, CHUNKS * (b + 1))
                    after(pe, summed_done, b)
                    for t in range(TILES):
                        rows = tile_rows(t)
                        last = nc.tensor.matmul(out_ps[0:SEQ, 0:DIM], probs_t[0:rows, t, :], keys[p][0:rows, t, :],
                                                start=(t == 0), stop=(t == TILES - 1))
                    last.then_inc(attended, 1)

                def step(b, p, j):
                    for u in range(TURNS):
                        turn(b, p, j, u)
                    for c in range(CHUNKS):
                        turn_probs(b - 1, 1 - p, c)
                    scores(b, p)
                    attend(b - 1, 1 - p)

                for u in range(TURNS):
                    turn(0, 0, 0, u)
                scores(0, 0)
                step(1, 1, 0)
                with pe.Fori(1, BATCH // 2) as j:
                    for p in range(2):
                        step(2 * j + p, p, j)
                for c in range(CHUNKS):
                    turn_probs(BATCH - 1, 1, c)
                attend(BATCH - 1, 1)

            @block.vector
            def _(dve):
                chain = Chain(dve, dve_chain_sem)
                FRONT_LINKS, BACK_LINKS = 2, 4

                def turn_copy(b, p, u):
                    dve.wait_ge(turned, TURNS * b + u + 1)
                    if u <= 2:
                        after(dve, scores_done, b)
                    bank = turn_bank(p, u)
                    if u == 0:
                        last = nc.vector.tensor_copy(x_t[:, :, :], bank[:, 0:KD * SEQ].rearrange("p (k s) -> p k s", k=KD))
                    else:
                        k, c = (u - 1) // CHUNKS, (u - 1) % CHUNKS
                        at, width = chunk_columns(c)
                        last = nc.vector.tensor_copy(keys_t[p][:, k, at:at + width], bank[:, 0:width])
                    last.then_inc(copied_dve, 1)

                def hide(b, p, j):
                    dve.wait_ge(mask_in[p], 16 * (j + 1))
                    after(dve, scores_done, b - 1 if not isinstance(b, int) or b >= 1 else 0)
                    flags = mask_row[p][:, :].bitcast(U8)
                    body = (TILES - 1) * TILE
                    nc.vector.tensor_scalar(
                        mask_bias[p][:, 0:body].rearrange("o (t p) -> o p t", p=TILE),
                        flags[:, 0:body].rearrange("o (p t) -> o p t", p=TILE), -HIDDEN, HIDDEN, ALU.mult, ALU.add)
                    nc.vector.tensor_scalar(mask_bias[p][:, body:CTX], flags[:, body:CTX], -HIDDEN, HIDDEN,
                                            ALU.mult, ALU.add).then_inc(mask_ready, 1)

                def maximum(b):
                    dve.wait_ge(scores_done, b + 1)
                    after(dve, probs_ready, b)
                    nc.vector.tensor_reduce(part_max[:, 0:1], score_ps[0:SEQ, 0:2, 0:FOUR * TILE], AX.XY, ALU.max)
                    chain(nc.vector.tensor_reduce(part_max[:, 1:2], score_ps[0:SEQ, 2, 0:CTX - 2 * FOUR * TILE], AX.X, ALU.max))
                    chain(nc.vector.tensor_tensor(out=row_max[:, :], in0=part_max[:, 0:1], in1=part_max[:, 1:2], op=ALU.max))
                    nc.vector.tensor_scalar(neg_max[:, :], row_max[:, :], -SCALE, None, ALU.mult).then_inc(max_ready, 1)

                def sums(b):
                    dve.wait_ge(probs_ready, b + 1)
                    nc.vector.tensor_scalar(any_key[:, :], row_max[:, :], HIDDEN / 2, None, ALU.is_gt)
                    chain(nc.vector.tensor_tensor(out=inv_sum[:, :], in0=part_sum[:, 0:1], in1=part_sum[:, 1:2], op=ALU.add))
                    chain(nc.vector.reciprocal(inv_sum[:, :], inv_sum[:, :]))
                    chain(nc.vector.tensor_tensor(out=factor[:, :], in0=inv_sum[:, :], in1=any_key[:, :], op=ALU.mult))

                def residual_norm(b, p):
                    dve.wait_ge(attended, b + 1)
                    nc.vector.scalar_tensor_tensor(out=summed[:, :], in0=out_ps[0:SEQ, 0:DIM], scalar=factor[:, 0:1],
                                                   in1=x_row[p][:, :], op0=ALU.mult, op1=ALU.add).then_inc(summed_done, 1)
                    dve.wait_ge(summed_done, b + 1)
                    nc.vector.bn_stats(stats[:, :], summed[:, :])
                    dve.drain()
                    chain(nc.vector.bn_aggr(mean_var[:, :], stats[:, :]))
                    nc.vector.tensor_scalar_add(var_eps[:, :], mean_var[:, 1:2], LN_EPS).then_inc(var_ready, 1)
                    dve.wait_ge(rstd_ready, b + 1)
                    nc.vector.tensor_scalar(x_tokens[:, b, :], summed[:, :], mean_var[:, 0:1], rstd[:, 0:1],
                                            ALU.subtract, ALU.mult).then_inc(x_new, 1)

                def step(b, p, j):
                    chain.begin(FRONT_LINKS + (b - 1) * (FRONT_LINKS + BACK_LINKS))
                    turn_copy(b, p, 0)
                    sums(b - 1)
                    for u in range(2, TURNS, 2):
                        turn_copy(b, p, u)
                    hide(b, p, j)
                    maximum(b)
                    residual_norm(b - 1, 1 - p)
                    assert chain.n == FRONT_LINKS + BACK_LINKS

                chain.begin(0)
                for u in range(0, TURNS, 2):
                    turn_copy(0, 0, u)
                hide(0, 0, 0)
                maximum(0)
                step(1, 1, 0)
                with dve.Fori(1, BATCH // 2) as j:
                    for p in range(2):
                        step(2 * j + p, p, j)
                chain.begin(FRONT_LINKS + (BATCH - 1) * (FRONT_LINKS + BACK_LINKS))
                sums(BATCH - 1)
                residual_norm(BATCH - 1, 1)
                dve.wait_ge(x_new, BATCH)


def cross_attention_pass(nc, x_in_dram, ctx, x_out_dram, ident):
    PARTS_Q = (0, 0, 0, 1, 1, 2)
    PARTS_K = (0, 1, 2, 0, 1, 0)
    STACK = len(PARTS_Q) * HD
    ROWS = STACK + 3
    SCALE = float(HD) ** -0.5
    HIDDEN_SCORE = -10000.0
    REACH = CTX - SEQ - (TILES - 1) * TILE
    FOUR_Q = FOUR * SEQ
    VALUE = HD + 1
    KEY_UNITS = KD * CHUNKS
    HH = HEADS // 2
    A_PER_SUBSTEP = (2, 1, 1) * 4 + (0, 0, 0, 0)
    LAST_ROW = BATCH - 1
    UNITS = (("key", 0, 0), ("query", 1, 1), ("key", 2, 1), ("key", 3, 2), ("key", 4, 3), ("key", 5, 4), ("key", 6, 5),
             ("hidden", 7, 0), ("query", 9, 0), ("neg_max", 14, 0))
    OPENING = KEY_UNITS + 1

    def unit_plan(last):
        kept = [x for x in UNITS if not last or x[0] in ("hidden", "neg_max") or x == ("query", 1, 1)]
        return [(kind, s, n, at) for at, (kind, s, n) in enumerate(kept)]

    parts_dram = nc.dram_tensor("key_parts", (2, KD, 3, 128, CTX), BF16, kind="Internal").ap()
    max_dram = nc.dram_tensor("max_parts", (2, 3, HEADS, SEQ), BF16, kind="Internal").ap()
    with ExitStack() as stack:
        mem = Memory(nc, stack, "cross")
        keys = [mem.sbuf(f"keys{p}", [LAST, TILES, DIM]) for p in range(2)]
        values = [mem.sbuf(f"values{p}", [LAST, TILES, HEADS, VALUE]) for p in range(2)]
        parts = mem.sbuf("parts", [128, 3, KD, CTX], BF16)
        rest = mem.sbuf("rest", [128, 2, FOUR * TILE + LAST - TILE])
        key_op = [mem.sbuf(f"key_op{p}", [ROWS, HEADS, CTX], BF16) for p in range(2)]
        query_op = [mem.sbuf(f"query_op{p}", [ROWS, HEADS, SEQ], BF16) for p in range(2)]
        x_q = mem.sbuf("x_q", [SEQ, DIM])
        x_rest = mem.sbuf("x_rest", [SEQ, DIM])
        q_parts = mem.sbuf("q_parts", [SEQ, HEADS, len(PARTS_Q), HD], BF16)
        key_max = mem.sbuf("key_max", [LAST, HEADS, SEQ])
        row_max = mem.sbuf("row_max", [SEQ, HEADS])
        neg_max = mem.sbuf("neg_max", [SEQ, HEADS])
        neg_rest = mem.sbuf("neg_rest", [HEADS, SEQ])
        neg_parts = mem.sbuf("neg_parts", [HEADS, 3, SEQ], BF16)
        hidden_arg = mem.sbuf("hidden_arg", [SEQ, HEADS])
        hidden_prob = [mem.sbuf(f"hidden_prob{p}", [SEQ, HEADS]) for p in range(2)]
        hidden_sum = [mem.sbuf(f"hidden_sum{p}", [SEQ, HEADS, VALUE]) for p in range(2)]
        probs = mem.sbuf("probs", [LAST, 2, CHUNKS, FOUR_Q])
        weighted = mem.sbuf("weighted", [SEQ, HEADS, VALUE])
        inv_sum = mem.sbuf("inv_sum", [SEQ, HEADS])
        attn = mem.sbuf("attn", [SEQ, DIM])
        x_res = mem.sbuf("x_res", [SEQ, DIM])
        stats = mem.sbuf("stats", [SEQ, 6])
        mean_var = mem.sbuf("mean_var", [SEQ, 2])
        var_eps = mem.sbuf("var_eps", [SEQ, 1])
        rstd = mem.sbuf("rstd", [SEQ, 1])
        result = mem.sbuf("result", [SEQ, DIM])
        ident_bf = mem.sbuf("ident_bf", [128, 128], BF16)
        hides = mem.sbuf("hides", [LAST, SEQ])
        hides_bf = mem.sbuf("hides_bf", [LAST, SEQ], BF16)
        floor = mem.sbuf("floor", [SEQ, 1])
        minus_half = mem.sbuf("minus_half", [SEQ, 1])
        zeros = mem.sbuf("zeros", [128, 1])

        max_ps = mem.psum("max_ps", [128, CHUNKS, BANK])
        prob_ps = mem.psum("prob_ps", [128, CHUNKS, BANK])
        turn_ps = mem.psum("turn_ps", [128, BANK])
        out_ps = mem.psum("out_ps", [128, BANK])

        keys_in = [mem.sem(f"keys_in{p}") for p in range(2)]
        stacked = [[mem.sem(f"stacked{p}{k}") for k in range(KD)] for p in range(2)]
        written = [[mem.sem(f"written{p}{k}") for k in range(KD)] for p in range(2)]
        max_out = [mem.sem(f"max_out{p}") for p in range(2)]
        max_in = [mem.sem(f"max_in{p}") for p in range(2)]
        x_q_in, x_res_in, x_out = mem.sem("x_q_in"), mem.sem("x_res_in"), mem.sem("x_out")
        consts_ready, dve_chain_sem, pool_chain_sem = mem.sem("consts_ready"), mem.sem("dve_order"), mem.sem("pool_order")
        key_turned, query_turned = mem.sem("key_turned"), mem.sem("query_turned")
        hidden_turned, neg_turned = mem.sem("hidden_turned"), mem.sem("neg_turned")
        turn_free = mem.sem("turn_free")
        hi_ready, low_ready, q_parts_ready, values_ready = (mem.sem("hi_ready"), mem.sem("low_ready"),
                                                            mem.sem("q_parts_ready"), mem.sem("values_ready"))
        max_scores, key_max_ready = mem.sem("max_scores"), mem.sem("key_max_ready")
        key_max_turned, key_max_reduced = mem.sem("key_max_turned"), mem.sem("key_max_reduced")
        neg_parts_ready, arg_ready, hidden_ready = (mem.sem("neg_parts_ready"),
                                                                   mem.sem("arg_ready"), mem.sem("hidden_ready"))
        prob_scores, probs_ready, applied = mem.sem("prob_scores"), mem.sem("probs_ready"), mem.sem("applied")
        weighed, var_ready, rstd_ready, finished = (mem.sem("weighed"), mem.sem("var_ready"), mem.sem("rstd_ready"),
                                                    mem.sem("finished"))
        CONSTS = 5

        def number(x):
            return isinstance(x, int)

        def rows_before(n, back):
            return max(n - back, 0) if number(n) else n - back

        def first_unit(b):
            return OPENING + len(UNITS) * b

        with nc.Block() as block:

            @block.sync
            def _(sp):
                def load_keys(n, p):
                    if number(n) and n >= 2:
                        sp.wait_ge(key_turned, KEY_UNITS * (n - 1))
                    after(sp, values_ready, rows_before(n, 1))
                    load_context(sp, keys[p], ctx[n], keys_in[p])

                def load_queries(n):
                    after(sp, q_parts_ready, n)
                    sp.dma_start(x_q[:, :], x_in_dram[n]).then_inc(x_q_in, 16)

                def load_residual(n):
                    after(sp, finished, n)
                    sp.dma_start(x_res[:, :], x_in_dram[n]).then_inc(x_res_in, 16)

                def write_parts(n, p, k):
                    sp.wait_ge(low_ready, KEY_UNITS * n + CHUNKS * (k + 1))
                    sp.dma_start(parts_dram[p, k].rearrange("j r c -> r j c"), parts[:, :, k, :]).then_inc(written[p][k], 16)

                def stack_keys(n, p, j, k):
                    in_dram = 16 * (j + 1)
                    if not number(n) or n >= 2:
                        used = HEADS * (n - 2) + HH * (k + 1)
                        sp.wait_ge(prob_scores, used)
                        sp.nop()
                    sp.wait_ge(written[p][k], in_dram)
                    for block_row, part in enumerate(PARTS_K):
                        sp.dma_start(key_op[p][HD * block_row:HD * (block_row + 1), HH * k:HH * (k + 1), :],
                                     parts_dram[p, k, part].rearrange("(h r) c -> r h c", r=HD)).then_inc(stacked[p][k], 16)

                def stack_max(b, p, j):
                    sp.wait_ge(neg_parts_ready, b + 1)
                    sp.dma_start(max_dram[p].rearrange("j h q -> h j q"), neg_parts[:, :, :]).then_inc(max_out[p], 16)
                    sp.wait_ge(max_out[p], 16 * (j + 1))
                    sp.dma_start(query_op[p][STACK:ROWS, :, :], max_dram[p]).then_inc(max_in[p], 16)

                def store(b):
                    sp.wait_ge(finished, b + 1)
                    sp.dma_start(x_out_dram[b], result[:, :]).then_inc(x_out, 16)

                def step(b, p, j):
                    prepare = not number(b) or b < LAST_ROW
                    if not number(b) or b >= 2:
                        store(b - 2)
                    if not number(b) or b >= 1:
                        load_residual(b - 1)
                    if prepare:
                        load_queries(b + 1)
                    if not number(b) or b + 2 <= LAST_ROW:
                        load_keys(b + 2, p)
                    if prepare:
                        write_parts(b + 1, 1 - p, 0)
                        write_parts(b + 1, 1 - p, 1)
                        stack_keys(b + 1, 1 - p, j + p, 0)
                    stack_max(b, p, j)
                    if prepare:
                        stack_keys(b + 1, 1 - p, j + p, 1)

                load_keys(0, 0)
                load_queries(0)
                load_keys(1, 1)
                for k in range(KD):
                    write_parts(0, 0, k)
                    stack_keys(0, 0, 0, k)
                step(0, 0, 0)
                step(1, 1, 0)
                with sp.Fori(1, BATCH // 2 - 1) as j:
                    step(2 * j, 0, j)
                    step(2 * j + 1, 1, j)
                step(BATCH - 2, 0, BATCH // 2 - 1)
                step(LAST_ROW, 1, BATCH // 2 - 1)
                store(LAST_ROW - 1)
                load_residual(LAST_ROW)
                store(LAST_ROW)
                sp.wait_ge(x_out, 16 * BATCH)

            @block.gpsimd
            def _(pool):
                chain = Chain(pool, pool_chain_sem)
                nc.gpsimd.memset(minus_half[:, :], -0.5).then_inc(consts_ready, 1)
                nc.gpsimd.tensor_copy(ident_bf[:, :], ident[:, :]).then_inc(consts_ready, 1)
                chain(nc.gpsimd.memset(hides[:, :], 0.0))
                chain(nc.gpsimd.affine_select(out=hides[:, :], in_=hides[:, :], compare_op=ALU.is_ge, fill=1.0, base=REACH,
                                              pattern=[[1, SEQ]], channel_multiplier=-1))
                nc.gpsimd.tensor_scalar(hides_bf[:, :], hides[:, :], NEG, None, ALU.mult).then_inc(consts_ready, 1)
                chain(nc.gpsimd.memset(floor[:, :], HIDDEN_SCORE / SCALE))
                nc.gpsimd.affine_select(out=floor[:, :], in_=floor[:, :], compare_op=ALU.is_ge, fill=NEG, base=SEQ - 2,
                                        pattern=[[0, 1]], channel_multiplier=-1).then_inc(consts_ready, 1)
                for p in range(2):
                    chain(nc.gpsimd.memset(values[p][:, :, :, HD:VALUE], 1.0))
                    chain(nc.gpsimd.memset(key_op[p][STACK:ROWS, :, :], 1.0))
                nc.gpsimd.memset(zeros[:, :], 0.0).then_inc(consts_ready, 1)
                pool.wait_ge(consts_ready, CONSTS)
                OPENING_LINKS = chain.n

                def plain(out, in_):
                    nothing = zeros[0:out.shape[0], 0:1]
                    for _ in range(len(out.shape) - 2):
                        nothing = nothing.unsqueeze(2)
                    return nc.gpsimd.tensor_tensor(out=out, in0=in_, in1=nothing.to_broadcast(list(out.shape)), op=ALU.add)

                def copy_values(b, p, j):
                    pool.wait_ge(keys_in[p], 32 * (j + 1))
                    after(pool, applied, HEADS * rows_before(b, 1))
                    plain(values[p][0:TILE, 0:TILES - 1, :, 0:HD],
                          keys[p][0:TILE, 0:TILES - 1, :].rearrange("k t (h e) -> k t h e", h=HEADS))
                    plain(values[p][:, TILES - 1, :, 0:HD],
                          keys[p][:, TILES - 1, :].rearrange("k (h e) -> k h e", h=HEADS)).then_inc(values_ready, 1)

                def low_parts(n, u, before):
                    k, c = u // CHUNKS, u % CHUNKS
                    at, width = chunk_columns(c)
                    pool.wait_ge(turn_free, before + 1)
                    chain(plain(parts[:, 1, k, at:at + width], rest[:, u % 2, 0:width]))
                    nc.gpsimd.tensor_tensor(out=parts[:, 2, k, at:at + width], in0=rest[:, u % 2, 0:width],
                                            in1=parts[:, 1, k, at:at + width], op=ALU.subtract).then_inc(low_ready, 1)

                def split_queries(n):
                    pool.wait_ge(x_q_in, 16 * (n + 1))
                    after(pool, query_turned, 2 * n)
                    xh = x_q[:, :].rearrange("q (h e) -> q h e", h=HEADS)
                    rh = x_rest[:, :].rearrange("q (h e) -> q h e", h=HEADS)
                    thrice = [SEQ, HEADS, 3, HD]
                    chain(plain(q_parts[:, :, 0:3, :], xh.unsqueeze(2).to_broadcast(thrice)))
                    chain(nc.gpsimd.tensor_tensor(out=rh, in0=xh, in1=q_parts[:, :, 0, :], op=ALU.subtract))
                    twice = [SEQ, HEADS, 2, HD]
                    chain(plain(q_parts[:, :, 3:5, :], rh.unsqueeze(2).to_broadcast(twice)))
                    nc.gpsimd.tensor_tensor(out=q_parts[:, :, 5, :], in0=rh, in1=q_parts[:, :, 3, :],
                                            op=ALU.subtract).then_inc(q_parts_ready, 1)

                def power(b):
                    pool.wait_ge(var_ready, b + 1)
                    nc.gpsimd.tensor_tensor(out=rstd[:, :], in0=var_eps[:, :], in1=minus_half[:, :],
                                            op=ALU.pow).then_inc(rstd_ready, 1)

                def step(b, p, j):
                    last = number(b) and b == LAST_ROW
                    copy_values(b, p, j)
                    if not number(b) or b >= 2:
                        power(b - 2)
                    for kind, s, n, at in unit_plan(last):
                        if kind == "key":
                            low_parts(b + 1, n, first_unit(b) + at)
                        if kind == "key" and n == 1:
                            split_queries(b + 1)

                STEP_LINKS = KEY_UNITS + 3
                chain.begin(OPENING_LINKS)
                for u in range(KEY_UNITS):
                    low_parts(0, u, u)
                split_queries(0)
                opened = chain.n + OPENING_LINKS

                def numbered(b, p, j):
                    chain.begin(opened + STEP_LINKS * b)
                    step(b, p, j)
                    assert chain.n == (0 if number(b) and b == LAST_ROW else STEP_LINKS)

                numbered(0, 0, 0)
                numbered(1, 1, 0)
                with pool.Fori(1, BATCH // 2 - 1) as j:
                    numbered(2 * j, 0, j)
                    numbered(2 * j + 1, 1, j)
                numbered(BATCH - 2, 0, BATCH // 2 - 1)
                numbered(LAST_ROW, 1, BATCH // 2 - 1)
                power(LAST_ROW - 1)
                power(LAST_ROW)

            @block.scalar
            def _(act):
                act.wait_ge(consts_ready, CONSTS)

                def hi_part(n, p, j, u):
                    k, c = u // CHUNKS, u % CHUNKS
                    at, width = chunk_columns(c)
                    act.wait_ge(key_turned, KEY_UNITS * n + u + 1)
                    if c == 0:
                        after(act, written[1 - p][k], 16 * (j + p))
                    nc.scalar.activation(parts[:, 0, k, at:at + width], turn_ps[:, 0:width], ACT.Copy).then_inc(hi_ready, 1)

                def hidden_values(b, p):
                    act.wait_ge(hidden_turned, b + 1)
                    after(act, weighed, rows_before(b, 1))
                    nc.scalar.activation(hidden_sum[p][:, :, :],
                                         turn_ps[0:SEQ, 0:HEADS * VALUE].rearrange("q (h e) -> q h e", h=HEADS),
                                         ACT.Copy).then_inc(turn_free, 1)

                def hidden_probability(b, p):
                    act.wait_ge(arg_ready, b + 1)
                    nc.scalar.activation(hidden_prob[p][:, :], hidden_arg[:, :], ACT.Exp).then_inc(hidden_ready, 1)

                def exponentials(r, h):
                    act.wait_ge(prob_scores, HEADS * r + h + 1)
                    if h >= 2:
                        act.wait_ge(applied, HEADS * r + h - 1)
                    else:
                        after(act, applied, HEADS * r + h - 1 if not number(r) or r >= 1 else 0)
                    nc.scalar.activation(probs[:, h % 2, :, :], prob_ps[0:LAST, :, 0:FOUR_Q], ACT.Exp,
                                         scale=SCALE).then_inc(probs_ready, 1)

                def step(b, p, j):
                    plan = {s: (kind, n) for kind, s, n, _ in unit_plan(number(b) and b == LAST_ROW)}
                    for s in range(HEADS):
                        if not number(b) or b >= 1:
                            exponentials(b - 1, s)
                        kind, n = plan.get(s, (None, 0))
                        if kind == "key":
                            hi_part(b + 1, 1 - p, j + p, n)
                        if kind == "hidden":
                            hidden_values(b, p)
                        if s == 14:
                            hidden_probability(b, p)

                for u in range(KEY_UNITS):
                    hi_part(0, 0, 0, u)
                step(0, 0, 0)
                step(1, 1, 0)
                with act.Fori(1, BATCH // 2 - 1) as j:
                    step(2 * j, 0, j)
                    step(2 * j + 1, 1, j)
                step(BATCH - 2, 0, BATCH // 2 - 1)
                step(LAST_ROW, 1, BATCH // 2 - 1)
                for h in range(HEADS):
                    exponentials(LAST_ROW, h)

            @block.tensor
            def _(pe):
                pe.wait_ge(consts_ready, CONSTS)

                def turn_keys(n, p, j, u, before):
                    k, c = u // CHUNKS, u % CHUNKS
                    if u == 0:
                        pe.wait_ge(keys_in[p], 32 * (j + 1))
                    after(pe, turn_free, before)
                    for i in range(FOUR):
                        t = FOUR * c + i
                        rows = tile_rows(t)
                        last = nc.tensor.transpose(turn_ps[:, i * TILE:i * TILE + rows],
                                                   keys[p][0:rows, t, k * 128:(k + 1) * 128], ident[0:rows, 0:rows])
                    last.then_inc(key_turned, 1)

                def turn_queries(n, half, before):
                    pe.wait_ge(q_parts_ready, n + 1)
                    pe.wait_ge(turn_free, before)
                    bank = turn_ps[:, :].bitcast(BF16)
                    for i in range(HH):
                        last = nc.tensor.transpose(bank[0:STACK, i * SEQ:(i + 1) * SEQ],
                                                   q_parts[:, HH * half + i, :, :].rearrange("q c e -> q (c e)"),
                                                   ident_bf[0:SEQ, 0:SEQ])
                    last.then_inc(query_turned, 1)

                def sum_hidden(b, p, before):
                    pe.wait_ge(values_ready, b + 1)
                    pe.wait_ge(turn_free, before)
                    nc.tensor.matmul(turn_ps[0:SEQ, 0:HEADS * VALUE], hides[:, :],
                                     values[p][:, TILES - 1, :, :].rearrange("k h e -> k (h e)"),
                                     start=True, stop=True).then_inc(hidden_turned, 1)

                def turn_neg_max(b, before):
                    pe.wait_ge(arg_ready, b + 1)
                    pe.wait_ge(turn_free, before)
                    nc.tensor.transpose(turn_ps[0:HEADS, 0:SEQ], neg_max[:, :], ident[0:SEQ, 0:SEQ]).then_inc(neg_turned, 1)

                def head_scores(ps, p, h, rows):
                    for t in range(TILES):
                        target = ps[0:LAST, t // FOUR, (t % FOUR) * SEQ:(t % FOUR + 1) * SEQ]
                        if t == TILES - 1:
                            nc.tensor.matmul(target, ident_bf[0:LAST, 0:LAST], hides_bf[:, :], start=True, stop=False)
                        last = nc.tensor.matmul(target, key_op[p][0:rows, h, t * TILE:t * TILE + LAST],
                                                query_op[p][0:rows, h, :], start=(t < TILES - 1), stop=True)
                    return last

                def scores_for_max(b, p, j, h):
                    if h % HH == 0:
                        pe.wait_ge(stacked[p][h // HH], 16 * len(PARTS_K) * (j + 1))
                        if h == 0:
                            pe.wait_ge(turn_free, OPENING if number(b) and b == 0 else first_unit(b) - 1)
                        else:
                            pe.wait_ge(turn_free, first_unit(b) + (1 if number(b) and b == LAST_ROW else 2))
                    if h == 0:
                        after(pe, key_max_reduced, 2 * b)
                    else:
                        pe.wait_ge(key_max_ready, HEADS * b + h)
                    head_scores(max_ps, p, h, STACK).then_inc(max_scores, 1)

                def turn_key_max(b, half):
                    pe.wait_ge(key_max_ready, HEADS * (b + 1))
                    if half:
                        pe.wait_ge(key_max_reduced, 2 * b + 1)
                    for i in range(12 if half == 0 else 4):
                        last = nc.tensor.transpose(max_ps[0:SEQ, i // 4, (i % 4) * LAST:(i % 4 + 1) * LAST],
                                                   key_max[:, 12 * half + i, :], ident[0:LAST, 0:LAST])
                    last.then_inc(key_max_turned, 1)

                def scores_for_probs(r, p, j, h):
                    if h == 0:
                        pe.wait_ge(max_in[p], 16 * (j + 1))
                    after(pe, probs_ready, HEADS * r + h)
                    head_scores(prob_ps, p, h, ROWS).then_inc(prob_scores, 1)

                def apply(r, p, h):
                    pe.wait_ge(probs_ready, HEADS * r + h + 1)
                    if h == 0:
                        after(pe, weighed, r)
                    for t in range(TILES):
                        rows = tile_rows(t)
                        last = nc.tensor.matmul(out_ps[0:SEQ, VALUE * h:VALUE * (h + 1)],
                                                probs[0:rows, h % 2, t // FOUR, (t % FOUR) * SEQ:(t % FOUR + 1) * SEQ],
                                                values[p][0:rows, t, h, :], start=(t == 0), stop=(t == TILES - 1))
                    last.then_inc(applied, 1)

                def step(b, p, j):
                    plan = {s: (kind, n, at) for kind, s, n, at in unit_plan(number(b) and b == LAST_ROW)}
                    going = not number(b) or b >= 1
                    a = 0
                    for s in range(HEADS):
                        if going:
                            scores_for_probs(b - 1, 1 - p, j - 1 + p, s)
                        for _ in range(A_PER_SUBSTEP[s]):
                            scores_for_max(b, p, j, a)
                            a += 1
                        if s in (12, 13):
                            turn_key_max(b, s - 12)
                        kind, n, at = plan.get(s, (None, 0, 0))
                        before = first_unit(b) + at
                        if kind == "key":
                            turn_keys(b + 1, 1 - p, j + p, n, before)
                        if kind == "query":
                            turn_queries(b if n == 1 else b + 1, n, before)
                        if kind == "hidden":
                            sum_hidden(b, p, before)
                        if kind == "neg_max":
                            turn_neg_max(b, before)
                        if going and s:
                            apply(b - 1, 1 - p, s - 1)
                    if going:
                        apply(b - 1, 1 - p, HEADS - 1)

                for u in range(KEY_UNITS):
                    turn_keys(0, 0, 0, u, u)
                turn_queries(0, 0, KEY_UNITS)
                step(0, 0, 0)
                step(1, 1, 0)
                with pe.Fori(1, BATCH // 2 - 1) as j:
                    step(2 * j, 0, j)
                    step(2 * j + 1, 1, j)
                step(BATCH - 2, 0, BATCH // 2 - 1)
                step(LAST_ROW, 1, BATCH // 2 - 1)
                for h in range(HEADS):
                    scores_for_probs(LAST_ROW, 1, BATCH // 2 - 1, h)
                    if h:
                        apply(LAST_ROW, 1, h - 1)
                apply(LAST_ROW, 1, HEADS - 1)

            @block.vector
            def _(dve):
                chain = Chain(dve, dve_chain_sem)
                dve.wait_ge(consts_ready, CONSTS)

                def key_rest(n, u, before):
                    width = chunk_columns(u % CHUNKS)[1]
                    dve.wait_ge(hi_ready, KEY_UNITS * n + u + 1)
                    if u >= 2:
                        dve.wait_ge(low_ready, KEY_UNITS * n + u - 1)
                    else:
                        after(dve, low_ready, KEY_UNITS * n + u - 1 if not number(n) or n >= 1 else 0)
                    k, c = u // CHUNKS, u % CHUNKS
                    at = chunk_columns(c)[0]
                    nc.vector.tensor_tensor(out=rest[:, u % 2, 0:width], in0=turn_ps[:, 0:width],
                                            in1=parts[:, 0, k, at:at + width], op=ALU.subtract).then_inc(turn_free, 1)

                def query_copy(n, p, half):
                    dve.wait_ge(query_turned, 2 * n + half + 1)
                    if not number(n) or n >= 2:
                        dve.wait_ge(prob_scores, HEADS * (n - 2) + HH * (half + 1))
                    nc.vector.tensor_copy(query_op[p][0:STACK, HH * half:HH * (half + 1), :],
                                          turn_ps[:, :].bitcast(BF16)[0:STACK, 0:HH * SEQ]
                                          .rearrange("r (h q) -> r h q", h=HH)).then_inc(turn_free, 1)

                def head_max(b, h):
                    dve.wait_ge(max_scores, HEADS * b + h + 1)
                    if h == 0:
                        after(dve, key_max_turned, 2 * b)
                    nc.vector.tensor_reduce(key_max[:, h, :],
                                            max_ps[0:LAST, :, 0:FOUR_Q].rearrange("k c (t q) -> k q c t", t=FOUR),
                                            AX.XY, ALU.max).then_inc(key_max_ready, 1)

                def reduce_keys(b, half):
                    dve.wait_ge(key_max_turned, 2 * b + half + 1)
                    heads = 12 if half == 0 else 4
                    view = max_ps[0:SEQ, 0:heads // 4, 0:4 * LAST].rearrange("q c (h k) -> q c h k", h=4)
                    nc.vector.tensor_reduce(row_max[:, 12 * half:12 * half + heads].rearrange("q (c h) -> q c h", h=4), view,
                                            AX.X, ALU.max).then_inc(key_max_reduced, 1)

                def negate_max(b):
                    dve.wait_ge(key_max_reduced, 2 * (b + 1))
                    after(dve, hidden_ready, b)
                    chain(nc.vector.tensor_scalar(neg_max[:, :], row_max[:, :], floor[:, 0:1], -1.0, ALU.max, ALU.mult))
                    chain(nc.vector.tensor_scalar(hidden_arg[:, :], neg_max[:, :], SCALE, HIDDEN_SCORE, ALU.mult, ALU.add))
                    nc.vector.tensor_scalar(hidden_arg[:, :], hidden_arg[:, :], 0.0, None, ALU.min).then_inc(arg_ready, 1)

                def split_neg_max(b, p, j):
                    dve.wait_ge(neg_turned, b + 1)
                    after(dve, max_in[1 - p], 16 * (j + p))
                    bank = turn_ps[0:HEADS, 0:SEQ]
                    chain(nc.vector.tensor_copy(neg_parts[:, 0, :], bank))
                    nc.vector.tensor_tensor(out=neg_rest[:, :], in0=bank, in1=neg_parts[:, 0, :],
                                            op=ALU.subtract).then_inc(turn_free, 1)
                    dve.wait_ge(turn_free, first_unit(b) + (3 if number(b) and b == LAST_ROW else len(UNITS)))
                    chain(nc.vector.tensor_copy(neg_parts[:, 1, :], neg_rest[:, :]))
                    nc.vector.tensor_tensor(out=neg_parts[:, 2, :], in0=neg_rest[:, :], in1=neg_parts[:, 1, :],
                                            op=ALU.subtract).then_inc(neg_parts_ready, 1)

                def finish(r, p):
                    dve.wait_ge(hidden_ready, r + 1)
                    dve.wait_ge(applied, HEADS * (r + 1))
                    three = [SEQ, HEADS, VALUE]
                    chain(nc.vector.tensor_tensor(out=weighted[:, :, :], in0=hidden_sum[p][:, :, :],
                                                  in1=hidden_prob[p][:, :].unsqueeze(2).to_broadcast(three), op=ALU.mult))
                    nc.vector.tensor_tensor(out=weighted[:, :, :], in0=weighted[:, :, :],
                                            in1=out_ps[0:SEQ, 0:HEADS * VALUE].rearrange("q (h e) -> q h e", h=HEADS),
                                            op=ALU.add).then_inc(weighed, 1)
                    dve.wait_ge(weighed, r + 1)
                    chain(nc.vector.reciprocal(inv_sum[:, :].unsqueeze(2), weighted[:, :, HD:VALUE]))
                    chain(nc.vector.tensor_tensor(out=attn[:, :].rearrange("q (h e) -> q h e", h=HEADS),
                                                  in0=weighted[:, :, 0:HD],
                                                  in1=inv_sum[:, :].unsqueeze(2).to_broadcast([SEQ, HEADS, HD]), op=ALU.mult))
                    dve.wait_ge(x_res_in, 16 * (r + 1))
                    chain(nc.vector.tensor_tensor(out=attn[:, :], in0=attn[:, :], in1=x_res[:, :], op=ALU.add))
                    nc.vector.bn_stats(stats[:, :], attn[:, :])
                    dve.drain()
                    chain(nc.vector.bn_aggr(mean_var[:, :], stats[:, :]))
                    nc.vector.tensor_scalar_add(var_eps[:, :], mean_var[:, 1:2], LN_EPS).then_inc(var_ready, 1)
                    dve.wait_ge(rstd_ready, r + 1)
                    after(dve, x_out, 16 * r)
                    nc.vector.tensor_scalar(result[:, :], attn[:, :], mean_var[:, 0:1], rstd[:, 0:1],
                                            ALU.subtract, ALU.mult).then_inc(finished, 1)

                FRONT_LINKS, BACK_LINKS = 4, 5

                def step(b, p, j):
                    last_row = number(b) and b == LAST_ROW
                    if number(b) and b <= 2:
                        chain.begin(FRONT_LINKS * b)
                    else:
                        chain.begin(FRONT_LINKS * b + BACK_LINKS * (b - 2))
                    plan = {s: (kind, n, at) for kind, s, n, at in unit_plan(last_row)}
                    a = 0
                    for s in range(HEADS):
                        for _ in range(A_PER_SUBSTEP[s]):
                            head_max(b, a)
                            a += 1
                        if s == 0 and (not number(b) or b >= 2):
                            finish(b - 2, p)
                        if s in (12, 13):
                            reduce_keys(b, s - 12)
                        if s == 13:
                            negate_max(b)
                        kind, n, at = plan.get(s, (None, 0, 0))
                        if kind == "key":
                            key_rest(b + 1, n, first_unit(b) + at)
                        if kind == "query":
                            query_copy(b if n == 1 else b + 1, p if n == 1 else 1 - p, n)
                        if kind == "neg_max":
                            split_neg_max(b, p, j)
                    assert chain.n == FRONT_LINKS + (0 if number(b) and b < 2 else BACK_LINKS)

                for u in range(KEY_UNITS):
                    key_rest(0, u, u)
                query_copy(0, 0, 0)
                step(0, 0, 0)
                step(1, 1, 0)
                with dve.Fori(1, BATCH // 2 - 1) as j:
                    step(2 * j, 0, j)
                    step(2 * j + 1, 1, j)
                step(BATCH - 2, 0, BATCH // 2 - 1)
                step(LAST_ROW, 1, BATCH // 2 - 1)
                chain.begin(FRONT_LINKS * BATCH + BACK_LINKS * (BATCH - 2))
                finish(LAST_ROW - 1, 0)
                finish(LAST_ROW, 1)


def build(nc, ap, out):
    before_cross = nc.dram_tensor("before_cross", (BATCH, SEQ, DIM), F32, kind="Internal").ap()
    after_cross = nc.dram_tensor("after_cross", (BATCH, SEQ, DIM), F32, kind="Internal").ap()
    with ExitStack() as outer:
        mem = Memory(nc, outer, "shared")
        ident = mem.sbuf("ident", [128, 128])
        minus_half = mem.sbuf("minus_half", [128, 1])
        constants_pass(nc, ident, minus_half)
        with ExitStack() as inner:
            x_tokens = Memory(nc, inner, "layer0").sbuf("x_tokens", [SEQ, BATCH, DIM])
            self_attention_pass(nc, "attn0", x_tokens, ap["x"], ident, minus_half, ap["L0_attn_Wq"], ap["L0_attn_bq"],
                                ap["L0_attn_Wk"], ap["L0_attn_bk"], ap["L0_attn_Wv"], ap["L0_attn_bv"], ap["L0_attn_Wo"],
                                ap["L0_attn_bo"], ap["L0_attn_ln_g"], ap["L0_attn_ln_b"])
            memory_attention_pass(nc, x_tokens, ap["ctx_2048"], ap["mask_BxS2_bk0"], ident, minus_half)
            experts_pass(nc, x_tokens, ident, minus_half, ap["L0_ffn_Wg"], ap["L0_ffn_Wu"], ap["L0_ffn_Wd"],
                         ap["L0_ffn_Wr"], ap["L0_ffn_temperature"])
            self_attention_pass(nc, "attn1", x_tokens, None, ident, minus_half, ap["L1_attn_wq"], ap["L1_attn_bq"],
                                ap["L1_attn_wk"], ap["L1_attn_bk"], ap["L1_attn_wv"], ap["L1_attn_bv"], ap["L1_attn_wp"],
                                ap["L1_attn_bp"], None, None)
            store_pass(nc, "spill", x_tokens, before_cross)
        cross_attention_pass(nc, before_cross, ap["ctx_2048"], after_cross, ident)
        with ExitStack() as inner:
            x_tokens = Memory(nc, inner, "layer1").sbuf("x_tokens", [SEQ, BATCH, DIM])
            load_pass(nc, "reload", x_tokens, after_cross)
            quantized_ffn_pass(nc, x_tokens, ident, minus_half, ap["L1_ffn_w_gate"], ap["L1_ffn_w_up"],
                               ap["L1_ffn_w_down"], ap["L1_ffn_s_gate"], ap["L1_ffn_s_up"], ap["L1_ffn_s_down"])
            store_pass(nc, "result", x_tokens, out)


def kernel(**inputs):
    import numpy as np
    import concourse.bacc as bacc
    from concourse.bass_utils import run_bass_kernel_spmd as run
    nc=bacc.Bacc("TRN2", target_bir_lowering=False, num_devices=1)
    arrays={}; ap={}
    for name,a in inputs.items():
        a=np.ascontiguousarray(a)
        if a.dtype.itemsize==1: a=a.view(np.int32)
        arrays["in_"+name]=a
        ap[name]=nc.dram_tensor("in_"+name,a.shape,mybir.dt.from_np(a.dtype),kind="ExternalInput").ap()
    out=nc.dram_tensor("out",(BATCH,SEQ,DIM),F32,kind="ExternalOutput").ap()
    build(nc,ap,out)
    r=run(nc,[arrays],core_ids=[0])
    return r.results[0]["out"]
```

```python
import concourse.bass as bass
from concourse import mybir
from contextlib import ExitStack

F32 = mybir.dt.float32
BF16 = mybir.dt.bfloat16
U8 = mybir.dt.uint8
I8 = mybir.dt.int8
ALU = mybir.AluOpType
ACT = mybir.ActivationFunctionType
AX = mybir.AxisListType

BATCH, SEQ, DIM, HEADS = 32, 100, 256, 16
HD = DIM // HEADS
KD = DIM // 128
HPB = 128 // HD
CTX = 1444
EXPERTS, EXPERT_F = 8, 256
INTER = 1024
LN_EPS = 1e-5
NEG = -1e30
BANK = 512
GROUP = 4


class Memory:

    def __init__(self, nc, stack, prefix):
        self.nc, self.stack, self.prefix, self.sems = nc, stack, prefix, []
        stack.callback(self.release)

    def sbuf(self, name, shape, dt=F32):
        return self.stack.enter_context(self.nc.sbuf_tensor(f"{self.prefix}_{name}", shape, dt))

    def psum(self, name, shape, dt=F32):
        return self.stack.enter_context(self.nc.psum_tensor(f"{self.prefix}_{name}", shape, dt))

    def sem(self, name):
        sem = self.nc.alloc_semaphore(f"{self.prefix}_{name}")
        self.sems.append(sem)
        return sem

    def release(self):
        if self.sems:
            self.nc.clear_and_free_semaphores(self.sems)
            self.nc.all_engine_barrier()


def after(engine, sem, count):
    if not isinstance(count, int) or count > 0:
        engine.wait_ge(sem, count)


class Chain:

    def __init__(self, engine, sem):
        self.engine, self.sem, self.origin, self.n = engine, sem, 0, 0

    def begin(self, origin):
        self.origin, self.n = origin, 0

    def __call__(self, instruction):
        self.n += 1
        instruction.then_inc(self.sem, 1)
        self.engine.wait_ge(self.sem, self.origin + self.n)


def self_attention_pass(nc, prefix, x_tokens, x_dram, ident, minus_half, wq, bq, wk, bk, wv, bv, wo, bo, ln_g, ln_b):
    pre_norm = ln_g is not None
    with ExitStack() as stack:
        mem = Memory(nc, stack, prefix)
        w_sb = {n: mem.sbuf(n, [128, KD, DIM]) for n in ("wq", "wk", "wv", "wo")}
        bias_q = mem.sbuf("bias_q", [128, KD])
        bias_k = mem.sbuf("bias_k", [128, KD])
        bias_v = mem.sbuf("bias_v", [SEQ, DIM])
        bias_o = mem.sbuf("bias_o", [SEQ, DIM])
        gain = mem.sbuf("gain", [128, KD]) if pre_norm else None
        shift = mem.sbuf("shift", [128, KD]) if pre_norm else None
        head_rows = mem.sbuf("head_rows", [128, HPB])
        causal = mem.sbuf("causal", [SEQ, 4 * SEQ], BF16)
        ident_bf = mem.sbuf("ident_bf", [128, 128], BF16)
        normed = mem.sbuf("normed", [SEQ, DIM])
        x_t = mem.sbuf("x_t", [128, KD, SEQ])
        q_t = mem.sbuf("q_t", [128, KD, SEQ])
        k_heads = mem.sbuf("k_heads", [128, KD, HPB, SEQ])
        v_ones = mem.sbuf("v_ones", [SEQ, HEADS, HD + 1])
        v_raw = mem.sbuf("v_raw", [SEQ, DIM])
        row_max = mem.sbuf("row_max", [SEQ, HEADS])
        probs = mem.sbuf("probs", [SEQ, HEADS, SEQ])
        probs_t = mem.sbuf("probs_t", [SEQ, HEADS, SEQ])
        inv_sum = mem.sbuf("inv_sum", [SEQ, HEADS])
        mixed = mem.sbuf("mixed", [SEQ, DIM])
        mixed_t = mem.sbuf("mixed_t", [128, KD, SEQ])
        x_bias = mem.sbuf("x_bias", [SEQ, DIM])
        summed = mem.sbuf("summed", [SEQ, DIM])
        stats = mem.sbuf("stats", [SEQ, 6])
        mean_var = mem.sbuf("mean_var", [SEQ, 2])
        var_eps = mem.sbuf("var_eps", [SEQ, 1])
        rstd = mem.sbuf("rstd", [SEQ, 1])
        stats0 = mem.sbuf("stats0", [SEQ, 6])
        mean_var0 = mem.sbuf("mean_var0", [SEQ, 2])
        var_eps0 = mem.sbuf("var_eps0", [SEQ, 1])
        rstd0 = mem.sbuf("rstd0", [SEQ, 1])

        score_ps = mem.psum("score_ps", [128, 4, BANK])
        turn_ps = mem.psum("turn_ps", [128, 2, BANK])
        misc_ps = mem.psum("misc_ps", [128, BANK])
        out_ps = mem.psum("out_ps", [128, BANK])

        weights_in = mem.sem("weights_in")
        x_in = mem.sem("x_in")
        const_ready = mem.sem("const_ready")
        pool_chain_sem = mem.sem("pool_order")
        dve_chain_sem = mem.sem("dve_order")
        normed_ready, var0_ready, rstd0_ready = mem.sem("normed_ready"), mem.sem("var0_ready"), mem.sem("rstd0_ready")
        xt_done, xt_ready = mem.sem("xt_done"), mem.sem("xt_ready")
        qk_done, v_done = mem.sem("qk_done"), mem.sem("v_done")
        q_ready, k_ready, v_ready = mem.sem("q_ready"), mem.sem("k_ready"), mem.sem("v_ready")
        v_copied = mem.sem("v_copied")
        scores_done, shifted = mem.sem("scores_done"), mem.sem("shifted")
        probs_ready = mem.sem("probs_ready")
        turned, turned_copied = mem.sem("turned"), mem.sem("turned_copied")
        attended, mixed_ready = mem.sem("attended"), mem.sem("mixed_ready")
        mixed_turned, mixed_t_ready = mem.sem("mixed_turned"), mem.sem("mixed_t_ready")
        projected, x_bias_ready = mem.sem("projected"), mem.sem("x_bias_ready")
        summed_done, var_ready, rstd_ready, x_new = (mem.sem("summed_done"), mem.sem("var_ready"),
                                                     mem.sem("rstd_ready"), mem.sem("x_new"))
        WEIGHTS = 16 * (8 + (2 if pre_norm else 0))
        CONSTS = 4
        TURNS = 2
        HT = HEADS // TURNS

        with nc.Block() as block:

            @block.sync
            def _(sp):
                if x_dram is not None:
                    for r in range(0, BATCH, 4):
                        sp.dma_start(x_tokens[:, r:r + 4, :],
                                     x_dram[r:r + 4].rearrange("b s d -> s b d")).then_inc(x_in, 16)
                for name, w in (("wq", wq), ("wk", wk), ("wv", wv), ("wo", wo)):
                    sp.dma_start(w_sb[name][:, :, :], w.rearrange("(k p) n -> p k n", p=128)).then_inc(weights_in, 16)
                with nc.allow_non_contiguous_dma(reason="256 bias values, once"):
                    sp.dma_start(bias_q[:, :], bq.rearrange("(k p) -> p k", p=128)).then_inc(weights_in, 16)
                    sp.dma_start(bias_k[:, :], bk.rearrange("(k p) -> p k", p=128)).then_inc(weights_in, 16)
                    if pre_norm:
                        sp.dma_start(gain[:, :], ln_g.rearrange("(k p) -> p k", p=128)).then_inc(weights_in, 16)
                        sp.dma_start(shift[:, :], ln_b.rearrange("(k p) -> p k", p=128)).then_inc(weights_in, 16)
                sp.dma_start(bias_v[:, :], bv.partition_broadcast(SEQ)).then_inc(weights_in, 16)
                sp.dma_start(bias_o[:, :], bo.partition_broadcast(SEQ)).then_inc(weights_in, 16)
                sp.wait_ge(weights_in, WEIGHTS)

            @block.gpsimd
            def _(pool):
                chain = Chain(pool, pool_chain_sem)
                chain(nc.gpsimd.memset(head_rows[:, :], 1.0))
                chain(nc.gpsimd.affine_select(out=head_rows[:, :], in_=head_rows[:, :], compare_op=ALU.is_ge, fill=0.0,
                                              base=0, pattern=[[-HD, HPB]], channel_multiplier=1))
                nc.gpsimd.affine_select(out=head_rows[:, :], in_=head_rows[:, :], compare_op=ALU.is_ge, fill=0.0,
                                        base=HD - 1, pattern=[[HD, HPB]], channel_multiplier=-1).then_inc(const_ready, 1)
                chain(nc.gpsimd.memset(causal[:, :], 0.0))
                cv = causal[:, :].rearrange("q (h k) -> q h k", h=4)
                nc.gpsimd.affine_select(out=cv, in_=cv, compare_op=ALU.is_ge, fill=NEG, base=0,
                                        pattern=[[0, 4], [-1, SEQ]], channel_multiplier=1).then_inc(const_ready, 1)
                nc.gpsimd.tensor_copy(ident_bf[:, :], ident[:, :]).then_inc(const_ready, 1)
                nc.gpsimd.memset(v_ones[:, :, HD:HD + 1], 1.0).then_inc(const_ready, 1)
                pool.wait_ge(weights_in, WEIGHTS)
                if x_dram is not None:
                    pool.wait_ge(x_in, 16 * (BATCH // 4))

                def norm_power(i):
                    if pre_norm:
                        pool.wait_ge(var0_ready, i + 1)
                        nc.gpsimd.tensor_tensor(out=rstd0[:, :], in0=var_eps0[:, :], in1=minus_half[0:SEQ, :],
                                                op=ALU.pow).then_inc(rstd0_ready, 1)

                def residual_bias(i):
                    after(pool, summed_done, i)
                    nc.gpsimd.tensor_tensor(out=x_bias[:, :], in0=x_tokens[:, i, :], in1=bias_o[:, :],
                                            op=ALU.add).then_inc(x_bias_ready, 1)

                def final_power(i):
                    pool.wait_ge(var_ready, i + 1)
                    nc.gpsimd.tensor_tensor(out=rstd[:, :], in0=var_eps[:, :], in1=minus_half[0:SEQ, :],
                                            op=ALU.pow).then_inc(rstd_ready, 1)

                def values(i):
                    pool.wait_ge(v_copied, i + 1)
                    after(pool, attended, i)
                    nc.gpsimd.tensor_tensor(out=v_ones[:, :, 0:HD], in0=v_raw[:, :].rearrange("s (h e) -> s h e", h=HEADS),
                                            in1=bias_v[:, :].rearrange("s (h e) -> s h e", h=HEADS),
                                            op=ALU.add).then_inc(v_ready, 1)

                def step(i, back=True, ahead=True):
                    if back:
                        residual_bias(i - 2)
                    if ahead:
                        norm_power(i + 1)
                    if back:
                        final_power(i - 2)
                    values(i)

                norm_power(0)
                step(0, back=False)
                step(1, back=False)
                with pool.Fori(2, BATCH - 1) as i:
                    step(i)
                step(BATCH - 1, ahead=False)
                for i in (BATCH - 2, BATCH - 1):
                    residual_bias(i)
                    final_power(i)

            @block.scalar
            def _(act):
                act.wait_ge(weights_in, WEIGHTS)

                def queries(i):
                    act.wait_ge(qk_done, i + 1)
                    after(act, scores_done, i)
                    for k in range(KD):
                        last = nc.scalar.activation(q_t[:, k, :], turn_ps[:, 0, k * SEQ:(k + 1) * SEQ],
                                                    ACT.Identity, bias=bias_q[:, k:k + 1])
                    last.then_inc(q_ready, 1)

                def exponentials(i):
                    act.wait_ge(shifted, i + 1)
                    nc.scalar.activation(probs[:, :, :], probs[:, :, :], ACT.Exp,
                                         scale=float(HD) ** -0.5).then_inc(probs_ready, 1)

                def turned_copy(i, t):
                    act.wait_ge(turned, TURNS * i + t + 1)
                    if t == 0:
                        after(act, attended, i)
                    nc.scalar.activation(
                        probs_t[:, HT * t:HT * (t + 1), :].rearrange("k (b h) q -> k b (h q)", b=2),
                        turn_ps[0:SEQ, :, 0:4 * SEQ], ACT.Copy).then_inc(turned_copied, 1)

                def values_copy(i):
                    act.wait_ge(v_done, i + 1)
                    after(act, v_ready, i)
                    nc.scalar.activation(v_raw[:, :], turn_ps[0:SEQ, 1, 0:DIM], ACT.Copy).then_inc(v_copied, 1)

                def step(i):
                    queries(i)
                    values_copy(i)
                    turned_copy(i - 1, 0)
                    turned_copy(i - 1, 1)
                    exponentials(i)

                queries(0)
                values_copy(0)
                exponentials(0)
                step(1)
                with act.Fori(2, BATCH) as i:
                    step(i)
                turned_copy(BATCH - 1, 0)
                turned_copy(BATCH - 1, 1)

            @block.tensor
            def _(pe):
                pe.wait_ge(weights_in, WEIGHTS)
                pe.wait_ge(const_ready, CONSTS)

                def turn_x(i):
                    pe.wait_ge(normed_ready, i + 1)
                    for k in range(KD):
                        last = nc.tensor.transpose(misc_ps[:, k * SEQ:(k + 1) * SEQ],
                                                   normed[:, k * 128:(k + 1) * 128], ident[0:SEQ, 0:SEQ])
                    last.then_inc(xt_done, 1)

                def project(i):
                    pe.wait_ge(xt_ready, i + 1)
                    after(pe, turned_copied, TURNS * (i - 1) if not isinstance(i, int) or i >= 1 else 0)
                    after(pe, v_copied, i)
                    for n, name in enumerate(("wq", "wk")):
                        for m in range(KD):
                            for k in range(KD):
                                last = nc.tensor.matmul(turn_ps[:, 0, (n * KD + m) * SEQ:(n * KD + m + 1) * SEQ],
                                                        w_sb[name][:, k, m * 128:(m + 1) * 128], x_t[:, k, :],
                                                        start=(k == 0), stop=(k == KD - 1))
                    last.then_inc(qk_done, 1)
                    for k in range(KD):
                        last = nc.tensor.matmul(turn_ps[0:SEQ, 1, 0:DIM], x_t[:, k, :], w_sb["wv"][:, k, :],
                                                start=(k == 0), stop=(k == KD - 1))
                    last.then_inc(v_done, 1)

                def scores(i):
                    pe.wait_ge(q_ready, i + 1)
                    pe.wait_ge(k_ready, i + 1)
                    after(pe, shifted, i)
                    for b in range(4):
                        k, half = b // 2, b % 2
                        nc.tensor.matmul(score_ps[0:SEQ, b, 0:4 * SEQ], q_t[:, k, :],
                                         k_heads[:, k, 4 * half:4 * half + 4, :], start=True, stop=False)
                        last = nc.tensor.matmul(score_ps[0:SEQ, b, 0:4 * SEQ], ident_bf[0:SEQ, 0:SEQ], causal[:, :],
                                                start=False, stop=True)
                    last.then_inc(scores_done, 1)

                def turn_probs(i, t):
                    if t == 0:
                        pe.wait_ge(probs_ready, i + 1)
                        pe.wait_ge(v_copied, BATCH if isinstance(i, int) and i == BATCH - 1 else i + 2)
                    else:
                        pe.wait_ge(turned_copied, TURNS * i + t)
                    for h in range(HT):
                        last = nc.tensor.transpose(turn_ps[0:SEQ, h // 4, (h % 4) * SEQ:(h % 4 + 1) * SEQ],
                                                   probs[:, HT * t + h, :], ident[0:SEQ, 0:SEQ])
                    last.then_inc(turned, 1)

                def attend(i):
                    pe.wait_ge(turned_copied, TURNS * (i + 1))
                    pe.wait_ge(v_ready, i + 1)
                    after(pe, summed_done, i)
                    for h in range(HEADS):
                        last = nc.tensor.matmul(out_ps[0:SEQ, (HD + 1) * h:(HD + 1) * (h + 1)], probs_t[:, h, :],
                                                v_ones[:, h, :], start=True, stop=True)
                    last.then_inc(attended, 1)

                def turn_mixed(i):
                    pe.wait_ge(mixed_ready, i + 1)
                    for k in range(KD):
                        last = nc.tensor.transpose(misc_ps[:, (KD + k) * SEQ:(KD + k + 1) * SEQ],
                                                   mixed[:, k * 128:(k + 1) * 128], ident[0:SEQ, 0:SEQ])
                    last.then_inc(mixed_turned, 1)

                def project_out(i):
                    pe.wait_ge(mixed_t_ready, i + 1)
                    for k in range(KD):
                        last = nc.tensor.matmul(out_ps[0:SEQ, 0:DIM], mixed_t[:, k, :], w_sb["wo"][:, k, :],
                                                start=(k == 0), stop=(k == KD - 1))
                    last.then_inc(projected, 1)

                def step(i, back=True, ahead=True):
                    project(i)
                    if back:
                        turn_mixed(i - 2)
                    scores(i)
                    if back:
                        project_out(i - 2)
                    turn_probs(i - 1, 0)
                    if ahead:
                        turn_x(i + 1)
                    turn_probs(i - 1, 1)
                    attend(i - 1)

                turn_x(0)
                project(0)
                scores(0)
                turn_x(1)
                step(1, back=False)
                with pe.Fori(2, BATCH - 1) as i:
                    step(i)
                step(BATCH - 1, ahead=False)
                turn_mixed(BATCH - 2)
                project_out(BATCH - 2)
                turn_probs(BATCH - 1, 0)
                turn_probs(BATCH - 1, 1)
                attend(BATCH - 1)
                turn_mixed(BATCH - 1)
                project_out(BATCH - 1)

            @block.vector
            def _(dve):
                chain = Chain(dve, dve_chain_sem)
                NORM_LINKS = 1 if pre_norm else 0
                dve.wait_ge(weights_in, WEIGHTS)
                dve.wait_ge(const_ready, CONSTS)
                if x_dram is not None:
                    dve.wait_ge(x_in, 16 * (BATCH // 4))

                def norm_before(i):
                    after(dve, xt_done, i)
                    if pre_norm:
                        nc.vector.bn_stats(stats0[:, :], x_tokens[:, i, :])
                        dve.drain()
                        chain(nc.vector.bn_aggr(mean_var0[:, :], stats0[:, :]))
                        nc.vector.tensor_scalar_add(var_eps0[:, :], mean_var0[:, 1:2], LN_EPS).then_inc(var0_ready, 1)
                        dve.wait_ge(rstd0_ready, i + 1)
                        nc.vector.tensor_scalar(normed[:, :], x_tokens[:, i, :], mean_var0[:, 0:1], rstd0[:, 0:1],
                                                ALU.subtract, ALU.mult).then_inc(normed_ready, 1)
                    else:
                        nc.vector.tensor_copy(normed[:, :], x_tokens[:, i, :]).then_inc(normed_ready, 1)

                def x_turned(i):
                    dve.wait_ge(xt_done, i + 1)
                    after(dve, v_done, i)
                    if pre_norm:
                        for k in range(KD):
                            last = nc.vector.tensor_scalar(x_t[:, k, :], misc_ps[:, k * SEQ:(k + 1) * SEQ],
                                                           gain[:, k:k + 1], shift[:, k:k + 1], ALU.mult, ALU.add)
                    else:
                        last = nc.vector.tensor_copy(x_t[:, :, :], misc_ps[:, 0:KD * SEQ].rearrange("p (k s) -> p k s", k=KD))
                    last.then_inc(xt_ready, 1)

                def keys(i):
                    dve.wait_ge(qk_done, i + 1)
                    dve.wait_ge(q_ready, i + 1)
                    after(dve, scores_done, i)
                    for k in range(KD):
                        source = turn_ps[:, 0, (KD + k) * SEQ:(KD + k + 1) * SEQ]
                        last = nc.vector.scalar_tensor_tensor(
                            out=k_heads[:, k, :, :], in0=source.unsqueeze(1).to_broadcast([128, HPB, SEQ]),
                            scalar=bias_k[:, k:k + 1], in1=head_rows[:, :].unsqueeze(2).to_broadcast([128, HPB, SEQ]),
                            op0=ALU.add, op1=ALU.mult)
                    last.then_inc(k_ready, 1)

                def take_max(i):
                    dve.wait_ge(scores_done, i + 1)
                    view = score_ps[0:SEQ, :, 0:4 * SEQ].rearrange("q b (h k) -> q b h k", h=4)
                    chain(nc.vector.tensor_reduce(row_max[:, :].rearrange("q (b h) -> q b h", b=4), view, AX.X, ALU.max))

                def shift_scores(i):
                    view = score_ps[0:SEQ, :, 0:4 * SEQ].rearrange("q b (h k) -> q b h k", h=4)
                    after(dve, turned, TURNS * i)
                    nc.vector.tensor_tensor(out=probs[:, :, :].rearrange("q (b h) k -> q b h k", b=4), in0=view,
                                            in1=row_max[:, :].rearrange("q (b h) -> q b h", b=4).unsqueeze(3)
                                            .to_broadcast([SEQ, 4, 4, SEQ]),
                                            op=ALU.subtract).then_inc(shifted, 1)

                def normalize(i):
                    dve.wait_ge(attended, i + 1)
                    after(dve, mixed_turned, i)
                    view = out_ps[0:SEQ, 0:HEADS * (HD + 1)].rearrange("q (h e) -> q h e", h=HEADS)
                    chain(nc.vector.reciprocal(inv_sum[:, :].unsqueeze(2), view[:, :, HD:HD + 1]))
                    nc.vector.tensor_tensor(out=mixed[:, :].rearrange("q (h e) -> q h e", h=HEADS), in0=view[:, :, 0:HD],
                                            in1=inv_sum[:, :].unsqueeze(2).to_broadcast([SEQ, HEADS, HD]),
                                            op=ALU.mult).then_inc(mixed_ready, 1)

                def mixed_copy(i):
                    dve.wait_ge(mixed_turned, i + 1)
                    after(dve, projected, i)
                    nc.vector.tensor_copy(mixed_t[:, :, :], misc_ps[:, KD * SEQ:2 * KD * SEQ]
                                          .rearrange("p (k s) -> p k s", k=KD)).then_inc(mixed_t_ready, 1)

                def residual_norm(i):
                    dve.wait_ge(projected, i + 1)
                    dve.wait_ge(x_bias_ready, i + 1)
                    nc.vector.tensor_tensor(out=summed[:, :], in0=out_ps[0:SEQ, 0:DIM], in1=x_bias[:, :],
                                            op=ALU.add).then_inc(summed_done, 1)
                    dve.wait_ge(summed_done, i + 1)
                    nc.vector.bn_stats(stats[:, :], summed[:, :])
                    dve.drain()
                    chain(nc.vector.bn_aggr(mean_var[:, :], stats[:, :]))
                    nc.vector.tensor_scalar_add(var_eps[:, :], mean_var[:, 1:2], LN_EPS).then_inc(var_ready, 1)
                    dve.wait_ge(rstd_ready, i + 1)
                    nc.vector.tensor_scalar(x_tokens[:, i, :], summed[:, :], mean_var[:, 0:1], rstd[:, 0:1],
                                            ALU.subtract, ALU.mult).then_inc(x_new, 1)

                def links_before(i):
                    first = isinstance(i, int) and i == 1
                    return NORM_LINKS * (i + 1) + i + (i - 1) + (0 if first else i - 2)

                def step(i, back=True, ahead=True):
                    chain.begin(links_before(i))
                    keys(i)
                    if back:
                        mixed_copy(i - 2)
                    if ahead:
                        norm_before(i + 1)
                    take_max(i)
                    if back:
                        residual_norm(i - 2)
                    shift_scores(i)
                    if ahead:
                        x_turned(i + 1)
                    normalize(i - 1)
                    assert chain.n == 2 + (1 if back else 0) + (NORM_LINKS if ahead else 0)

                chain.begin(0)
                norm_before(0)
                x_turned(0)
                keys(0)
                take_max(0)
                shift_scores(0)
                norm_before(1)
                x_turned(1)
                step(1, back=False)
                with dve.Fori(2, BATCH - 1) as i:
                    step(i)
                step(BATCH - 1, ahead=False)
                chain.begin(NORM_LINKS * BATCH + BATCH + (BATCH - 1) + (BATCH - 2))
                mixed_copy(BATCH - 2)
                residual_norm(BATCH - 2)
                normalize(BATCH - 1)
                mixed_copy(BATCH - 1)
                residual_norm(BATCH - 1)
                dve.wait_ge(x_new, BATCH)


def load_pass(nc, prefix, x_tokens, source):
    with ExitStack() as stack:
        mem = Memory(nc, stack, prefix)
        loaded = mem.sem("loaded")
        with nc.Block() as block:

            @block.sync
            def _(sp):
                for r in range(0, BATCH, 4):
                    sp.dma_start(x_tokens[:, r:r + 4, :], source[r:r + 4].rearrange("b s d -> s b d")).then_inc(loaded, 16)
                sp.wait_ge(loaded, 16 * (BATCH // 4))


def store_pass(nc, prefix, x_tokens, out):
    with ExitStack() as stack:
        mem = Memory(nc, stack, prefix)
        stored = mem.sem("stored")
        with nc.Block() as block:

            @block.sync
            def _(sp):
                for r in range(0, BATCH, 4):
                    sp.dma_start(out[r:r + 4].rearrange("b s d -> s b d"), x_tokens[:, r:r + 4, :]).then_inc(stored, 16)
                sp.wait_ge(stored, 16 * (BATCH // 4))


def constants_pass(nc, ident, minus_half):
    with ExitStack() as stack:
        mem = Memory(nc, stack, "const")
        cleared = mem.sem("cleared")
        with nc.Block() as block:

            @block.gpsimd
            def _(pool):
                nc.gpsimd.memset(minus_half[:, :], -0.5).then_inc(cleared, 1)
                nc.gpsimd.memset(ident[:, :], 0.0).then_inc(cleared, 1)
                pool.wait_ge(cleared, 2)
                nc.gpsimd.affine_select(out=ident[:, :], in_=ident[:, :], compare_op=ALU.not_equal, fill=1.0, base=0,
                                        pattern=[[-1, 128]], channel_multiplier=1).then_inc(cleared, 1)
                pool.wait_ge(cleared, 3)


def experts_pass(nc, x_tokens, ident, minus_half, wg, wu, wd, wr, temperature):
    GROUPS = BATCH // GROUP
    TOK = GROUP * SEQ
    FT = EXPERT_F // 128
    UNITS = EXPERTS * FT
    GOLDEN_CENTER = 0.36787944117144233
    GOLDEN_LOWER = 0.2123179275482191
    GOLDEN_UPPER = 0.5
    with ExitStack() as stack:
        mem = Memory(nc, stack, "moe")
        wg_sb = mem.sbuf("wg", [128, EXPERTS, KD, EXPERT_F])
        wu_sb = mem.sbuf("wu", [128, EXPERTS, KD, EXPERT_F])
        wd_sb = mem.sbuf("wd", [128, EXPERTS, FT, DIM])
        wr_sb = mem.sbuf("wr", [128, KD, EXPERTS])
        temp = mem.sbuf("temp", [SEQ, 1])
        half_inv_temp = mem.sbuf("half_inv_temp", [SEQ, 1])
        lower_expert = mem.sbuf("lower_expert", [SEQ, EXPERTS, EXPERTS])
        x_rows = mem.sbuf("x_rows", [SEQ, GROUP, DIM])
        x_t = mem.sbuf("x_t", [128, KD, TOK])
        tanh_g = mem.sbuf("tanh_g", [128, 2, TOK])
        gated = mem.sbuf("gated", [128, 2, TOK])
        hidden_t = mem.sbuf("hidden_t", [128, 2 * FT, TOK])
        total = mem.sbuf("total", [SEQ, GROUP, DIM])
        SMALL = [SEQ, GROUP, EXPERTS]
        tanh_z, inh, dist, zone, narrow, wide, rank, mix = (mem.sbuf(n, SMALL) for n in (
            "tanh_z", "inh", "dist", "zone", "narrow", "wide", "rank", "mix"))
        greater = mem.sbuf("greater", [SEQ, GROUP, EXPERTS, EXPERTS])
        equal = mem.sbuf("equal", [SEQ, GROUP, EXPERTS, EXPERTS])
        weight_sum = mem.sbuf("weight_sum", [SEQ, GROUP])
        nobody = mem.sbuf("nobody", [SEQ, GROUP])
        stats = mem.sbuf("stats", [SEQ, GROUP, 6])
        mean_var = mem.sbuf("mean_var", [SEQ, GROUP, 2])
        var_eps = mem.sbuf("var_eps", [SEQ, GROUP])
        rstd = mem.sbuf("rstd", [SEQ, GROUP])

        gate_ps = mem.psum("gate_ps", [128, 2, BANK])
        up_ps = mem.psum("up_ps", [128, 2, BANK])
        out_ps = mem.psum("out_ps", [128, 2, BANK])
        xt_ps = mem.psum("xt_ps", [128, KD, BANK])

        weights_in, consts_ready = mem.sem("weights_in"), mem.sem("consts_ready")
        dve_chain_sem, pool_chain_sem = mem.sem("dve_order"), mem.sem("pool_order")
        xt_done, xt_ready, logits_done = mem.sem("xt_done"), mem.sem("xt_ready"), mem.sem("logits_done")
        router_tanh, distance_ready, router_exp = mem.sem("router_tanh"), mem.sem("distance_ready"), mem.sem("router_exp")
        gate_up_done, tanh_ready = mem.sem("gate_up_done"), mem.sem("tanh_ready")
        hidden_ready, down_done, added = mem.sem("hidden_ready"), mem.sem("down_done"), mem.sem("added")
        var_ready, rstd_ready, x_new = mem.sem("var_ready"), mem.sem("rstd_ready"), mem.sem("x_new")
        temp_ready, rows_ready = mem.sem("temp_ready"), mem.sem("rows_ready")
        WEIGHTS = 16 * 5

        with nc.Block() as block:

            @block.sync
            def _(sp):
                sp.dma_start(wr_sb[:, :, :], wr.rearrange("(k p) e -> p k e", p=128)).then_inc(weights_in, 16)
                sp.dma_start(temp[:, :], temperature.partition_broadcast(SEQ)).then_inc(weights_in, 16)
                sp.dma_start(wg_sb[:, :, :, :], wg.rearrange("e (k p) f -> p e k f", p=128)).then_inc(weights_in, 16)
                sp.dma_start(wu_sb[:, :, :, :], wu.rearrange("e (k p) f -> p e k f", p=128)).then_inc(weights_in, 16)
                sp.dma_start(wd_sb[:, :, :, :], wd.rearrange("e (k p) d -> p e k d", p=128)).then_inc(weights_in, 16)
                sp.wait_ge(weights_in, WEIGHTS)

            @block.gpsimd
            def _(pool):
                chain = Chain(pool, pool_chain_sem)
                chain(nc.gpsimd.memset(lower_expert[:, :, :], 1.0))
                nc.gpsimd.affine_select(out=lower_expert[:, :, :], in_=lower_expert[:, :, :], compare_op=ALU.is_gt,
                                        fill=0.0, base=0, pattern=[[1, EXPERTS], [-1, EXPERTS]],
                                        channel_multiplier=0).then_inc(consts_ready, 1)
                with pool.Fori(0, GROUPS) as g:
                    pool.wait_ge(var_ready, g + 1)
                    nc.gpsimd.tensor_tensor(out=rstd[:, :], in0=var_eps[:, :],
                                            in1=minus_half[0:SEQ, :].to_broadcast([SEQ, GROUP]),
                                            op=ALU.pow).then_inc(rstd_ready, 1)

            @block.scalar
            def _(act):
                act.wait_ge(weights_in, WEIGHTS)
                act.wait_ge(temp_ready, 1)

                def gate_tanh(g, u):
                    act.wait_ge(gate_up_done, UNITS * g + u + 1)
                    if u >= 2:
                        act.wait_ge(hidden_ready, UNITS * g + u - 1)
                    else:
                        after(act, hidden_ready, UNITS * g)
                    nc.scalar.activation(tanh_g[:, u % 2, :], gate_ps[:, u % 2, 0:TOK], ACT.Tanh,
                                         scale=0.5).then_inc(tanh_ready, 1)

                def step(g):
                    act.wait_ge(logits_done, g + 1)
                    nc.scalar.activation(tanh_z[:, :, :],
                                         xt_ps[0:SEQ, 0, TOK:TOK + GROUP * EXPERTS].rearrange("s (r e) -> s r e", r=GROUP),
                                         ACT.Tanh, scale=half_inv_temp[:, 0:1]).then_inc(router_tanh, 1)
                    gate_tanh(g, 0)
                    act.wait_ge(distance_ready, g + 1)
                    nc.scalar.activation(narrow[:, :, :], dist[:, :, :], ACT.Exp, scale=-1.0 / 0.1)
                    nc.scalar.activation(wide[:, :, :], dist[:, :, :], ACT.Exp, scale=-1.0 / 0.3).then_inc(router_exp, 1)
                    for u in range(1, UNITS):
                        gate_tanh(g, u)

                step(0)
                with act.Fori(1, GROUPS) as g:
                    step(g)

            @block.tensor
            def _(pe):
                pe.wait_ge(weights_in, WEIGHTS)

                def gate_up(g, u):
                    e, f = u // FT, u % FT
                    if u >= 2:
                        pe.wait_ge(hidden_ready, UNITS * g + u - 1)
                    else:
                        after(pe, hidden_ready, UNITS * g)
                    for w, ps in ((wg_sb, gate_ps), (wu_sb, up_ps)):
                        for k in range(KD):
                            last = nc.tensor.matmul(ps[:, u % 2, 0:TOK], w[:, e, k, f * 128:(f + 1) * 128], x_t[:, k, :],
                                                    start=(k == 0), stop=(k == KD - 1))
                    last.then_inc(gate_up_done, 1)

                def down(g, e):
                    pe.wait_ge(hidden_ready, UNITS * g + FT * (e + 1))
                    if e:
                        pe.wait_ge(added, EXPERTS * g + e)
                    else:
                        after(pe, added, EXPERTS * g)
                    for r in range(GROUP):
                        for k in range(FT):
                            last = nc.tensor.matmul(out_ps[0:SEQ, r // 2, (r % 2) * DIM:(r % 2 + 1) * DIM],
                                                    hidden_t[:, (FT * e + k) % (2 * FT), r * SEQ:(r + 1) * SEQ],
                                                    wd_sb[:, e, k, :], start=(k == 0), stop=(k == FT - 1))
                    last.then_inc(down_done, 1)

                def turn_x(g):
                    pe.wait_ge(rows_ready, g + 1)
                    after(pe, xt_ready, g)
                    after(pe, router_tanh, g)
                    for k in range(KD):
                        for r in range(GROUP):
                            last = nc.tensor.transpose(xt_ps[:, k, r * SEQ:(r + 1) * SEQ],
                                                       x_rows[:, r, k * 128:(k + 1) * 128], ident[0:SEQ, 0:SEQ])
                    last.then_inc(xt_done, 1)

                def step(g, ahead=True):
                    pe.wait_ge(xt_ready, g + 1)
                    for r in range(GROUP):
                        for k in range(KD):
                            last = nc.tensor.matmul(xt_ps[0:SEQ, 0, TOK + r * EXPERTS:TOK + (r + 1) * EXPERTS],
                                                    x_t[:, k, r * SEQ:(r + 1) * SEQ], wr_sb[:, k, :],
                                                    start=(k == 0), stop=(k == KD - 1))
                    last.then_inc(logits_done, 1)
                    for e in range(EXPERTS):
                        for f in range(FT):
                            gate_up(g, FT * e + f)
                        if ahead and e == EXPERTS - 1:
                            turn_x(g + 1)
                        if e:
                            down(g, e - 1)
                    down(g, EXPERTS - 1)

                turn_x(0)
                step(0)
                with pe.Fori(1, GROUPS - 1) as g:
                    step(g)
                step(GROUPS - 1, ahead=False)

            @block.vector
            def _(dve):
                chain = Chain(dve, dve_chain_sem)
                LINKS = 24 + UNITS + 1
                dve.wait_ge(weights_in, WEIGHTS)
                dve.wait_ge(consts_ready, 1)
                chain.begin(0)
                chain(nc.vector.reciprocal(half_inv_temp[:, :], temp[:, :]))
                nc.vector.tensor_scalar(half_inv_temp[:, :], half_inv_temp[:, :], 0.5, None, ALU.mult).then_inc(temp_ready, 1)

                def gather_rows(g):
                    after(dve, xt_done, g)
                    nc.vector.tensor_copy(x_rows[:, :, :], x_tokens[:, bass.ds(g * GROUP, GROUP), :]).then_inc(rows_ready, 1)

                def distances(g):
                    dve.wait_ge(router_tanh, g + 1)
                    chain(nc.vector.tensor_scalar(inh[:, :, :], tanh_z[:, :, :], 0.5, 0.5, ALU.mult, ALU.add))
                    chain(nc.vector.tensor_scalar(dist[:, :, :], inh[:, :, :], GOLDEN_CENTER, None, ALU.subtract))
                    nc.vector.scalar_tensor_tensor(out=dist[:, :, :], in0=dist[:, :, :], scalar=-1.0, in1=dist[:, :, :],
                                                   op0=ALU.mult, op1=ALU.max).then_inc(distance_ready, 1)
                    chain(nc.vector.tensor_scalar(zone[:, :, :], inh[:, :, :], GOLDEN_LOWER, None, ALU.is_ge))
                    chain(nc.vector.scalar_tensor_tensor(out=zone[:, :, :], in0=inh[:, :, :], scalar=GOLDEN_UPPER,
                                                         in1=zone[:, :, :], op0=ALU.is_le, op1=ALU.mult))

                def route(g):
                    dve.wait_ge(router_exp, g + 1)
                    ej = [SEQ, GROUP, EXPERTS, EXPERTS]
                    of_j, of_e = wide[:, :, :].unsqueeze(2).to_broadcast(ej), wide[:, :, :].unsqueeze(3).to_broadcast(ej)
                    nc.vector.tensor_tensor(out=greater[:, :, :, :], in0=of_j, in1=of_e, op=ALU.is_gt)
                    chain(nc.vector.tensor_tensor(out=equal[:, :, :, :], in0=of_j, in1=of_e, op=ALU.is_equal))
                    chain(nc.vector.tensor_tensor(out=equal[:, :, :, :], in0=equal[:, :, :, :],
                                                  in1=lower_expert[:, :, :].unsqueeze(1).to_broadcast(ej), op=ALU.mult))
                    chain(nc.vector.tensor_tensor(out=greater[:, :, :, :], in0=greater[:, :, :, :], in1=equal[:, :, :, :],
                                                  op=ALU.add))
                    chain(nc.vector.tensor_reduce(rank[:, :, :], greater[:, :, :, :], AX.X, ALU.add))
                    chain(nc.vector.scalar_tensor_tensor(out=wide[:, :, :], in0=rank[:, :, :], scalar=2.0,
                                                         in1=wide[:, :, :], op0=ALU.is_lt, op1=ALU.mult))
                    chain(nc.vector.tensor_reduce(weight_sum[:, :], wide[:, :, :], AX.X, ALU.add))
                    chain(nc.vector.tensor_scalar(weight_sum[:, :], weight_sum[:, :], 1e-8, None, ALU.max))
                    chain(nc.vector.reciprocal(weight_sum[:, :], weight_sum[:, :]))
                    chain(nc.vector.tensor_tensor(out=wide[:, :, :], in0=wide[:, :, :],
                                                  in1=weight_sum[:, :].unsqueeze(2).to_broadcast(SMALL), op=ALU.mult))
                    chain(nc.vector.tensor_tensor(out=narrow[:, :, :], in0=narrow[:, :, :], in1=zone[:, :, :], op=ALU.mult))
                    chain(nc.vector.tensor_reduce(weight_sum[:, :], narrow[:, :, :], AX.X, ALU.add))
                    chain(nc.vector.tensor_scalar(nobody[:, :], weight_sum[:, :], 1e-8, None, ALU.is_lt))
                    chain(nc.vector.tensor_tensor(out=wide[:, :, :], in0=wide[:, :, :],
                                                  in1=nobody[:, :].unsqueeze(2).to_broadcast(SMALL), op=ALU.mult))
                    chain(nc.vector.tensor_scalar(nobody[:, :], nobody[:, :], -1.0, 1.0, ALU.mult, ALU.add))
                    chain(nc.vector.tensor_tensor(out=narrow[:, :, :], in0=narrow[:, :, :],
                                                  in1=nobody[:, :].unsqueeze(2).to_broadcast(SMALL), op=ALU.mult))
                    chain(nc.vector.tensor_tensor(out=narrow[:, :, :], in0=narrow[:, :, :], in1=wide[:, :, :], op=ALU.add))
                    chain(nc.vector.tensor_reduce(weight_sum[:, :], narrow[:, :, :], AX.X, ALU.add))
                    chain(nc.vector.tensor_scalar(weight_sum[:, :], weight_sum[:, :], 1e-8, None, ALU.max))
                    chain(nc.vector.reciprocal(weight_sum[:, :], weight_sum[:, :]))
                    chain(nc.vector.tensor_tensor(out=mix[:, :, :], in0=narrow[:, :, :],
                                                  in1=weight_sum[:, :].unsqueeze(2).to_broadcast(SMALL), op=ALU.mult))

                def hidden(g, u):
                    dve.wait_ge(tanh_ready, UNITS * g + u + 1)
                    if u >= 2 * FT:
                        dve.wait_ge(down_done, EXPERTS * g + u // FT - 1)
                    else:
                        after(dve, down_done, EXPERTS * g)
                    chain(nc.vector.scalar_tensor_tensor(out=gated[:, u % 2, :], in0=tanh_g[:, u % 2, :], scalar=1.0,
                                                         in1=gate_ps[:, u % 2, 0:TOK], op0=ALU.add, op1=ALU.mult))
                    nc.vector.scalar_tensor_tensor(out=hidden_t[:, u % (2 * FT), :], in0=gated[:, u % 2, :], scalar=0.5,
                                                   in1=up_ps[:, u % 2, 0:TOK], op0=ALU.mult,
                                                   op1=ALU.mult).then_inc(hidden_ready, 1)

                def add_expert(g, e):
                    dve.wait_ge(down_done, EXPERTS * g + e + 1)
                    if e:
                        dve.wait_ge(added, EXPERTS * g + e)
                    for r in range(GROUP):
                        base = total[:, r, :] if e else x_tokens[:, g * GROUP + r, :]
                        last = nc.vector.scalar_tensor_tensor(
                            out=total[:, r, :], in0=out_ps[0:SEQ, r // 2, (r % 2) * DIM:(r % 2 + 1) * DIM],
                            scalar=mix[:, r, e:e + 1], in1=base, op0=ALU.mult, op1=ALU.add)
                    last.then_inc(added, 1)

                def layer_norm(g):
                    dve.wait_ge(added, EXPERTS * (g + 1))
                    for r in range(GROUP):
                        nc.vector.bn_stats(stats[:, r, :], total[:, r, :])
                    dve.drain()
                    for r in range(GROUP):
                        last = nc.vector.bn_aggr(mean_var[:, r, :], stats[:, r, :])
                    chain(last)
                    nc.vector.tensor_scalar_add(var_eps[:, :], mean_var[:, :, 1], LN_EPS).then_inc(var_ready, 1)
                    dve.wait_ge(rstd_ready, g + 1)
                    for r in range(GROUP):
                        last = nc.vector.tensor_scalar(x_tokens[:, g * GROUP + r, :], total[:, r, :], mean_var[:, r, 0:1],
                                                       rstd[:, r:r + 1], ALU.subtract, ALU.mult)
                    last.then_inc(x_new, 1)

                def copy_xt(g):
                    dve.wait_ge(xt_done, g + 1)
                    after(dve, gate_up_done, UNITS * g)
                    nc.vector.tensor_copy(x_t[:, :, :], xt_ps[:, :, 0:TOK]).then_inc(xt_ready, 1)

                def step(g, ahead=True):
                    chain.begin(1 + g * LINKS)
                    distances(g)
                    hidden(g, 0)
                    route(g)
                    hidden(g, 1)
                    for e in range(1, EXPERTS):
                        for f in range(FT):
                            hidden(g, FT * e + f)
                        if ahead and e == EXPERTS - 3:
                            gather_rows(g + 1)
                        if ahead and e == EXPERTS - 1:
                            copy_xt(g + 1)
                        add_expert(g, e - 1)
                    add_expert(g, EXPERTS - 1)
                    layer_norm(g)
                    assert chain.n == LINKS

                gather_rows(0)
                copy_xt(0)
                step(0)
                with dve.Fori(1, GROUPS - 1) as g:
                    step(g)
                step(GROUPS - 1, ahead=False)
                dve.wait_ge(x_new, GROUPS)


def quantized_ffn_pass(nc, x_tokens, ident, minus_half, w_gate, w_up, w_down, s_gate, s_up, s_down):
    GROUPS = BATCH // GROUP
    TOK = GROUP * SEQ
    FT = INTER // 128
    with ExitStack() as stack:
        mem = Memory(nc, stack, "qffn")
        packed = mem.sbuf("packed", [128, KD, INTER // 4], mybir.dt.int32)
        packed_up = mem.sbuf("packed_up", [128, KD, INTER // 4], mybir.dt.int32)
        packed_down = mem.sbuf("packed_down", [128, FT, DIM // 4], mybir.dt.int32)
        gate_sb = mem.sbuf("gate_w", [128, KD, INTER])
        up_sb = mem.sbuf("up_w", [128, KD, INTER])
        down_sb = mem.sbuf("down_w", [128, FT, DIM])
        gate_scale = mem.sbuf("gate_scale", [128, FT])
        up_scale = mem.sbuf("up_scale", [128, FT])
        half_gate_scale = mem.sbuf("half_gate_scale", [128, FT])
        product_scale = mem.sbuf("product_scale", [128, FT])
        down_scale = mem.sbuf("down_scale", [SEQ, DIM])
        x_rows = mem.sbuf("x_rows", [SEQ, GROUP, DIM])
        x_t = mem.sbuf("x_t", [128, KD, TOK])
        tanh_g = mem.sbuf("tanh_g", [128, 2, TOK])
        gated = mem.sbuf("gated", [128, 2, TOK])
        hidden_t = mem.sbuf("hidden_t", [128, FT, TOK])
        total = mem.sbuf("total", [SEQ, GROUP, DIM])
        stats = mem.sbuf("stats", [SEQ, GROUP, 6])
        mean_var = mem.sbuf("mean_var", [SEQ, GROUP, 2])
        var_eps = mem.sbuf("var_eps", [SEQ, GROUP])
        rstd = mem.sbuf("rstd", [SEQ, GROUP])

        gate_ps = mem.psum("gate_ps", [128, 2, BANK])
        up_ps = mem.psum("up_ps", [128, 2, BANK])
        out_ps = mem.psum("out_ps", [128, 2, BANK])
        xt_ps = mem.psum("xt_ps", [128, KD, BANK])

        weights_in, weights_ready, scales_ready = mem.sem("weights_in"), mem.sem("weights_ready"), mem.sem("scales_ready")
        dve_chain_sem = mem.sem("dve_order")
        rows_ready, xt_done, xt_ready = mem.sem("rows_ready"), mem.sem("xt_done"), mem.sem("xt_ready")
        gate_up_done, tanh_ready, hidden_ready = mem.sem("gate_up_done"), mem.sem("tanh_ready"), mem.sem("hidden_ready")
        down_done, summed = mem.sem("down_done"), mem.sem("summed")
        var_ready, rstd_ready, x_new = mem.sem("var_ready"), mem.sem("rstd_ready"), mem.sem("x_new")
        WEIGHTS = 16 * 6

        with nc.Block() as block:

            @block.sync
            def _(sp):
                sp.dma_start(packed[:, :, :], w_gate.rearrange("(k p) n -> p k n", p=128)).then_inc(weights_in, 16)
                sp.dma_start(packed_up[:, :, :], w_up.rearrange("(k p) n -> p k n", p=128)).then_inc(weights_in, 16)
                sp.dma_start(packed_down[:, :, :], w_down.rearrange("(k p) n -> p k n", p=128)).then_inc(weights_in, 16)
                with nc.allow_non_contiguous_dma(reason="scales, once"):
                    sp.dma_start(gate_scale[:, :], s_gate.rearrange("(t p) -> p t", p=128)).then_inc(weights_in, 16)
                    sp.dma_start(up_scale[:, :], s_up.rearrange("(t p) -> p t", p=128)).then_inc(weights_in, 16)
                sp.dma_start(down_scale[:, :], s_down.partition_broadcast(SEQ)).then_inc(weights_in, 16)
                sp.wait_ge(weights_in, WEIGHTS)

            @block.gpsimd
            def _(pool):
                with pool.Fori(0, GROUPS) as g:
                    pool.wait_ge(var_ready, g + 1)
                    nc.gpsimd.tensor_tensor(out=rstd[:, :], in0=var_eps[:, :],
                                            in1=minus_half[0:SEQ, :].to_broadcast([SEQ, GROUP]),
                                            op=ALU.pow).then_inc(rstd_ready, 1)

            @block.scalar
            def _(act):
                act.wait_ge(weights_in, WEIGHTS)
                nc.scalar.activation(up_sb[:, :, :], packed_up[:, :, :].bitcast(I8), ACT.Copy).then_inc(weights_ready, 1)
                act.wait_ge(scales_ready, 1)

                def gate_tanh(g, u):
                    act.wait_ge(gate_up_done, FT * g + u + 1)
                    if u >= 2:
                        act.wait_ge(hidden_ready, FT * g + u - 1)
                    else:
                        after(act, hidden_ready, FT * g)
                    nc.scalar.activation(tanh_g[:, u % 2, :], gate_ps[:, u % 2, 0:TOK], ACT.Tanh,
                                         scale=half_gate_scale[:, u:u + 1]).then_inc(tanh_ready, 1)

                def step(g):
                    for u in range(FT):
                        gate_tanh(g, u)

                step(0)
                with act.Fori(1, GROUPS) as g:
                    step(g)

            @block.tensor
            def _(pe):
                pe.wait_ge(weights_ready, 3)

                def gate_up(g, u):
                    if u >= 2:
                        pe.wait_ge(hidden_ready, FT * g + u - 1)
                    else:
                        after(pe, hidden_ready, FT * g)
                    for w, ps in ((gate_sb, gate_ps), (up_sb, up_ps)):
                        for k in range(KD):
                            last = nc.tensor.matmul(ps[:, u % 2, 0:TOK], w[:, k, u * 128:(u + 1) * 128], x_t[:, k, :],
                                                    start=(k == 0), stop=(k == KD - 1))
                    last.then_inc(gate_up_done, 1)

                def turn_x(g):
                    pe.wait_ge(rows_ready, g + 1)
                    after(pe, xt_ready, g)
                    for k in range(KD):
                        for r in range(GROUP):
                            last = nc.tensor.transpose(xt_ps[:, k, r * SEQ:(r + 1) * SEQ],
                                                       x_rows[:, r, k * 128:(k + 1) * 128], ident[0:SEQ, 0:SEQ])
                    last.then_inc(xt_done, 1)

                def step(g, ahead=True):
                    pe.wait_ge(xt_ready, g + 1)
                    for u in range(FT):
                        gate_up(g, u)
                    if ahead:
                        turn_x(g + 1)
                    pe.wait_ge(hidden_ready, FT * (g + 1))
                    after(pe, summed, g)
                    for r in range(GROUP):
                        for k in range(FT):
                            last = nc.tensor.matmul(out_ps[0:SEQ, r // 2, (r % 2) * DIM:(r % 2 + 1) * DIM],
                                                    hidden_t[:, k, r * SEQ:(r + 1) * SEQ], down_sb[:, k, :],
                                                    start=(k == 0), stop=(k == FT - 1))
                    last.then_inc(down_done, 1)

                turn_x(0)
                step(0)
                with pe.Fori(1, GROUPS - 1) as g:
                    step(g)
                step(GROUPS - 1, ahead=False)

            @block.vector
            def _(dve):
                chain = Chain(dve, dve_chain_sem)
                LINKS = FT + 2
                dve.wait_ge(weights_in, WEIGHTS)
                nc.vector.tensor_copy(gate_sb[:, :, :], packed[:, :, :].bitcast(I8)).then_inc(weights_ready, 1)
                nc.vector.tensor_copy(down_sb[:, :, :], packed_down[:, :, :].bitcast(I8)).then_inc(weights_ready, 1)
                chain.begin(0)
                chain(nc.vector.tensor_scalar(half_gate_scale[:, :], gate_scale[:, :], 0.5, None, ALU.mult))
                nc.vector.tensor_tensor(out=product_scale[:, :], in0=half_gate_scale[:, :], in1=up_scale[:, :],
                                        op=ALU.mult).then_inc(scales_ready, 1)
                dve.wait_ge(scales_ready, 1)

                def hidden(g, u):
                    dve.wait_ge(tanh_ready, FT * g + u + 1)
                    after(dve, down_done, g)
                    chain(nc.vector.scalar_tensor_tensor(out=gated[:, u % 2, :], in0=tanh_g[:, u % 2, :], scalar=1.0,
                                                         in1=gate_ps[:, u % 2, 0:TOK], op0=ALU.add, op1=ALU.mult))
                    nc.vector.scalar_tensor_tensor(out=hidden_t[:, u, :], in0=gated[:, u % 2, :],
                                                   scalar=product_scale[:, u:u + 1],
                                                   in1=up_ps[:, u % 2, 0:TOK], op0=ALU.mult,
                                                   op1=ALU.mult).then_inc(hidden_ready, 1)

                def gather_rows(g):
                    after(dve, xt_done, g)
                    nc.vector.tensor_copy(x_rows[:, :, :], x_tokens[:, bass.ds(g * GROUP, GROUP), :]).then_inc(rows_ready, 1)

                def copy_xt(g):
                    dve.wait_ge(xt_done, g + 1)
                    after(dve, gate_up_done, FT * g)
                    nc.vector.tensor_copy(x_t[:, :, :], xt_ps[:, :, 0:TOK]).then_inc(xt_ready, 1)

                def step(g, ahead=True):
                    chain.begin(1 + g * LINKS)
                    for u in range(FT):
                        hidden(g, u)
                        if ahead and u == FT // 2:
                            gather_rows(g + 1)
                    if ahead:
                        copy_xt(g + 1)
                    dve.wait_ge(down_done, g + 1)
                    view = out_ps[0:SEQ, :, :].rearrange("s b (r d) -> s (b r) d", r=2)
                    chain(nc.vector.tensor_tensor(out=total[:, :, :], in0=view,
                                                  in1=down_scale[:, :].unsqueeze(1).to_broadcast([SEQ, GROUP, DIM]),
                                                  op=ALU.mult))
                    nc.vector.tensor_tensor(out=total[:, :, :], in0=total[:, :, :],
                                            in1=x_tokens[:, bass.ds(g * GROUP, GROUP), :], op=ALU.add).then_inc(summed, 1)
                    dve.wait_ge(summed, g + 1)
                    for r in range(GROUP):
                        nc.vector.bn_stats(stats[:, r, :], total[:, r, :])
                    dve.drain()
                    for r in range(GROUP):
                        last = nc.vector.bn_aggr(mean_var[:, r, :], stats[:, r, :])
                    chain(last)
                    nc.vector.tensor_scalar_add(var_eps[:, :], mean_var[:, :, 1], LN_EPS).then_inc(var_ready, 1)
                    dve.wait_ge(rstd_ready, g + 1)
                    for r in range(GROUP):
                        last = nc.vector.tensor_scalar(x_tokens[:, g * GROUP + r, :], total[:, r, :], mean_var[:, r, 0:1],
                                                       rstd[:, r:r + 1], ALU.subtract, ALU.mult)
                    last.then_inc(x_new, 1)
                    assert chain.n == LINKS

                gather_rows(0)
                copy_xt(0)
                step(0)
                with dve.Fori(1, GROUPS - 1) as g:
                    step(g)
                step(GROUPS - 1, ahead=False)
                dve.wait_ge(x_new, GROUPS)


TILES = 12
TILE = 120
LAST = CTX - (TILES - 1) * TILE
FOUR = 4
CHUNKS = TILES // FOUR


def tile_rows(t):
    return LAST if t == TILES - 1 else TILE


def chunk_columns(c):
    return c * FOUR * TILE, sum(tile_rows(t) for t in range(FOUR * c, FOUR * c + FOUR))


def load_context(engine, destination, ctx_row, arrived):
    body = (TILES - 1) * TILE
    engine.dma_start(destination[0:TILE, 0:TILES - 1, :],
                     ctx_row[0:body].rearrange("(p t) d -> p t d", t=TILES - 1)).then_inc(arrived, 16)
    engine.dma_start(destination[0:LAST, TILES - 1, :], ctx_row[body:CTX]).then_inc(arrived, 16)


def memory_attention_pass(nc, x_tokens, ctx, mask_words, ident, minus_half):
    SCALE = float(DIM) ** -0.5
    HIDDEN = NEG / SCALE
    AHEAD = 4
    TURNS = 1 + KD * CHUNKS
    with ExitStack() as stack:
        mem = Memory(nc, stack, "memory")
        keys = [mem.sbuf(f"keys{p}", [LAST, TILES, DIM]) for p in range(AHEAD)]
        keys_t = [mem.sbuf(f"keys_t{p}", [128, KD, CTX]) for p in range(2)]
        mask_row = [mem.sbuf(f"mask_row{p}", [1, CTX // 4], mybir.dt.int32) for p in range(AHEAD)]
        mask_bias = [mem.sbuf(f"mask_bias{p}", [1, CTX], BF16) for p in range(2)]
        ones_row = mem.sbuf("ones_row", [1, SEQ], BF16)
        x_row = [mem.sbuf(f"x_row{p}", [SEQ, DIM]) for p in range(AHEAD)]
        x_t = mem.sbuf("x_t", [128, KD, SEQ])
        probs = mem.sbuf("probs", [SEQ, CTX])
        probs_t = mem.sbuf("probs_t", [LAST, TILES, SEQ])
        part_max = mem.sbuf("part_max", [SEQ, 2])
        row_max = mem.sbuf("row_max", [SEQ, 1])
        neg_max = mem.sbuf("neg_max", [SEQ, 1])
        any_key = mem.sbuf("any_key", [SEQ, 1])
        part_sum = mem.sbuf("part_sum", [SEQ, 2])
        inv_sum = mem.sbuf("inv_sum", [SEQ, 1])
        factor = mem.sbuf("factor", [SEQ, 1])
        summed = mem.sbuf("summed", [SEQ, DIM])
        stats = mem.sbuf("stats", [SEQ, 6])
        mean_var = mem.sbuf("mean_var", [SEQ, 2])
        var_eps = mem.sbuf("var_eps", [SEQ, 1])
        rstd = mem.sbuf("rstd", [SEQ, 1])

        turn_ps = mem.psum("turn_ps", [128, 2, BANK])
        score_ps = mem.psum("score_ps", [128, CHUNKS, BANK])
        probs_ps = mem.psum("probs_ps", [128, 2, BANK])
        out_ps = mem.psum("out_ps", [128, BANK])

        keys_in = [mem.sem(f"keys_in{p}") for p in range(AHEAD)]
        mask_in = [mem.sem(f"mask_in{p}") for p in range(AHEAD)]
        ones_ready, dve_chain_sem, pool_chain_sem = mem.sem("ones_ready"), mem.sem("dve_order"), mem.sem("pool_order")
        x_row_ready, mask_ready = mem.sem("x_row_ready"), mem.sem("mask_ready")
        turned = mem.sem("turned")
        copied_dve, copied_act = mem.sem("copied_dve"), mem.sem("copied_act")
        scores_done, max_ready, probs_ready = mem.sem("scores_done"), mem.sem("max_ready"), mem.sem("probs_ready")
        probs_turned, probs_copied, attended = mem.sem("probs_turned"), mem.sem("probs_copied"), mem.sem("attended")
        summed_done, var_ready, rstd_ready, x_new = (mem.sem("summed_done"), mem.sem("var_ready"),
                                                     mem.sem("rstd_ready"), mem.sem("x_new"))
        DVE_TURNS, ACT_TURNS = (TURNS + 1) // 2, TURNS // 2

        def turn_bank(p, u):
            return turn_ps[:, (TURNS * p + u) % 2, :]

        def previous_copied(engine, b, u):
            back = u - 2
            row = b if back >= 0 else b - 1
            back %= TURNS
            if back % 2 == 0:
                after(engine, copied_dve, DVE_TURNS * row + back // 2 + 1 if not isinstance(row, int) or row >= 0 else 0)
            else:
                after(engine, copied_act, ACT_TURNS * row + back // 2 + 1 if not isinstance(row, int) or row >= 0 else 0)

        def reused(b):
            return b - AHEAD + 1 if not isinstance(b, int) or b >= AHEAD else 0

        with nc.Block() as block:

            @block.sync
            def _(sp):
                def load(b, p):
                    after(sp, attended, reused(b))
                    load_context(sp, keys[p], ctx[b], keys_in[p])
                    after(sp, mask_ready, reused(b))
                    sp.dma_start(mask_row[p][:, :], mask_words[bass.ds(b, 1), :]).then_inc(mask_in[p], 16)

                for p in range(AHEAD):
                    load(p, p)
                with sp.Fori(1, BATCH // AHEAD) as j:
                    for p in range(AHEAD):
                        load(AHEAD * j + p, p)

            @block.gpsimd
            def _(pool):
                nc.gpsimd.memset(ones_row[:, :], 1.0).then_inc(ones_ready, 1)

                def front(b, p):
                    after(pool, summed_done, reused(b))
                    nc.gpsimd.tensor_copy(x_row[p][:, :], x_tokens[:, b, :]).then_inc(x_row_ready, 1)

                def back(b):
                    pool.wait_ge(var_ready, b + 1)
                    nc.gpsimd.tensor_tensor(out=rstd[:, :], in0=var_eps[:, :], in1=minus_half[0:SEQ, :],
                                            op=ALU.pow).then_inc(rstd_ready, 1)

                for p in range(AHEAD):
                    front(p, p)
                back(0)
                with pool.Fori(1, BATCH // AHEAD) as j:
                    for p in range(AHEAD):
                        front(AHEAD * j + p, p)
                        back(AHEAD * (j - 1) + p + 1)
                for b in range(BATCH - AHEAD + 1, BATCH):
                    back(b)

            @block.scalar
            def _(act):
                def key_copy(b, p, u):
                    act.wait_ge(turned, TURNS * b + u + 1)
                    if u == 1:
                        after(act, scores_done, b - 1 if not isinstance(b, int) or b >= 1 else 0)
                    k, c = (u - 1) // CHUNKS, (u - 1) % CHUNKS
                    at, width = chunk_columns(c)
                    nc.scalar.activation(keys_t[p % 2][:, k, at:at + width], turn_bank(p, u)[:, 0:width],
                                         ACT.Copy).then_inc(copied_act, 1)

                def exponentials(b):
                    act.wait_ge(max_ready, b + 1)
                    after(act, probs_turned, CHUNKS * b)
                    body = 2 * FOUR * TILE
                    nc.scalar.activation(probs[:, 0:body].rearrange("q (c k) -> q c k", c=2),
                                         score_ps[0:SEQ, 0:2, 0:FOUR * TILE], ACT.Exp, bias=neg_max[:, 0:1],
                                         scale=SCALE, accum_out=part_sum[:, 0:1])
                    nc.scalar.activation(probs[:, body:CTX], score_ps[0:SEQ, 2, 0:CTX - body], ACT.Exp,
                                         bias=neg_max[:, 0:1], scale=SCALE,
                                         accum_out=part_sum[:, 1:2]).then_inc(probs_ready, 1)

                def probs_copy(b, p, c):
                    act.wait_ge(probs_turned, CHUNKS * b + c + 1)
                    if c == 0:
                        after(act, attended, b)
                    bank = probs_ps[:, (CHUNKS * p + c) % 2, :]
                    full = FOUR if c < CHUNKS - 1 else FOUR - 1
                    last = nc.scalar.activation(probs_t[0:TILE, FOUR * c:FOUR * c + full, :],
                                                bank[0:TILE, 0:full * SEQ].rearrange("k (t q) -> k t q", t=full), ACT.Copy)
                    if full < FOUR:
                        last = nc.scalar.activation(probs_t[0:LAST, TILES - 1, :], bank[0:LAST, full * SEQ:FOUR * SEQ],
                                                    ACT.Copy)
                    last.then_inc(probs_copied, 1)

                def step(b, p):
                    for u in range(1, TURNS, 2):
                        key_copy(b, p, u)
                    for c in range(CHUNKS):
                        probs_copy(b - 1, (p - 1) % AHEAD, c)
                    exponentials(b)

                for u in range(1, TURNS, 2):
                    key_copy(0, 0, u)
                exponentials(0)
                for p in range(1, AHEAD):
                    step(p, p)
                with act.Fori(1, BATCH // AHEAD) as j:
                    for p in range(AHEAD):
                        step(AHEAD * j + p, p)
                for c in range(CHUNKS):
                    probs_copy(BATCH - 1, AHEAD - 1, c)

            @block.tensor
            def _(pe):
                pe.wait_ge(ones_ready, 1)

                def turn(b, p, j, u):
                    if u == 0:
                        pe.wait_ge(x_row_ready, b + 1)
                    if u == 1:
                        pe.wait_ge(keys_in[p], 32 * (j + 1))
                    previous_copied(pe, b, u)
                    bank = turn_bank(p, u)
                    if u == 0:
                        for k in range(KD):
                            last = nc.tensor.transpose(bank[:, k * SEQ:(k + 1) * SEQ],
                                                       x_row[p][:, k * 128:(k + 1) * 128], ident[0:SEQ, 0:SEQ])
                    else:
                        k, c = (u - 1) // CHUNKS, (u - 1) % CHUNKS
                        for n in range(FOUR):
                            t = FOUR * c + n
                            rows = tile_rows(t)
                            last = nc.tensor.transpose(bank[:, n * TILE:n * TILE + rows],
                                                       keys[p][0:rows, t, k * 128:(k + 1) * 128], ident[0:rows, 0:rows])
                    last.then_inc(turned, 1)

                def scores(b, p):
                    pe.wait_ge(mask_ready, b + 1)
                    pe.wait_ge(copied_dve, DVE_TURNS * (b + 1))
                    pe.wait_ge(copied_act, ACT_TURNS * (b + 1))
                    after(pe, probs_ready, b)
                    for c in range(CHUNKS):
                        at, width = chunk_columns(c)
                        nc.tensor.matmul(score_ps[0:SEQ, c, 0:width], ones_row[:, :], mask_bias[p % 2][:, at:at + width],
                                         start=True, stop=False)
                        for k in range(KD):
                            last = nc.tensor.matmul(score_ps[0:SEQ, c, 0:width], x_t[:, k, :],
                                                    keys_t[p % 2][:, k, at:at + width], start=False, stop=(k == KD - 1))
                    last.then_inc(scores_done, 1)

                def turn_probs(b, p, c):
                    if c == 0:
                        pe.wait_ge(probs_ready, b + 1)
                    after(pe, probs_copied, CHUNKS * b + c - 1 if not isinstance(b, int) or CHUNKS * b + c >= 1 else 0)
                    bank = probs_ps[:, (CHUNKS * p + c) % 2, :]
                    for n in range(FOUR):
                        t = FOUR * c + n
                        rows = tile_rows(t)
                        last = nc.tensor.transpose(bank[0:rows, n * SEQ:(n + 1) * SEQ],
                                                   probs[:, t * TILE:t * TILE + rows], ident[0:SEQ, 0:SEQ])
                    last.then_inc(probs_turned, 1)

                def attend(b, p):
                    pe.wait_ge(probs_copied, CHUNKS * (b + 1))
                    after(pe, summed_done, b)
                    for t in range(TILES):
                        rows = tile_rows(t)
                        last = nc.tensor.matmul(out_ps[0:SEQ, 0:DIM], probs_t[0:rows, t, :], keys[p][0:rows, t, :],
                                                start=(t == 0), stop=(t == TILES - 1))
                    last.then_inc(attended, 1)

                def step(b, p, j):
                    for u in range(TURNS):
                        turn(b, p, j, u)
                    for c in range(CHUNKS):
                        turn_probs(b - 1, (p - 1) % AHEAD, c)
                    scores(b, p)
                    attend(b - 1, (p - 1) % AHEAD)

                for u in range(TURNS):
                    turn(0, 0, 0, u)
                scores(0, 0)
                for p in range(1, AHEAD):
                    step(p, p, 0)
                with pe.Fori(1, BATCH // AHEAD) as j:
                    for p in range(AHEAD):
                        step(AHEAD * j + p, p, j)
                for c in range(CHUNKS):
                    turn_probs(BATCH - 1, AHEAD - 1, c)
                attend(BATCH - 1, AHEAD - 1)

            @block.vector
            def _(dve):
                chain = Chain(dve, dve_chain_sem)
                FRONT_LINKS, BACK_LINKS = 2, 4

                def turn_copy(b, p, u):
                    dve.wait_ge(turned, TURNS * b + u + 1)
                    if u <= 2:
                        after(dve, scores_done, b)
                    bank = turn_bank(p, u)
                    if u == 0:
                        last = nc.vector.tensor_copy(x_t[:, :, :], bank[:, 0:KD * SEQ].rearrange("p (k s) -> p k s", k=KD))
                    else:
                        k, c = (u - 1) // CHUNKS, (u - 1) % CHUNKS
                        at, width = chunk_columns(c)
                        last = nc.vector.tensor_copy(keys_t[p % 2][:, k, at:at + width], bank[:, 0:width])
                    last.then_inc(copied_dve, 1)

                def hide(b, p, j):
                    dve.wait_ge(mask_in[p], 16 * (j + 1))
                    after(dve, scores_done, b - 1 if not isinstance(b, int) or b >= 1 else 0)
                    flags = mask_row[p][:, :].bitcast(U8)
                    body = (TILES - 1) * TILE
                    nc.vector.tensor_scalar(
                        mask_bias[p % 2][:, 0:body].rearrange("o (t p) -> o p t", p=TILE),
                        flags[:, 0:body].rearrange("o (p t) -> o p t", p=TILE), -HIDDEN, HIDDEN, ALU.mult, ALU.add)
                    nc.vector.tensor_scalar(mask_bias[p % 2][:, body:CTX], flags[:, body:CTX], -HIDDEN, HIDDEN,
                                            ALU.mult, ALU.add).then_inc(mask_ready, 1)

                def maximum(b):
                    dve.wait_ge(scores_done, b + 1)
                    after(dve, probs_ready, b)
                    nc.vector.tensor_reduce(part_max[:, 0:1], score_ps[0:SEQ, 0:2, 0:FOUR * TILE], AX.XY, ALU.max)
                    chain(nc.vector.tensor_reduce(part_max[:, 1:2], score_ps[0:SEQ, 2, 0:CTX - 2 * FOUR * TILE], AX.X, ALU.max))
                    chain(nc.vector.tensor_tensor(out=row_max[:, :], in0=part_max[:, 0:1], in1=part_max[:, 1:2], op=ALU.max))
                    nc.vector.tensor_scalar(neg_max[:, :], row_max[:, :], -SCALE, None, ALU.mult).then_inc(max_ready, 1)

                def sums(b):
                    dve.wait_ge(probs_ready, b + 1)
                    nc.vector.tensor_scalar(any_key[:, :], row_max[:, :], HIDDEN / 2, None, ALU.is_gt)
                    chain(nc.vector.tensor_tensor(out=inv_sum[:, :], in0=part_sum[:, 0:1], in1=part_sum[:, 1:2], op=ALU.add))
                    chain(nc.vector.reciprocal(inv_sum[:, :], inv_sum[:, :]))
                    chain(nc.vector.tensor_tensor(out=factor[:, :], in0=inv_sum[:, :], in1=any_key[:, :], op=ALU.mult))

                def residual_norm(b, p):
                    dve.wait_ge(attended, b + 1)
                    after(dve, x_new, b)
                    nc.vector.scalar_tensor_tensor(out=summed[:, :], in0=out_ps[0:SEQ, 0:DIM], scalar=factor[:, 0:1],
                                                   in1=x_row[p][:, :], op0=ALU.mult, op1=ALU.add).then_inc(summed_done, 1)
                    dve.wait_ge(summed_done, b + 1)
                    nc.vector.bn_stats(stats[:, :], summed[:, :])
                    dve.drain()
                    chain(nc.vector.bn_aggr(mean_var[:, :], stats[:, :]))
                    nc.vector.tensor_scalar_add(var_eps[:, :], mean_var[:, 1:2], LN_EPS).then_inc(var_ready, 1)

                def scale_rows(b):
                    dve.wait_ge(rstd_ready, b + 1)
                    nc.vector.tensor_scalar(x_tokens[:, b, :], summed[:, :], mean_var[:, 0:1], rstd[:, 0:1],
                                            ALU.subtract, ALU.mult).then_inc(x_new, 1)

                def step(b, p, j):
                    chain.begin(FRONT_LINKS + (b - 1) * (FRONT_LINKS + BACK_LINKS))
                    turn_copy(b, p, 0)
                    if not isinstance(b, int) or b >= 2:
                        scale_rows(b - 2)
                    sums(b - 1)
                    for u in range(2, TURNS, 2):
                        turn_copy(b, p, u)
                    hide(b, p, j)
                    maximum(b)
                    residual_norm(b - 1, (p - 1) % AHEAD)
                    assert chain.n == FRONT_LINKS + BACK_LINKS

                chain.begin(0)
                for u in range(0, TURNS, 2):
                    turn_copy(0, 0, u)
                hide(0, 0, 0)
                maximum(0)
                for p in range(1, AHEAD):
                    step(p, p, 0)
                with dve.Fori(1, BATCH // AHEAD) as j:
                    for p in range(AHEAD):
                        step(AHEAD * j + p, p, j)
                chain.begin(FRONT_LINKS + (BATCH - 1) * (FRONT_LINKS + BACK_LINKS))
                sums(BATCH - 1)
                scale_rows(BATCH - 2)
                residual_norm(BATCH - 1, AHEAD - 1)
                scale_rows(BATCH - 1)
                dve.wait_ge(x_new, BATCH)


def cross_attention_pass(nc, x_in_dram, ctx, x_out_dram, ident):
    PARTS_Q = (0, 0, 0, 1, 1, 2)
    PARTS_K = (0, 1, 2, 0, 1, 0)
    STACK = len(PARTS_Q) * HD
    ROWS = STACK + 3
    SCALE = float(HD) ** -0.5
    HIDDEN_SCORE = -10000.0
    REACH = CTX - SEQ - (TILES - 1) * TILE
    FOUR_Q = FOUR * SEQ
    VALUE = HD + 1
    KEY_UNITS = KD * CHUNKS
    HH = HEADS // 2
    MAX_CHUNK = 482
    HIDES_AT = (TILES - 1) * TILE - (CHUNKS - 1) * MAX_CHUNK
    NEG_ROW = STACK
    FULL = 128
    KEY_COLUMNS = (TILES - 1) * TILE + FULL
    OUT_ROWS = 32
    VALUE_COLUMNS = HEADS * VALUE + OUT_ROWS - VALUE
    LAST_ROW = BATCH - 1
    UNITS = (("key", 0, 0), ("out", 1, 0), ("neg", 3, 1), ("query", 4, 1), ("key", 5, 1), ("key", 6, 2), ("key", 7, 3),
             ("key", 8, 4), ("key", 9, 5), ("hidden", 10, 0), ("query", 11, 0), ("neg", 12, 0))
    OPENING = KEY_UNITS + 1

    def unit_plan(b):
        kept = UNITS
        if isinstance(b, int) and b < 2:
            kept = [x for x in kept if x[0] != "out" and (b > 0 or x != ("neg", 3, 1))]
        if isinstance(b, int) and b == LAST_ROW:
            kept = [x for x in kept if x[0] in ("out", "hidden", "neg") or x == ("query", 4, 1)]
        return [(kind, s, n, at) for at, (kind, s, n) in enumerate(kept)]

    def units_of(b):
        return len(unit_plan(b))

    parts_dram = nc.dram_tensor("key_parts", (2, KD, 3, 128, CTX), BF16, kind="Internal").ap()
    with ExitStack() as stack:
        mem = Memory(nc, stack, "cross")
        keys = [mem.sbuf(f"keys{p}", [LAST, TILES, DIM]) for p in range(2)]
        values = [mem.sbuf(f"values{p}", [LAST, TILES, VALUE_COLUMNS]) for p in range(2)]
        parts = mem.sbuf("parts", [128, 3, KD, CTX], BF16)
        rest = mem.sbuf("rest", [128, 2, FOUR * TILE + LAST - TILE])
        key_op = [mem.sbuf(f"key_op{p}", [ROWS, HEADS, KEY_COLUMNS], BF16) for p in range(2)]
        query_op = [mem.sbuf(f"query_op{p}", [ROWS, HEADS, SEQ], BF16) for p in range(2)]
        x_q = mem.sbuf("x_q", [SEQ, DIM])
        x_rest = mem.sbuf("x_rest", [SEQ, DIM])
        q_parts = mem.sbuf("q_parts", [SEQ, HEADS, len(PARTS_Q), HD], BF16)
        part_max = mem.sbuf("part_max", [SEQ, HEADS, 2])
        row_max = mem.sbuf("row_max", [SEQ, HEADS])
        neg_max = mem.sbuf("neg_max", [SEQ, HEADS])
        neg_rest = mem.sbuf("neg_rest", [SEQ, HEADS])
        neg_parts = mem.sbuf("neg_parts", [SEQ, HEADS, 3], BF16)
        hidden_arg = mem.sbuf("hidden_arg", [SEQ, HEADS])
        hidden_prob = [mem.sbuf(f"hidden_prob{p}", [SEQ, HEADS]) for p in range(2)]
        hidden_sum = [mem.sbuf(f"hidden_sum{p}", [SEQ, HEADS, VALUE]) for p in range(2)]
        probs = mem.sbuf("probs", [LAST, 2, CHUNKS, FOUR_Q])
        out_t = mem.sbuf("out_t", [128, FOUR_Q])
        weighted = mem.sbuf("weighted", [SEQ, HEADS, VALUE])
        inv_sum = mem.sbuf("inv_sum", [SEQ, HEADS])
        attn = mem.sbuf("attn", [SEQ, DIM])
        x_res = mem.sbuf("x_res", [SEQ, DIM])
        stats = mem.sbuf("stats", [SEQ, 6])
        mean_var = mem.sbuf("mean_var", [SEQ, 2])
        var_eps = mem.sbuf("var_eps", [SEQ, 1])
        rstd = mem.sbuf("rstd", [SEQ, 1])
        result = mem.sbuf("result", [SEQ, DIM])
        ident_bf = mem.sbuf("ident_bf", [128, 128], BF16)
        hides = mem.sbuf("hides", [LAST, SEQ])
        hides_bf = mem.sbuf("hides_bf", [LAST, SEQ], BF16)
        hides_q = mem.sbuf("hides_q", [SEQ, MAX_CHUNK - HIDES_AT], BF16)
        floor = mem.sbuf("floor", [SEQ, 1])
        minus_half = mem.sbuf("minus_half", [SEQ, 1])
        zeros = mem.sbuf("zeros", [128, 1])
        ones = mem.sbuf("ones", [ROWS - STACK, CTX], BF16)

        max_ps = mem.psum("max_ps", [128, CHUNKS, BANK])
        prob_ps = mem.psum("prob_ps", [128, CHUNKS, BANK])
        turn_ps = mem.psum("turn_ps", [128, BANK])
        out_ps = mem.psum("out_ps", [128, BANK])

        keys_in = [mem.sem(f"keys_in{p}") for p in range(2)]
        stacked = [[mem.sem(f"stacked{p}{k}") for k in range(KD)] for p in range(2)]
        written = [[mem.sem(f"written{p}{k}") for k in range(KD)] for p in range(2)]
        x_q_in, x_res_in, x_out = mem.sem("x_q_in"), mem.sem("x_res_in"), mem.sem("x_out")
        consts_ready, dve_chain_sem, pool_chain_sem = mem.sem("consts_ready"), mem.sem("dve_order"), mem.sem("pool_order")
        ones_ready, ones_in = mem.sem("ones_ready"), mem.sem("ones_in")
        key_turned, query_turned = mem.sem("key_turned"), mem.sem("query_turned")
        hidden_turned, neg_turned = mem.sem("hidden_turned"), mem.sem("neg_turned")
        turn_free = mem.sem("turn_free")
        hi_ready, low_ready, q_parts_ready, values_ready = (mem.sem("hi_ready"), mem.sem("low_ready"),
                                                            mem.sem("q_parts_ready"), mem.sem("values_ready"))
        max_scores, max_taken = mem.sem("max_scores"), mem.sem("max_taken")
        third_scores, third_taken = mem.sem("third_scores"), mem.sem("third_taken")
        neg_parts_ready, arg_ready, hidden_ready = (mem.sem("neg_parts_ready"),
                                                                   mem.sem("arg_ready"), mem.sem("hidden_ready"))
        prob_scores, probs_ready, applied = mem.sem("prob_scores"), mem.sem("probs_ready"), mem.sem("applied")
        out_copied, out_turned = mem.sem("out_copied"), mem.sem("out_turned")
        var_ready, rstd_ready, finished = (mem.sem("var_ready"), mem.sem("rstd_ready"),
                                                    mem.sem("finished"))
        CONSTS = 5

        def number(x):
            return isinstance(x, int)

        def rows_before(n, back):
            return max(n - back, 0) if number(n) else n - back

        def first_unit(b):
            if number(b) and b < 2:
                return OPENING + units_of(0) * b
            return OPENING + units_of(0) + units_of(1) + len(UNITS) * (b - 2)

        def units_to(b, unit):
            if number(b) and b == BATCH:
                return first_unit(LAST_ROW) + units_of(LAST_ROW) + 2
            return first_unit(b) + 1 + [x[0:3] for x in unit_plan(b)].index(unit)

        def head_values(p):
            return values[p][:, :, 0:HEADS * VALUE].rearrange("k t (h e) -> k t h e", h=HEADS)

        with nc.Block() as block:

            @block.sync
            def _(sp):
                def load_keys(n, p):
                    if number(n) and n >= 2:
                        sp.wait_ge(key_turned, KEY_UNITS * (n - 1))
                    after(sp, values_ready, rows_before(n, 1))
                    load_context(sp, keys[p], ctx[n], keys_in[p])

                def load_queries(n):
                    after(sp, q_parts_ready, n)
                    sp.dma_start(x_q[:, :], x_in_dram[n]).then_inc(x_q_in, 16)

                def load_residual(n):
                    after(sp, finished, n)
                    sp.dma_start(x_res[:, :], x_in_dram[n]).then_inc(x_res_in, 16)

                def write_parts(n, p, k):
                    sp.wait_ge(low_ready, KEY_UNITS * n + CHUNKS * (k + 1))
                    sp.dma_start(parts_dram[p, k].rearrange("j r c -> r j c"), parts[:, :, k, :]).then_inc(written[p][k], 16)

                def stack_keys(n, p, j, k):
                    in_dram = 16 * (j + 1)
                    if not number(n) or n >= 2:
                        used = HEADS * (n - 2) + HH * (k + 1)
                        sp.wait_ge(prob_scores, used)
                        sp.nop()
                    sp.wait_ge(written[p][k], in_dram)
                    for block_row, part in enumerate(PARTS_K):
                        sp.dma_start(key_op[p][HD * block_row:HD * (block_row + 1), HH * k:HH * (k + 1), 0:CTX],
                                     parts_dram[p, k, part].rearrange("(h r) c -> r h c", r=HD)).then_inc(stacked[p][k], 16)

                def store(b):
                    sp.wait_ge(finished, b + 1)
                    sp.dma_start(x_out_dram[b], result[:, :]).then_inc(x_out, 16)

                def step(b, p, j):
                    prepare = not number(b) or b < LAST_ROW
                    if not number(b) or b >= 2:
                        store(b - 2)
                    if not number(b) or b >= 1:
                        load_residual(b - 1)
                    if prepare:
                        load_queries(b + 1)
                    if not number(b) or b + 2 <= LAST_ROW:
                        load_keys(b + 2, p)
                    if prepare:
                        write_parts(b + 1, 1 - p, 0)
                        write_parts(b + 1, 1 - p, 1)
                        stack_keys(b + 1, 1 - p, j + p, 0)
                    if prepare:
                        stack_keys(b + 1, 1 - p, j + p, 1)

                load_keys(0, 0)
                load_queries(0)
                load_keys(1, 1)
                sp.wait_ge(ones_ready, 1)
                for p in range(2):
                    sp.dma_start(key_op[p][STACK:ROWS, :, 0:CTX],
                                 ones[:, :].unsqueeze(1).to_broadcast([ROWS - STACK, HEADS, CTX])).then_inc(ones_in, 16)
                for k in range(KD):
                    write_parts(0, 0, k)
                    stack_keys(0, 0, 0, k)
                step(0, 0, 0)
                step(1, 1, 0)
                with sp.Fori(1, BATCH // 2 - 1) as j:
                    step(2 * j, 0, j)
                    step(2 * j + 1, 1, j)
                step(BATCH - 2, 0, BATCH // 2 - 1)
                step(LAST_ROW, 1, BATCH // 2 - 1)
                store(LAST_ROW - 1)
                load_residual(LAST_ROW)
                store(LAST_ROW)
                sp.wait_ge(x_out, 16 * BATCH)

            @block.gpsimd
            def _(pool):
                chain = Chain(pool, pool_chain_sem)
                nc.gpsimd.memset(minus_half[:, :], -0.5).then_inc(consts_ready, 1)
                nc.gpsimd.tensor_copy(ident_bf[:, :], ident[:, :]).then_inc(consts_ready, 1)
                nc.gpsimd.memset(ones[:, :], 1.0).then_inc(ones_ready, 1)
                chain(nc.gpsimd.memset(hides[:, :], 0.0))
                chain(nc.gpsimd.affine_select(out=hides[:, :], in_=hides[:, :], compare_op=ALU.is_ge, fill=1.0, base=REACH,
                                              pattern=[[1, SEQ]], channel_multiplier=-1))
                nc.gpsimd.tensor_scalar(hides_bf[:, :], hides[:, :], NEG, None, ALU.mult).then_inc(consts_ready, 1)
                chain(nc.gpsimd.memset(hides_q[:, :], 0.0))
                chain(nc.gpsimd.affine_select(out=hides_q[:, :], in_=hides_q[:, :], compare_op=ALU.is_ge, fill=NEG, base=REACH,
                                              pattern=[[-1, MAX_CHUNK - HIDES_AT]], channel_multiplier=1))
                chain(nc.gpsimd.memset(floor[:, :], HIDDEN_SCORE / SCALE))
                nc.gpsimd.affine_select(out=floor[:, :], in_=floor[:, :], compare_op=ALU.is_ge, fill=NEG, base=SEQ - 2,
                                        pattern=[[0, 1]], channel_multiplier=-1).then_inc(consts_ready, 1)
                for p in range(2):
                    chain(nc.gpsimd.memset(values[p][:, :, :], 1.0))
                    chain(nc.gpsimd.memset(key_op[p][:, :, CTX:KEY_COLUMNS], 1.0))
                nc.gpsimd.memset(zeros[:, :], 0.0).then_inc(consts_ready, 1)
                pool.wait_ge(consts_ready, CONSTS)
                OPENING_LINKS = chain.n

                def plain(out, in_):
                    nothing = zeros[0:out.shape[0], 0:1]
                    for _ in range(len(out.shape) - 2):
                        nothing = nothing.unsqueeze(2)
                    return nc.gpsimd.tensor_tensor(out=out, in0=in_, in1=nothing.to_broadcast(list(out.shape)), op=ALU.add)

                def copy_values(b, p, j):
                    pool.wait_ge(keys_in[p], 32 * (j + 1))
                    after(pool, applied, HEADS * rows_before(b, 1))
                    plain(head_values(p)[0:TILE, 0:TILES - 1, :, 0:HD],
                          keys[p][0:TILE, 0:TILES - 1, :].rearrange("k t (h e) -> k t h e", h=HEADS))
                    plain(head_values(p)[:, TILES - 1, :, 0:HD],
                          keys[p][:, TILES - 1, :].rearrange("k (h e) -> k h e", h=HEADS)).then_inc(values_ready, 1)

                def low_parts(n, u, before):
                    k, c = u // CHUNKS, u % CHUNKS
                    at, width = chunk_columns(c)
                    pool.wait_ge(turn_free, before + 1)
                    chain(plain(parts[:, 1, k, at:at + width], rest[:, u % 2, 0:width]))
                    nc.gpsimd.tensor_tensor(out=parts[:, 2, k, at:at + width], in0=rest[:, u % 2, 0:width],
                                            in1=parts[:, 1, k, at:at + width], op=ALU.subtract).then_inc(low_ready, 1)

                def split_queries(n):
                    pool.wait_ge(x_q_in, 16 * (n + 1))
                    after(pool, query_turned, 2 * n)
                    xh = x_q[:, :].rearrange("q (h e) -> q h e", h=HEADS)
                    rh = x_rest[:, :].rearrange("q (h e) -> q h e", h=HEADS)
                    thrice = [SEQ, HEADS, 3, HD]
                    chain(plain(q_parts[:, :, 0:3, :], xh.unsqueeze(2).to_broadcast(thrice)))
                    chain(nc.gpsimd.tensor_tensor(out=rh, in0=xh, in1=q_parts[:, :, 0, :], op=ALU.subtract))
                    twice = [SEQ, HEADS, 2, HD]
                    chain(plain(q_parts[:, :, 3:5, :], rh.unsqueeze(2).to_broadcast(twice)))
                    nc.gpsimd.tensor_tensor(out=q_parts[:, :, 5, :], in0=rh, in1=q_parts[:, :, 3, :],
                                            op=ALU.subtract).then_inc(q_parts_ready, 1)

                def power(b):
                    pool.wait_ge(var_ready, b + 1)
                    nc.gpsimd.tensor_tensor(out=rstd[:, :], in0=var_eps[:, :], in1=minus_half[:, :],
                                            op=ALU.pow).then_inc(rstd_ready, 1)

                def step(b, p, j):
                    copy_values(b, p, j)
                    if not number(b) or b >= 2:
                        power(b - 2)
                    for kind, s, n, at in unit_plan(b):
                        if kind == "key":
                            low_parts(b + 1, n, first_unit(b) + at)
                        if kind == "key" and n == 1:
                            split_queries(b + 1)

                STEP_LINKS = KEY_UNITS + 3
                chain.begin(OPENING_LINKS)
                for u in range(KEY_UNITS):
                    low_parts(0, u, u)
                split_queries(0)
                opened = chain.n + OPENING_LINKS

                def numbered(b, p, j):
                    chain.begin(opened + STEP_LINKS * b)
                    step(b, p, j)
                    assert chain.n == (0 if number(b) and b == LAST_ROW else STEP_LINKS)

                numbered(0, 0, 0)
                numbered(1, 1, 0)
                with pool.Fori(1, BATCH // 2 - 1) as j:
                    numbered(2 * j, 0, j)
                    numbered(2 * j + 1, 1, j)
                numbered(BATCH - 2, 0, BATCH // 2 - 1)
                numbered(LAST_ROW, 1, BATCH // 2 - 1)
                power(LAST_ROW - 1)
                power(LAST_ROW)

            @block.scalar
            def _(act):
                act.wait_ge(consts_ready, CONSTS)

                def hi_part(n, p, j, u):
                    k, c = u // CHUNKS, u % CHUNKS
                    at, width = chunk_columns(c)
                    act.wait_ge(key_turned, KEY_UNITS * n + u + 1)
                    if c == 0:
                        after(act, written[1 - p][k], 16 * (j + p))
                    nc.scalar.activation(parts[:, 0, k, at:at + width], turn_ps[:, 0:width], ACT.Copy).then_inc(hi_ready, 1)

                def query_copy(n, p, half):
                    act.wait_ge(query_turned, 2 * n + half + 1)
                    if not number(n) or n >= 2:
                        act.wait_ge(prob_scores, HEADS * (n - 2) + HH * (half + 1))
                    nc.scalar.activation(query_op[p][0:STACK, HH * half:HH * (half + 1), :],
                                          turn_ps[:, :].bitcast(BF16)[0:STACK, 0:HH * SEQ]
                                          .rearrange("r (h q) -> r h q", h=HH), ACT.Copy).then_inc(turn_free, 1)

                def neg_copy(r, p, half):
                    act.wait_ge(neg_turned, 2 * r + half + 1)
                    at = slice(HH * half, HH * (half + 1))
                    nc.scalar.activation(query_op[p][NEG_ROW:ROWS, at, :],
                                          turn_ps[:, :].bitcast(BF16)[NEG_ROW:ROWS, 0:HH * SEQ]
                                          .rearrange("r (h q) -> r h q", h=HH), ACT.Copy).then_inc(turn_free, 1)

                def hidden_values(b, p):
                    act.wait_ge(hidden_turned, b + 1)
                    after(act, finished, rows_before(b, 1))
                    nc.scalar.activation(hidden_sum[p][:, :, :],
                                         turn_ps[0:SEQ, 0:HEADS * VALUE].rearrange("q (h e) -> q h e", h=HEADS),
                                         ACT.Copy).then_inc(turn_free, 1)

                def hidden_probability(b, p):
                    act.wait_ge(arg_ready, b + 1)
                    after(act, finished, rows_before(b, 1))
                    nc.scalar.activation(hidden_prob[p][:, :], hidden_arg[:, :], ACT.Exp).then_inc(hidden_ready, 1)

                def exponentials(r, h):
                    act.wait_ge(prob_scores, HEADS * r + h + 1)
                    if h >= 2:
                        act.wait_ge(applied, HEADS * r + h - 1)
                    else:
                        after(act, applied, HEADS * r + h - 1 if not number(r) or r >= 1 else 0)
                    nc.scalar.activation(probs[:, h % 2, :, :], prob_ps[0:LAST, :, 0:FOUR_Q], ACT.Exp,
                                         scale=SCALE).then_inc(probs_ready, 1)

                def copy_out(r):
                    act.wait_ge(applied, HEADS * (r + 1))
                    after(act, out_turned, r)
                    nc.scalar.activation(out_t[:, :], out_ps[:, 0:FOUR_Q], ACT.Copy).then_inc(out_copied, 1)

                def step(b, p, j):
                    plan = {s: (kind, n) for kind, s, n, _ in unit_plan(b)}
                    if not number(b) or b >= 2:
                        copy_out(b - 2)
                    for s in range(HEADS):
                        if not number(b) or b >= 1:
                            exponentials(b - 1, s)
                        kind, n = plan.get(s, (None, 0))
                        if kind == "key":
                            hi_part(b + 1, 1 - p, j + p, n)
                        if kind == "hidden":
                            hidden_values(b, p)
                        if kind == "query":
                            query_copy(b if n == 1 else b + 1, p if n == 1 else 1 - p, n)
                        if kind == "neg":
                            neg_copy(b - n, 1 - p if n == 1 else p, n)
                        if s == 4 and (not number(b) or b >= 1):
                            hidden_probability(b - 1, 1 - p)

                for u in range(KEY_UNITS):
                    hi_part(0, 0, 0, u)
                query_copy(0, 0, 0)
                step(0, 0, 0)
                step(1, 1, 0)
                with act.Fori(1, BATCH // 2 - 1) as j:
                    step(2 * j, 0, j)
                    step(2 * j + 1, 1, j)
                step(BATCH - 2, 0, BATCH // 2 - 1)
                step(LAST_ROW, 1, BATCH // 2 - 1)
                copy_out(LAST_ROW - 1)
                for h in range(HEADS):
                    exponentials(LAST_ROW, h)
                    if h == 2:
                        hidden_probability(LAST_ROW, 1)
                        neg_copy(LAST_ROW, 1, 1)
                copy_out(LAST_ROW)

            @block.tensor
            def _(pe):
                pe.wait_ge(consts_ready, CONSTS)

                def turn_keys(n, p, j, u, before):
                    k, c = u // CHUNKS, u % CHUNKS
                    if u == 0:
                        pe.wait_ge(keys_in[p], 32 * (j + 1))
                    after(pe, turn_free, before)
                    for i in range(FOUR):
                        t = FOUR * c + i
                        rows = tile_rows(t)
                        last = nc.tensor.transpose(turn_ps[:, i * TILE:i * TILE + rows],
                                                   keys[p][0:rows, t, k * 128:(k + 1) * 128], ident[0:rows, 0:rows])
                    last.then_inc(key_turned, 1)

                def turn_queries(n, half, before):
                    pe.wait_ge(q_parts_ready, n + 1)
                    pe.wait_ge(turn_free, before)
                    bank = turn_ps[:, :].bitcast(BF16)
                    for i in range(HH):
                        last = nc.tensor.transpose(bank[0:STACK, i * SEQ:(i + 1) * SEQ],
                                                   q_parts[:, HH * half + i, :, :].rearrange("q c e -> q (c e)"),
                                                   ident_bf[0:SEQ, 0:SEQ])
                    last.then_inc(query_turned, 1)

                def sum_hidden(b, p, before):
                    pe.wait_ge(values_ready, b + 1)
                    pe.wait_ge(turn_free, before)
                    nc.tensor.matmul(turn_ps[0:SEQ, 0:HEADS * VALUE], hides[:, :],
                                     values[p][:, TILES - 1, 0:HEADS * VALUE],
                                     start=True, stop=True).then_inc(hidden_turned, 1)

                def turn_neg(r, half, before):
                    pe.wait_ge(neg_parts_ready, 2 * r + half + 1)
                    pe.wait_ge(turn_free, before)
                    bank = turn_ps[:, :].bitcast(BF16)
                    for i in range(HH):
                        last = nc.tensor.transpose(bank[NEG_ROW:ROWS, i * SEQ:(i + 1) * SEQ],
                                                   neg_parts[:, HH * half + i, :], ident_bf[0:SEQ, 0:SEQ])
                    last.then_inc(neg_turned, 1)

                def head_scores(p, h):
                    for t in range(TILES):
                        target = prob_ps[0:FULL, t // FOUR, (t % FOUR) * SEQ:(t % FOUR + 1) * SEQ]
                        if t == TILES - 1:
                            nc.tensor.matmul(target, ident_bf[0:LAST, 0:FULL], hides_bf[:, :], start=True, stop=False)
                        last = nc.tensor.matmul(target, key_op[p][:, h, t * TILE:t * TILE + FULL],
                                                query_op[p][:, h, :], start=(t < TILES - 1), stop=True)
                    return last

                def scores_for_max(b, p, j, h):
                    if h % HH == 0:
                        pe.wait_ge(stacked[p][h // HH], 16 * len(PARTS_K) * (j + 1))
                        if h == 0:
                            pe.wait_ge(turn_free, OPENING if number(b) and b == 0 else units_to(b - 1, ("query", 11, 0)))
                        else:
                            pe.wait_ge(turn_free, units_to(b, ("query", 4, 1)))
                    after(pe, max_taken, HEADS * b + h)
                    for c in range(CHUNKS):
                        if c == CHUNKS - 1:
                            last.then_inc(max_scores, 1)
                            after(pe, third_taken, HEADS * b + h)
                        last = nc.tensor.matmul(max_ps[0:SEQ, c, 0:MAX_CHUNK], query_op[p][0:STACK, h, :],
                                                key_op[p][0:STACK, h, c * MAX_CHUNK:(c + 1) * MAX_CHUNK],
                                                start=True, stop=(c < CHUNKS - 1))
                    nc.tensor.matmul(max_ps[0:SEQ, CHUNKS - 1, HIDES_AT:MAX_CHUNK], ident_bf[0:SEQ, 0:SEQ], hides_q[:, :],
                                     start=False, stop=True).then_inc(third_scores, 1)

                def turn_out(r, before):
                    pe.wait_ge(out_copied, r + 1)
                    pe.wait_ge(turn_free, before)
                    for g in range(FOUR):
                        last = nc.tensor.transpose(turn_ps[0:SEQ, g * 128:(g + 1) * 128], out_t[:, g * SEQ:(g + 1) * SEQ],
                                                   ident[:, :])
                    last.then_inc(out_turned, 1)

                def scores_for_probs(r, p, j, h):
                    if h == 0:
                        pe.wait_ge(turn_free, units_to(r, ("neg", 12, 0)))
                    if h == HH:
                        pe.wait_ge(turn_free, units_to(r + 1, ("neg", 3, 1)))
                    after(pe, probs_ready, HEADS * r + h)
                    head_scores(p, h).then_inc(prob_scores, 1)

                def apply(r, p, h):
                    pe.wait_ge(probs_ready, HEADS * r + h + 1)
                    if h == 0:
                        after(pe, out_copied, r)
                    g, i = h // FOUR, h % FOUR
                    for t in range(TILES):
                        rows = tile_rows(t)
                        last = nc.tensor.matmul(out_ps[OUT_ROWS * i:OUT_ROWS * (i + 1), SEQ * g:SEQ * (g + 1)],
                                                values[p][0:rows, t, VALUE * h:VALUE * h + OUT_ROWS],
                                                probs[0:rows, h % 2, t // FOUR, (t % FOUR) * SEQ:(t % FOUR + 1) * SEQ],
                                                start=(t == 0), stop=(t == TILES - 1))
                    last.then_inc(applied, 1)

                def step(b, p, j):
                    plan = {s: (kind, n, at) for kind, s, n, at in unit_plan(b)}
                    going = not number(b) or b >= 1
                    for s in range(HEADS):
                        if going:
                            scores_for_probs(b - 1, 1 - p, j - 1 + p, s)
                        scores_for_max(b, p, j, s)
                        kind, n, at = plan.get(s, (None, 0, 0))
                        before = first_unit(b) + at
                        if kind == "key":
                            turn_keys(b + 1, 1 - p, j + p, n, before)
                        if kind == "out":
                            turn_out(b - 2, before)
                        if kind == "query":
                            turn_queries(b if n == 1 else b + 1, n, before)
                        if kind == "hidden":
                            sum_hidden(b, p, before)
                        if kind == "neg":
                            turn_neg(b - n, n, before)
                        if going and s:
                            apply(b - 1, 1 - p, s - 1)
                    if going:
                        apply(b - 1, 1 - p, HEADS - 1)

                for u in range(KEY_UNITS):
                    turn_keys(0, 0, 0, u, u)
                turn_queries(0, 0, KEY_UNITS)
                step(0, 0, 0)
                pe.wait_ge(ones_in, 32)
                step(1, 1, 0)
                with pe.Fori(1, BATCH // 2 - 1) as j:
                    step(2 * j, 0, j)
                    step(2 * j + 1, 1, j)
                step(BATCH - 2, 0, BATCH // 2 - 1)
                step(LAST_ROW, 1, BATCH // 2 - 1)
                units = first_unit(LAST_ROW) + units_of(LAST_ROW)
                for h in range(HEADS):
                    scores_for_probs(LAST_ROW, 1, BATCH // 2 - 1, h)
                    if h == 1:
                        turn_out(LAST_ROW - 1, units)
                    if h == 2:
                        turn_neg(LAST_ROW, 1, units + 1)
                    if h:
                        apply(LAST_ROW, 1, h - 1)
                apply(LAST_ROW, 1, HEADS - 1)
                turn_out(LAST_ROW, units + 2)

            @block.vector
            def _(dve):
                chain = Chain(dve, dve_chain_sem)
                dve.wait_ge(consts_ready, CONSTS)

                def key_rest(n, u, before):
                    width = chunk_columns(u % CHUNKS)[1]
                    dve.wait_ge(hi_ready, KEY_UNITS * n + u + 1)
                    if u >= 2:
                        dve.wait_ge(low_ready, KEY_UNITS * n + u - 1)
                    else:
                        after(dve, low_ready, KEY_UNITS * n + u - 1 if not number(n) or n >= 1 else 0)
                    k, c = u // CHUNKS, u % CHUNKS
                    at = chunk_columns(c)[0]
                    nc.vector.tensor_tensor(out=rest[:, u % 2, 0:width], in0=turn_ps[:, 0:width],
                                            in1=parts[:, 0, k, at:at + width], op=ALU.subtract).then_inc(turn_free, 1)

                def head_max(b, h):
                    dve.wait_ge(max_scores, HEADS * b + h + 1)
                    nc.vector.tensor_reduce(part_max[:, h, 0:1], max_ps[0:SEQ, 0:2, 0:MAX_CHUNK], AX.XY,
                                            ALU.max).then_inc(max_taken, 1)
                    dve.wait_ge(third_scores, HEADS * b + h + 1)
                    nc.vector.tensor_reduce(part_max[:, h, 1:2], max_ps[0:SEQ, 2, 0:MAX_CHUNK], AX.X,
                                            ALU.max).then_inc(third_taken, 1)

                def negate(r, half):
                    dve.wait_ge(third_taken, HEADS * r + HH * (half + 1))
                    if half == 0:
                        after(dve, arg_ready, r)
                    at = slice(HH * half, HH * (half + 1))
                    chain(nc.vector.tensor_tensor(out=row_max[:, at], in0=part_max[:, at, 0], in1=part_max[:, at, 1],
                                                  op=ALU.max))
                    chain(nc.vector.tensor_scalar(neg_max[:, at], row_max[:, at], floor[:, 0:1], -1.0, ALU.max, ALU.mult))
                    chain(nc.vector.tensor_copy(neg_parts[:, at, 0], neg_max[:, at]))
                    chain(nc.vector.tensor_tensor(out=neg_rest[:, at], in0=neg_max[:, at], in1=neg_parts[:, at, 0],
                                                  op=ALU.subtract))
                    chain(nc.vector.tensor_copy(neg_parts[:, at, 1], neg_rest[:, at]))
                    nc.vector.tensor_tensor(out=neg_parts[:, at, 2], in0=neg_rest[:, at], in1=neg_parts[:, at, 1],
                                            op=ALU.subtract).then_inc(neg_parts_ready, 1)

                def hidden_power(r):
                    after(dve, hidden_ready, r)
                    chain(nc.vector.tensor_scalar(hidden_arg[:, :], neg_max[:, :], SCALE, HIDDEN_SCORE, ALU.mult, ALU.add))
                    nc.vector.tensor_scalar(hidden_arg[:, :], hidden_arg[:, :], 0.0, None, ALU.min).then_inc(arg_ready, 1)

                def finish(r, p, before):
                    dve.wait_ge(hidden_ready, r + 1)
                    dve.wait_ge(out_turned, r + 1)
                    three = [SEQ, HEADS, VALUE]
                    chain(nc.vector.tensor_tensor(out=weighted[:, :, :], in0=hidden_sum[p][:, :, :],
                                                  in1=hidden_prob[p][:, :].unsqueeze(2).to_broadcast(three), op=ALU.mult))
                    nc.vector.tensor_tensor(out=weighted[:, :, :], in0=weighted[:, :, :],
                                            in1=turn_ps[0:SEQ, :].rearrange("q (h e) -> q h e", h=HEADS)[:, :, 0:VALUE],
                                            op=ALU.add).then_inc(turn_free, 1)
                    dve.wait_ge(turn_free, before + 1)
                    chain(nc.vector.reciprocal(inv_sum[:, :].unsqueeze(2), weighted[:, :, HD:VALUE]))
                    chain(nc.vector.tensor_tensor(out=attn[:, :].rearrange("q (h e) -> q h e", h=HEADS),
                                                  in0=weighted[:, :, 0:HD],
                                                  in1=inv_sum[:, :].unsqueeze(2).to_broadcast([SEQ, HEADS, HD]), op=ALU.mult))
                    dve.wait_ge(x_res_in, 16 * (r + 1))
                    chain(nc.vector.tensor_tensor(out=attn[:, :], in0=attn[:, :], in1=x_res[:, :], op=ALU.add))
                    nc.vector.bn_stats(stats[:, :], attn[:, :])
                    dve.drain()
                    chain(nc.vector.bn_aggr(mean_var[:, :], stats[:, :]))
                    nc.vector.tensor_scalar_add(var_eps[:, :], mean_var[:, 1:2], LN_EPS).then_inc(var_ready, 1)

                def scale_rows(r):
                    dve.wait_ge(rstd_ready, r + 1)
                    after(dve, x_out, 16 * r)
                    nc.vector.tensor_scalar(result[:, :], attn[:, :], mean_var[:, 0:1], rstd[:, 0:1],
                                            ALU.subtract, ALU.mult).then_inc(finished, 1)

                LINKS = {"first half": 5, "second half": 6, "finish": 5}

                def links_before(b):
                    return (LINKS["first half"] * b + LINKS["second half"] * rows_before(b, 1)
                            + LINKS["finish"] * rows_before(b, 2))

                def step(b, p, j):
                    chain.begin(links_before(b))
                    plan = {s: (kind, n, at) for kind, s, n, at in unit_plan(b)}
                    for s in range(HEADS):
                        head_max(b, s)
                        if s == 2 and (not number(b) or b >= 1):
                            negate(b - 1, 1)
                            hidden_power(b - 1)
                        if s == 3 and (not number(b) or b >= 2):
                            scale_rows(b - 2)
                        if s == 11:
                            negate(b, 0)
                        kind, n, at = plan.get(s, (None, 0, 0))
                        if kind == "key":
                            key_rest(b + 1, n, first_unit(b) + at)
                        if kind == "out":
                            finish(b - 2, p, first_unit(b) + at)

                for u in range(KEY_UNITS):
                    key_rest(0, u, u)
                step(0, 0, 0)
                step(1, 1, 0)
                with dve.Fori(1, BATCH // 2 - 1) as j:
                    step(2 * j, 0, j)
                    step(2 * j + 1, 1, j)
                step(BATCH - 2, 0, BATCH // 2 - 1)
                step(LAST_ROW, 1, BATCH // 2 - 1)
                chain.begin(links_before(BATCH))
                units = first_unit(LAST_ROW) + units_of(LAST_ROW)
                negate(LAST_ROW, 1)
                hidden_power(LAST_ROW)
                finish(LAST_ROW - 1, 0, units)
                scale_rows(LAST_ROW - 1)
                finish(LAST_ROW, 1, units + 2)
                scale_rows(LAST_ROW)


def build(nc, ap, out):
    before_cross = nc.dram_tensor("before_cross", (BATCH, SEQ, DIM), F32, kind="Internal").ap()
    after_cross = nc.dram_tensor("after_cross", (BATCH, SEQ, DIM), F32, kind="Internal").ap()
    with ExitStack() as outer:
        mem = Memory(nc, outer, "shared")
        ident = mem.sbuf("ident", [128, 128])
        minus_half = mem.sbuf("minus_half", [128, 1])
        constants_pass(nc, ident, minus_half)
        with ExitStack() as inner:
            x_tokens = Memory(nc, inner, "layer0").sbuf("x_tokens", [SEQ, BATCH, DIM])
            self_attention_pass(nc, "attn0", x_tokens, ap["x"], ident, minus_half, ap["L0_attn_Wq"], ap["L0_attn_bq"],
                                ap["L0_attn_Wk"], ap["L0_attn_bk"], ap["L0_attn_Wv"], ap["L0_attn_bv"], ap["L0_attn_Wo"],
                                ap["L0_attn_bo"], ap["L0_attn_ln_g"], ap["L0_attn_ln_b"])
            memory_attention_pass(nc, x_tokens, ap["ctx_2048"], ap["mask_BxS2_bk0"], ident, minus_half)
            experts_pass(nc, x_tokens, ident, minus_half, ap["L0_ffn_Wg"], ap["L0_ffn_Wu"], ap["L0_ffn_Wd"],
                         ap["L0_ffn_Wr"], ap["L0_ffn_temperature"])
            self_attention_pass(nc, "attn1", x_tokens, None, ident, minus_half, ap["L1_attn_wq"], ap["L1_attn_bq"],
                                ap["L1_attn_wk"], ap["L1_attn_bk"], ap["L1_attn_wv"], ap["L1_attn_bv"], ap["L1_attn_wp"],
                                ap["L1_attn_bp"], None, None)
            store_pass(nc, "spill", x_tokens, before_cross)
        cross_attention_pass(nc, before_cross, ap["ctx_2048"], after_cross, ident)
        with ExitStack() as inner:
            x_tokens = Memory(nc, inner, "layer1").sbuf("x_tokens", [SEQ, BATCH, DIM])
            load_pass(nc, "reload", x_tokens, after_cross)
            quantized_ffn_pass(nc, x_tokens, ident, minus_half, ap["L1_ffn_w_gate"], ap["L1_ffn_w_up"],
                               ap["L1_ffn_w_down"], ap["L1_ffn_s_gate"], ap["L1_ffn_s_up"], ap["L1_ffn_s_down"])
            store_pass(nc, "result", x_tokens, out)


def kernel(**inputs):
    import numpy as np
    import concourse.bacc as bacc
    from concourse.bass_utils import run_bass_kernel_spmd as run
    nc=bacc.Bacc("TRN2", target_bir_lowering=False, num_devices=1)
    arrays={}; ap={}
    for name,a in inputs.items():
        a=np.ascontiguousarray(a)
        if a.dtype.itemsize==1: a=a.view(np.int32)
        arrays["in_"+name]=a
        ap[name]=nc.dram_tensor("in_"+name,a.shape,mybir.dt.from_np(a.dtype),kind="ExternalInput").ap()
    out=nc.dram_tensor("out",(BATCH,SEQ,DIM),F32,kind="ExternalOutput").ap()
    build(nc,ap,out)
    r=run(nc,[arrays],core_ids=[0])
    return r.results[0]["out"]
```
